# Optimizing a Trainium2 kernel written in Bass

```python
import numpy as np
import jax
import jax.numpy as jnp

def _softmax(x, axis=-1):
    return jax.nn.softmax(x, axis=axis)

def _gelu(x):
    return jax.nn.gelu(x, approximate=True)

def _silu(x):
    return jax.nn.silu(x)

def _sigmoid(x):
    return jax.nn.sigmoid(x)

def _layernorm(x, axis=-1, eps=1e-05):
    m = jnp.mean(x, axis=axis, keepdims=True)
    v = jnp.var(x, axis=axis, keepdims=True)
    return (x - m) / jnp.sqrt(v + eps)

def _scatter_add(tgt, idx, src, axis=0):
    return tgt.at[idx].add(src)

def _segment_sum(src, seg, n):
    return jax.ops.segment_sum(src, seg, n)
kernel_name = 'mk_perceiver_d1_seqx_r4_dfd57a'

def setup_inputs(seed: int=0):
    np.random.seed(seed)
    _w = jnp.asarray

    def _rec_inputs():
        import jax
        import jax.numpy as jnp
        _rk = jax.random.key(seed)
        x = -0.0002928 + 1 * jax.random.normal(jax.random.fold_in(_rk, 1), (16, 64, 256), jnp.float32)
        _lenS = 64 - jax.random.randint(jax.random.fold_in(_rk, 7), (16,), 0, max(1, 64 // 4) + 1, jnp.int32)
        _lenS2 = 1601 - jax.random.randint(jax.random.fold_in(_rk, 8), (16,), 0, max(1, 1601 // 4) + 1, jnp.int32)
        _ctx_1024P = jax.random.normal(jax.random.fold_in(_rk, 11), (16, 16, 256), jnp.float32)
        _ctx_1024c = jax.random.dirichlet(jax.random.fold_in(_rk, 511), 0.3 * jnp.ones((16,), jnp.float32), (16, 1601))
        _ctx_1024t = jnp.einsum('bsk,bkd->bsd', _ctx_1024c, _ctx_1024P)
        _ctx_1024t = _ctx_1024t * jax.lax.rsqrt(jnp.mean(jnp.square(_ctx_1024t)) + 1e-12) * 0.953939
        ctx_1024 = -1.39393e-06 + 0.999914 * (_ctx_1024t + 0.3 * jax.random.normal(jax.random.fold_in(_rk, 611), (16, 1601, 256), jnp.float32))
        return (x, ctx_1024)
    x, ctx_1024 = _rec_inputs()

    def _L0_xattn_setup():
        import jax, jax.numpy as jnp
        import numpy as np
        HIDDEN = 256
        HEADS = 16
        HEAD_DIM = HIDDEN // HEADS
        key = jax.random.key(seed)
        ks = jax.random.split(key, 11)
        B, T, D = (2, 512, HIDDEN)
        s = 1.0 / np.sqrt(D)
        return {'query': jax.random.normal(ks[0], (B, T, D), jnp.float32), 'key': jax.random.normal(ks[1], (B, T, D), jnp.float32), 'value': jax.random.normal(ks[2], (B, T, D), jnp.float32), 'Wq': jax.random.normal(ks[3], (D, D), jnp.float32) * s, 'bq': jnp.zeros((D,), jnp.float32), 'Wk': jax.random.normal(ks[4], (D, D), jnp.float32) * s, 'bk': jnp.zeros((D,), jnp.float32), 'Wv': jax.random.normal(ks[5], (D, D), jnp.float32) * s, 'bv': jnp.zeros((D,), jnp.float32), 'Wo': jax.random.normal(ks[6], (D, D), jnp.float32) * s, 'bo': jnp.zeros((D,), jnp.float32)}
    _L0_xattn_all = _L0_xattn_setup()
    _L0_xattn_in = {k: v for k, v in _L0_xattn_all.items() if k in ('Wq', 'bq', 'Wk', 'bk', 'Wv', 'bv', 'Wo', 'bo')}
    del _L0_xattn_all

    def _L0_attn_setup():
        import jax, jax.numpy as jnp
        import numpy as np
        EPS_RMS = 1e-06
        EPS_Q = 1e-05

        def rmsnorm(x, g):
            var = jnp.mean(x * x, axis=-1, keepdims=True)
            return g * (x * jax.lax.rsqrt(var + EPS_RMS))

        def activation_quant(x):
            scale = 127.0 / jnp.clip(jnp.max(jnp.abs(x), axis=-1, keepdims=True), EPS_Q)
            y = jnp.clip(jnp.round(x * scale), -128, 127) / scale
            return x + jax.lax.stop_gradient(y - x)

        def weight_quant(w):
            s = jnp.clip(jnp.mean(jnp.abs(w)), EPS_Q)
            y = jnp.clip(jnp.round(w / s), -1, 1) * s
            return w + jax.lax.stop_gradient(y - w)

        def bitlinear(x, w, g):
            xq = activation_quant(rmsnorm(x, g))
            wq = weight_quant(w)
            return jnp.einsum('btc,oc->bto', xq, wq)
        key = jax.random.key(seed)
        ks = jax.random.split(key, 5)
        B, T, C = (2, 512, 256)
        std = 1.0 / np.sqrt(C)
        inp = {'x': jax.random.normal(ks[0], (B, T, C), jnp.float32), 'wq': jax.random.normal(ks[1], (C, C), jnp.float32) * std, 'wk': jax.random.normal(ks[2], (C, C), jnp.float32) * std, 'wv': jax.random.normal(ks[3], (C, C), jnp.float32) * std, 'wo': jax.random.normal(ks[4], (C, C), jnp.float32) * std, 'gq': jnp.ones((C,), jnp.float32), 'gk': jnp.ones((C,), jnp.float32), 'gv': jnp.ones((C,), jnp.float32), 'go': jnp.ones((C,), jnp.float32)}
        return inp
    _L0_attn_all = _L0_attn_setup()
    _L0_attn_in = {k: v for k, v in _L0_attn_all.items() if k in ('wq', 'wk', 'wv', 'wo', 'gq', 'gk', 'gv', 'go')}
    del _L0_attn_all

    def _L0_ffn_setup():
        import jax, jax.numpy as jnp
        import numpy as np
        B, L, D, H, E, TOP_K = (4, 512, 256, 1024, 8, 2)
        LN_EPS = 1e-05
        key = jax.random.key(seed)
        ks = jax.random.split(key, 8)
        x = jax.random.normal(ks[0], (B, L, D), dtype=jnp.float32)
        gate_w = jax.random.normal(ks[1], (D, E), dtype=jnp.float32) / np.sqrt(D)
        w1 = jax.random.normal(ks[2], (E, D, H), dtype=jnp.float32) / np.sqrt(D)
        b1 = jnp.zeros((E, H), dtype=jnp.float32)
        w2 = jax.random.normal(ks[3], (E, H, D), dtype=jnp.float32) / np.sqrt(H)
        b2 = jnp.zeros((E, D), dtype=jnp.float32)
        gamma = jnp.ones((D,), dtype=jnp.float32)
        beta = jnp.zeros((D,), dtype=jnp.float32)
        return {'x': x, 'gate_w': gate_w, 'w1': w1, 'b1': b1, 'w2': w2, 'b2': b2, 'gamma': gamma, 'beta': beta}
    _L0_ffn_all = _L0_ffn_setup()
    _L0_ffn_in = {k: v for k, v in _L0_ffn_all.items() if k in ('gate_w', 'w1', 'b1', 'w2', 'b2', 'gamma', 'beta')}
    del _L0_ffn_all
    return {'x': x, 'ctx_1024': ctx_1024, 'L0_xattn_Wq': _L0_xattn_in['Wq'], 'L0_xattn_bq': _L0_xattn_in['bq'], 'L0_xattn_Wk': _L0_xattn_in['Wk'], 'L0_xattn_bk': _L0_xattn_in['bk'], 'L0_xattn_Wv': _L0_xattn_in['Wv'], 'L0_xattn_bv': _L0_xattn_in['bv'], 'L0_xattn_Wo': _L0_xattn_in['Wo'], 'L0_xattn_bo': _L0_xattn_in['bo'], 'L0_attn_wq': _L0_attn_in['wq'], 'L0_attn_wk': _L0_attn_in['wk'], 'L0_attn_wv': _L0_attn_in['wv'], 'L0_attn_wo': _L0_attn_in['wo'], 'L0_attn_gq': _L0_attn_in['gq'], 'L0_attn_gk': _L0_attn_in['gk'], 'L0_attn_gv': _L0_attn_in['gv'], 'L0_attn_go': _L0_attn_in['go'], 'L0_ffn_gate_w': _L0_ffn_in['gate_w'], 'L0_ffn_w1': _L0_ffn_in['w1'], 'L0_ffn_b1': _L0_ffn_in['b1'], 'L0_ffn_w2': _L0_ffn_in['w2'], 'L0_ffn_b2': _L0_ffn_in['b2'], 'L0_ffn_gamma': _L0_ffn_in['gamma'], 'L0_ffn_beta': _L0_ffn_in['beta']}

def reference(x, ctx_1024, L0_xattn_Wq, L0_xattn_bq, L0_xattn_Wk, L0_xattn_bk, L0_xattn_Wv, L0_xattn_bv, L0_xattn_Wo, L0_xattn_bo, L0_attn_wq, L0_attn_wk, L0_attn_wv, L0_attn_wo, L0_attn_gq, L0_attn_gk, L0_attn_gv, L0_attn_go, L0_ffn_gate_w, L0_ffn_w1, L0_ffn_b1, L0_ffn_w2, L0_ffn_b2, L0_ffn_gamma, L0_ffn_beta):
    import jax
    import jax.numpy as jnp

    def _L0_xattn_ref(query, key, value, Wq, bq, Wk, bk, Wv, bv, Wo, bo):
        import jax, jax.numpy as jnp
        import numpy as np
        HIDDEN = 256
        HEADS = 16
        HEAD_DIM = HIDDEN // HEADS
        B, Tq, D = query.shape
        Tk = key.shape[1]
        H, Hd = (HEADS, HEAD_DIM)
        Q = (query @ Wq + bq).reshape(B, Tq, H, Hd).transpose(0, 2, 1, 3)
        K = (key @ Wk + bk).reshape(B, Tk, H, Hd).transpose(0, 2, 1, 3)
        V = (value @ Wv + bv).reshape(B, Tk, H, Hd).transpose(0, 2, 1, 3)
        scale = jnp.sqrt(jnp.asarray(Hd, Q.dtype))
        scores = jnp.einsum('bhqd,bhkd->bhqk', Q, K) / scale
        causal = jnp.triu(jnp.ones((Tq, Tk), bool), k=1)
        scores = jnp.where(causal[None, None], jnp.asarray(-jnp.inf, scores.dtype), scores)
        attn = jax.nn.softmax(scores, axis=-1)
        out = jnp.einsum('bhqk,bhkd->bhqd', attn, V)
        out = out.transpose(0, 2, 1, 3).reshape(B, Tq, D)
        return out @ Wo + bo

    def _L0_attn_ref(x, wq, wk, wv, wo, gq, gk, gv, go):
        import jax, jax.numpy as jnp
        import numpy as np
        EPS_RMS = 1e-06
        EPS_Q = 1e-05

        def rmsnorm(x, g):
            var = jnp.mean(x * x, axis=-1, keepdims=True)
            return g * (x * jax.lax.rsqrt(var + EPS_RMS))

        def activation_quant(x):
            scale = 127.0 / jnp.clip(jnp.max(jnp.abs(x), axis=-1, keepdims=True), EPS_Q)
            y = jnp.clip(jnp.round(x * scale), -128, 127) / scale
            return x + jax.lax.stop_gradient(y - x)

        def weight_quant(w):
            s = jnp.clip(jnp.mean(jnp.abs(w)), EPS_Q)
            y = jnp.clip(jnp.round(w / s), -1, 1) * s
            return w + jax.lax.stop_gradient(y - w)

        def bitlinear(x, w, g):
            xq = activation_quant(rmsnorm(x, g))
            wq = weight_quant(w)
            return jnp.einsum('btc,oc->bto', xq, wq)
        B, T, C = x.shape
        n_head = 16
        head_dim = C // n_head
        q = bitlinear(x, wq, gq).reshape(B, T, n_head, head_dim).transpose(0, 2, 1, 3)
        k = bitlinear(x, wk, gk).reshape(B, T, n_head, head_dim).transpose(0, 2, 1, 3)
        v = bitlinear(x, wv, gv).reshape(B, T, n_head, head_dim).transpose(0, 2, 1, 3)
        att = jnp.einsum('bhqd,bhkd->bhqk', q, k) * (1.0 / np.sqrt(head_dim))
        causal = jnp.tril(jnp.ones((T, T), dtype=bool))
        att = jnp.where(causal[None, None], att, -jnp.inf)
        att = jax.nn.softmax(att, axis=-1)
        y = jnp.einsum('bhqk,bhkd->bhqd', att, v)
        y = y.transpose(0, 2, 1, 3).reshape(B, T, C)
        return bitlinear(y, wo, go)

    def _L0_ffn_ref(x, gate_w, w1, b1, w2, b2, gamma, beta):
        import jax, jax.numpy as jnp
        import numpy as np
        B, L, D, H, E, TOP_K = (4, 512, 256, 1024, 8, 2)
        LN_EPS = 1e-05
        residual = x
        mu = jnp.mean(x, axis=-1, keepdims=True)
        var = jnp.mean(jnp.square(x - mu), axis=-1, keepdims=True)
        xn = (x - mu) * jax.lax.rsqrt(var + LN_EPS) * gamma + beta
        probs = jax.nn.softmax(jnp.einsum('bld,de->ble', xn, gate_w), axis=-1)
        w, idx = jax.lax.top_k(probs, TOP_K)
        w = w / jnp.sum(w, axis=-1, keepdims=True)
        cw = jnp.sum(w[..., None] * jax.nn.one_hot(idx, E, dtype=x.dtype), axis=2)
        h = jax.nn.gelu(jnp.einsum('bld,edh->eblh', xn, w1) + b1[:, None, None, :], approximate=False)
        out_e = jnp.einsum('eblh,ehd->ebld', h, w2) + b2[:, None, None, :]
        output = jnp.einsum('ble,ebld->bld', cw, out_e)
        return output + residual
    x = x + _L0_xattn_ref(_layernorm(x, axis=-1), ctx_1024, ctx_1024, L0_xattn_Wq, L0_xattn_bq, L0_xattn_Wk, L0_xattn_bk, L0_xattn_Wv, L0_xattn_bv, L0_xattn_Wo, L0_xattn_bo)
    x = x + _L0_attn_ref(_layernorm(x, axis=-1), L0_attn_wq, L0_attn_wk, L0_attn_wv, L0_attn_wo, L0_attn_gq, L0_attn_gk, L0_attn_gv, L0_attn_go)
    x = x + _L0_ffn_ref(_layernorm(x, axis=-1), L0_ffn_gate_w, L0_ffn_w1, L0_ffn_b1, L0_ffn_w2, L0_ffn_b2, L0_ffn_gamma, L0_ffn_beta)
    return x

_drawn_inputs = setup_inputs


def setup_inputs(seed=0):
    import zlib

    import numpy as np

    out = dict(_drawn_inputs(seed))
    spreads = {'L0_xattn_bq': (0.0, 0.1),
     'L0_xattn_bk': (0.0, 0.8),
     'L0_xattn_bv': (0.0, 0.1),
     'L0_xattn_bo': (0.0, 0.1),
     'L0_attn_gq': (1.0, 0.6),
     'L0_attn_gk': (1.0, 0.557),
     'L0_attn_gv': (1.0, 0.2),
     'L0_attn_go': (1.0, 0.2),
     'L0_ffn_b1': (0.0, 0.368),
     'L0_ffn_b2': (0.0, 0.1),
     'L0_ffn_gamma': (1.0, 0.2),
     'L0_ffn_beta': (0.0, 0.1)}
    factors = {}
    for name, (base, spread) in spreads.items():
        noise = np.random.default_rng([zlib.crc32(name.encode()), seed]).standard_normal(out[name].shape)
        drawn = base * np.exp(spread * noise) if base else spread * noise
        out[name] = jnp.asarray(drawn.astype(out[name].dtype))
    for name, factor in factors.items():
        out[name] = (out[name] * factor).astype(out[name].dtype)
    return out
```

```python
from contextlib import ExitStack

import numpy as np

import concourse.bass as bass
from concourse import mybir
from concourse.alu_op_type import AluOpType as ALU

ACT = mybir.ActivationFunctionType
AX = mybir.AxisListType
F32 = mybir.dt.float32
BF16 = mybir.dt.bfloat16
I32 = mybir.dt.int32

P = 128
B, S, D = 16, 64, 256
TOK = B * S
T = TOK // P
KC = D // P
H, HD = 16, 16
HG = P // HD
PAIRS = H // 2
VW = 2 * HD + 2
E, FF, TOPK = 8, 1024, 2
FC = FF // P
TILES = TOPK * T + E - 1
ROW = D + 1 + E
LN_EPS, RMS_EPS, Q_EPS = 1e-5, 1e-6, 1e-5
ROUND = 12582912.0
MASKED = -1e30
SCALE = HD ** -0.5


def at(start, size):
    return slice(start, start + size) if isinstance(start, int) else bass.ds(start, size)


def after(engine, semaphore, count):
    if not (isinstance(count, int) and count <= 0):
        engine.wait_ge(semaphore, count)


class Attention:

    def __init__(self, sem, name):
        self.xn_ready = sem(f"{name}_xn_ready")
        self.z_ready = sem(f"{name}_z_ready")
        self.amax_ready = sem(f"{name}_amax_ready")
        self.qscale_ready = sem(f"{name}_qscale_ready")
        self.deq_ready = sem(f"{name}_deq_ready")
        self.rounded = sem(f"{name}_rounded")
        self.ints_ready = sem(f"{name}_ints_ready")
        self.tr_done = sem(f"{name}_tr_done")
        self.tr_copied = sem(f"{name}_tr_copied")
        self.qk_done = sem(f"{name}_qk_done")
        self.v_done = sem(f"{name}_v_done")
        self.q_ready = sem(f"{name}_q_ready")
        self.k_ready = sem(f"{name}_k_ready")
        self.kt_done = sem(f"{name}_kt_done")
        self.kbd_ready = sem(f"{name}_kbd_ready")
        self.vbd_ready = sem(f"{name}_vbd_ready")
        self.scores_done = sem(f"{name}_scores_done")
        self.max_done = sem(f"{name}_max_done")
        self.exp_done = sem(f"{name}_exp_done")
        self.pt0_copied = sem(f"{name}_pt0_copied")
        self.pt1_copied = sem(f"{name}_pt1_copied")
        self.pv_done = sem(f"{name}_pv_done")
        self.rinv_ready = sem(f"{name}_rinv_ready")
        self.o_ready = sem(f"{name}_o_ready")
        self.sumsq_ready = sem(f"{name}_sumsq_ready")
        self.orms_ready = sem(f"{name}_orms_ready")
        self.oz_ready = sem(f"{name}_oz_ready")
        self.omax_ready = sem(f"{name}_omax_ready")
        self.oscale_ready = sem(f"{name}_oscale_ready")
        self.orounded = sem(f"{name}_orounded")
        self.oints_ready = sem(f"{name}_oints_ready")
        self.ot_done = sem(f"{name}_ot_done")
        self.ot_copied = sem(f"{name}_ot_copied")
        self.out_done = sem(f"{name}_out_done")
        self.x_done = sem(f"{name}_x_done")
        self.stats_done = sem(f"{name}_stats_done")
        self.mv_done = sem(f"{name}_mv_done")
        self.ctx_ready = [sem(f"{name}_ctx_ready{k}") for k in range(2)]
        self.shifted = [sem(f"{name}_shifted{k}") for k in range(2)]
        self.pt_done = [sem(f"{name}_pt_done{k}") for k in range(2)]


def program(nc, x, ctx_in, xWq, xbq, xWk, xbk, xWv, xbv, xWo, xbo, awq, awk, awv, awo,
            agq, agk, agv, ago, gate_w, w1, b1, w2, b2, gamma, beta, rows, acc, out):
    x_rows = x.rearrange("b s d -> (b s) d")
    out_rows = out.rearrange("b s d -> (b s) d")

    with ExitStack() as stack:
        def sb(name, shape, dt=F32):
            return stack.enter_context(nc.sbuf_tensor(name, shape, dt))

        def bank(name):
            return stack.enter_context(nc.psum_tensor(name, [P, 512], F32))

        def sem(name):
            return stack.enter_context(nc.semaphore(name))

        w1_sb = sb("w1_sb", [P, E, KC, FF])
        w2_sb = sb("w2_sb", [P, E, FC, D])
        wraw = w2_sb[:, E - 1].rearrange("p (w k) d -> p w k d", k=KC)
        bias_rows = sb("bias_rows", [E * FC + 2 * KC, P])
        bias_col = sb("bias_col", [P, E * FC + 2 * KC])
        b1_col = bias_col[:, 0:E * FC]
        bq_col = bias_col[:, E * FC:E * FC + KC]
        bk_col = bias_col[:, E * FC + KC:E * FC + 2 * KC]
        wproj = sb("wproj", [P, 4, KC, D])
        wtern = sb("wtern", [P, 4, KC, D], BF16)
        wabs = sb("wabs", [P, 4])
        wscale = sb("wscale", [P, 4])
        wrecip = sb("wrecip", [P, 4])
        qk_scale = sb("qk_scale", [P, 1])
        bv_row = sb("bv_row", [P, D])
        bo_row = sb("bo_row", [P, D])
        g_row = sb("g_row", [P, 4, D])
        gamma_row = sb("gamma_row", [P, D])
        beta_row = sb("beta_row", [P, D])
        gate_sb = sb("gate_sb", [P, KC, E])
        ident = sb("ident", [P, P])
        ident_bf = sb("ident_bf", [P, P], BF16)
        ones_bf = sb("ones_bf", [P, P], BF16)
        ones = sb("ones", [P, P])
        before = sb("before", [P, P], BF16)
        head_mask = sb("head_mask", [P, HG])
        causal = sb("causal", [P, S], BF16)
        neg_half = sb("neg_half", [P, T])
        round_col = sb("round_col", [P, 1])

        x_sb = sb("x_sb", [P, T, D])
        xr = sb("xr", [P, T, ROW])
        stats = sb("stats", [P, 6])
        mv_tile = sb("mv_tile", [P, 2])
        mv = sb("mv", [P, 3, T, 2])
        ve = sb("ve", [P, 6, T])
        rstd = sb("rstd", [P, 3, T])
        rboth = sb("rboth", [P, 2, T])
        ctx_sb = sb("ctx_sb", [P, 2, D])
        xn = sb("xn", [P, D])
        xcT = sb("xcT", [P, 4 * P])
        qT = sb("qT", [P, KC, P])
        kT = sb("kT", [P, KC, P])
        k_bd = sb("k_bd", [P, KC, 2, HG, S])
        v_bd = sb("v_bd", [P, 2, 2, PAIRS, VW])
        rmax = sb("rmax", [P, H])
        probs = sb("probs", [P, H, S])
        wround = probs[:].rearrange("p h s -> p (h s)").bitcast(BF16).rearrange("p (w k d) -> p w k d", w=4, k=KC)
        pT = sb("pT", [P, PAIRS, P])
        rinv = sb("rinv", [P, PAIRS, 2])
        o_sb = sb("o_sb", [P, D])
        oT = sb("oT", [P, KC, P])
        z = sb("z", [P, 3, D])
        zi = sb("zi", [P, 3, D], BF16)
        ziT = sb("ziT", [P, 3, KC, P], BF16)
        amax = sb("amax", [P, 3])
        arecip = sb("arecip", [P, 3])
        deq = sb("deq", [P, 2, 3])
        wfac = sb("wfac", [P, 3])
        osq = sb("osq", [P, D])
        base_f = sb("base_f", [P, 2, T])
        small = sb("small", [P, 8])
        oi = sb("oi", [P, D], BF16)
        oiT = sb("oiT", [P, KC, P], BF16)
        spare = [0]

        def reuse(*dims):
            n = int(np.prod(dims))
            a = wproj[:].rearrange("p w k d -> p (w k d)")[:, spare[0]:spare[0] + n]
            spare[0] += n
            names = "abc"[:len(dims)]
            return a if len(dims) == 1 else a.rearrange(
                f"p ({' '.join(names)}) -> p {' '.join(names)}", **dict(zip(names, dims)))

        b2_row = k_bd[:, :, :, :, :].rearrange("p a b c d -> p (a b c d)").rearrange("p (e d) -> p e d", e=E)
        fill = sb("fill", [P, ROW])
        gp = reuse(T, E)
        gp2 = reuse(T, E)
        eq = reuse(T, E)
        oh = reuse(2, T, E)
        oh_bf = sb("oh_bf", [P, T, E], BF16)
        rev = sb("rev", [P, E])
        gm = sb("gm", [P, 4, T])
        slots = reuse(T, E)
        slot_f = sb("slot_f", [P, 2, T])
        slot_i = sb("slot_i", [P, 2, T], I32)
        cnt = sb("cnt", [P, 4, E])
        cnt_i = sb("cnt_i", [P, 2, E], I32)
        tile_no = sb("tile_no", [P, TILES])
        tile_cmp = reuse(TILES, E)
        tile_f = sb("tile_f", [P, TILES])
        tile_e = sb("tile_e", [P, TILES], I32)
        xg = reuse(2, ROW)
        xgT = reuse(KC, P)
        h_sb = probs[:, :, :].rearrange("p h s -> p (h s)")
        gT = pT
        y_sb = reuse(2, D)
        tok_i = sb("tok_i", [P, 2], I32)

        bank_tr, bank_qk, bank_v = bank("bank_tr"), bank("bank_qk"), bank("bank_v")
        bank_s = [bank("bank_s0"), bank("bank_s1")]
        bank_p = [bank("bank_p0"), bank("bank_p1")]
        bank_o = bank("bank_o")

        cross = Attention(sem, "cross")
        own = Attention(sem, "own")
        x_ready, proj_ready, rows_ready, raw_ready, w_ready = (
            sem(n) for n in ("x_ready", "proj_ready", "rows_ready", "raw_ready", "w_ready"))
        const_ready, tables_ready = sem("const_ready"), sem("tables_ready")
        x_stats, x_ve, x_rstd = sem("x_stats"), sem("x_ve"), sem("x_rstd")
        bias_done, bias_ready = sem("bias_done"), sem("bias_ready")
        wabs_ready, wtot_done, wscale_ready, wrounded = (sem(n) for n in ("wabs_ready", "wtot_done", "wscale_ready", "wrounded"))
        wint_ready, wtr_done, wtr_copied = sem("wint_ready"), sem("wtr_done"), sem("wtr_copied")
        bo_added = sem("bo_added")
        ln1_ve, ln1_r, ln2_ve, ln2_r, both1 = (sem(n) for n in ("ln1_ve", "ln1_r", "ln2_ve", "ln2_r", "both1"))
        g_chain = sem("g_chain")
        base_ready, xr_ready, gtr_done, gtr_copied, logit_done = (
            sem(n) for n in ("base_ready", "xr_ready", "gtr_done", "gtr_copied", "logit_done"))
        max_ready, exp_ready, oh_ready, rank_done = (sem(n) for n in ("max_ready", "exp_ready", "oh_ready", "rank_done"))
        slot_ready, tile_ready, cw_ready = sem("slot_ready"), sem("tile_ready"), sem("cw_ready")
        b2_ready, dispatched, acc_ready = (sem(n) for n in ("b2_ready", "dispatched", "acc_ready"))
        xg_ready = [sem("xg_ready0"), sem("xg_ready1")]
        e_tr_done, e_tr_copied, up_done, h_ready, gelu_done, down_done, y_ready, tok_ready, y_sum = (
            sem(n) for n in ("e_tr_done", "e_tr_copied", "up_done", "h_ready", "gelu_done",
                             "down_done", "y_ready", "tok_ready", "y_sum"))
        y_added = [sem("y_added0"), sem("y_added1")]
        ht_done = [sem("ht_done0"), sem("ht_done1")]
        x_read, row_copied, rows_filled = sem("x_read"), sem("row_copied"), sem("rows_filled")
        out_stored = sem("out_stored")

        block = stack.enter_context(nc.Block())
        CONSTS, TABLES = 15, 8

        @block.sync
        def _(sp):
            def load_ctx(t, par):
                if not isinstance(t, int) or t >= 2:
                    sp.wait_ge(cross.tr_done, t - 1)
                for b in range(2):
                    src = ctx_in[at(2 * t + b, 1), 0:S, :].rearrange("b s d -> (b s) d")
                    sp.dma_start(ctx_sb[S * b:S * b + S, par, :], src).then_inc(cross.ctx_ready[par], 16)

            sp.dma_start(x_sb[:, :, :], x_rows.rearrange("(t p) d -> p t d", p=P)).then_inc(x_ready, 16)
            load_ctx(0, 0)
            load_ctx(1, 1)
            for n, w in enumerate((xWq, xWk, xWv, xWo)):
                sp.dma_start(wproj[:, n], w.rearrange("(k p) o -> p k o", p=P)).then_inc(proj_ready, 16)
            sp.dma_start(bias_rows[0:E * FC, :], b1.rearrange("e (c p) -> (e c) p", p=P)).then_inc(rows_ready, 16)
            for n, r in enumerate((xbq, xbk)):
                sp.dma_start(bias_rows[E * FC + KC * n:E * FC + KC * n + KC, :],
                             r.rearrange("(k p) -> k p", p=P)).then_inc(rows_ready, 16)
            for r, dst in ((xbv, bv_row[:]), (xbo, bo_row[:]), (agq, g_row[:, 0]), (agk, g_row[:, 1]),
                           (agv, g_row[:, 2]), (ago, g_row[:, 3]), (gamma, gamma_row[:]), (beta, beta_row[:])):
                sp.dma_start(dst, r.partition_broadcast(P)).then_inc(rows_ready, 16)
            sp.dma_start(gate_sb[:], gate_w.rearrange("(k p) e -> p k e", p=P)).then_inc(rows_ready, 16)
            for n, w in enumerate((awq, awk, awv, awo)):
                sp.dma_start(wraw[:, n], w.rearrange("(k p) c -> p k c", p=P)).then_inc(raw_ready, 16)
            with sp.Fori(1, T // 2) as r:
                load_ctx(2 * r, 0)
                load_ctx(2 * r + 1, 1)
            sp.wait_ge(tables_ready, 2)
            sp.dma_start(rows.rearrange("(j p) r -> p j r", p=P),
                         fill[:, :].unsqueeze(1).to_broadcast([P, TILES, ROW])).then_inc(rows_filled, 16)
            sp.dma_start(acc[TOK:TOK + P, :], fill[:, 0:D]).then_inc(rows_filled, 16)
            sp.wait_ge(wint_ready, 1)
            sp.dma_start(w2_sb[:, E - 1], w2[E - 1].rearrange("(c p) d -> p c d", p=P)).then_inc(w_ready, 16)
            sp.wait_ge(own.scores_done, 2 * T)
            sp.dma_start(b2_row, b2.partition_broadcast(P)).then_inc(b2_ready, 16)
            sp.wait_ge(base_ready, T)
            sp.dma_start(acc[0:TOK, :].rearrange("(t p) d -> p t d", p=P), x_sb[:]).then_inc(acc_ready, 16)

            def load_rows(j, par):
                if not isinstance(j, int) or j >= 2:
                    sp.wait_ge(y_ready, j - 1)
                    sp.wait_ge(e_tr_done, j - 1)
                    sp.wait_ge(tok_ready, j - 1)
                sp.dma_start(xg[:, par, :], rows[at(j * P, P), :]).then_inc(xg_ready[par], 16)

            sp.wait_ge(dispatched, 16 * TOPK * T)
            load_rows(0, 0)
            load_rows(1, 1)
            with sp.Fori(1, TILES // 2) as r:
                load_rows(2 * r, 0)
                load_rows(2 * r + 1, 1)
            load_rows(TILES - 1, 0)
            sp.wait_ge(y_added[0], 16 * (TILES - TILES // 2))
            sp.wait_ge(y_added[1], 16 * (TILES // 2))
            sp.dma_start(out_rows, acc[0:TOK, :]).then_inc(out_stored, 16)
            sp.wait_ge(out_stored, 16)

        @block.gpsimd
        def _(pool):
            made = [0]

            def const(ins):
                made[0] += 1
                ins.then_inc(const_ready, 1)
                pool.wait_ge(const_ready, made[0])

            const(pool.memset(ident[:], 0.0))
            const(pool.affine_select(out=ident[:], in_=ident[:], compare_op=ALU.not_equal, fill=1.0,
                                     base=0, pattern=[[-1, P]], channel_multiplier=1))
            const(pool.memset(neg_half[:], -0.5))
            const(pool.memset(head_mask[:], 1.0))
            const(pool.affine_select(out=head_mask[:], in_=head_mask[:], compare_op=ALU.is_ge, fill=0.0,
                                     base=0, pattern=[[-HD, HG]], channel_multiplier=1))
            const(pool.affine_select(out=head_mask[:], in_=head_mask[:], compare_op=ALU.is_ge, fill=0.0,
                                     base=HD - 1, pattern=[[HD, HG]], channel_multiplier=-1))
            const(pool.memset(causal[:], 0.0))
            for b in range(2):
                half = causal[S * b:S * b + S]
                const(pool.affine_select(out=half, in_=half, compare_op=ALU.is_ge, fill=MASKED,
                                         base=0, pattern=[[-1, S]], channel_multiplier=1))
            const(pool.tensor_copy(ident_bf[:], ident[:]))
            const(pool.memset(v_bd[:], 0.0))
            const(pool.memset(v_bd[0:S, :, :, :, 2 * HD], 1.0))
            const(pool.memset(v_bd[S:P, :, :, :, 2 * HD + 1], 1.0))
            const(pool.memset(round_col[:], ROUND))
            const(pool.memset(ones[:], 1.0))
            assert made[0] == CONSTS

            def table(ins):
                made[1] += 1
                ins.then_inc(tables_ready, 1)
                pool.wait_ge(tables_ready, made[1])

            made.append(0)
            table(pool.memset(fill[:], 0.0))
            table(pool.iota(fill[:, D:D + 1], pattern=[[0, 1]], base=TOK, channel_multiplier=1,
                            allow_small_or_imprecise_dtypes=True))
            table(pool.memset(ones_bf[:], 1.0))
            table(pool.memset(before[:], 1.0))
            table(pool.affine_select(out=before[:], in_=before[:], compare_op=ALU.is_gt, fill=0.0,
                                     base=0, pattern=[[1, P]], channel_multiplier=-1))
            table(pool.iota(rev[:], pattern=[[-1, E]], base=E, channel_multiplier=0,
                            allow_small_or_imprecise_dtypes=True))
            table(pool.iota(tile_no[:], pattern=[[1, TILES]], base=0, channel_multiplier=0,
                            allow_small_or_imprecise_dtypes=True))
            table(pool.iota(xr[:, :, D:D + 1], pattern=[[P, T], [0, 1]], base=0, channel_multiplier=1,
                            allow_small_or_imprecise_dtypes=True))
            assert made[1] == TABLES

            def inverse_root(dst, src, waits, done):
                for s, v in waits:
                    pool.wait_ge(s, v)
                pool.tensor_tensor(dst, src, neg_half[:, 0:src.shape[-1]], ALU.pow).then_inc(done, 1)

            inverse_root(rstd[:, 0], ve[:, 0], ((x_ve, 1), (const_ready, CONSTS)), x_rstd)
            inverse_root(rstd[:, 1], ve[:, 1], ((ln1_ve, 1),), ln1_r)
            inverse_root(rboth[:, 0], ve[:, 3], ((ln1_ve, 2),), ln1_r)

            with pool.Fori(0, T) as t:
                inverse_root(small[:, 1:2], small[:, 0:1], ((own.sumsq_ready, t + 1),), own.orms_ready)
            inverse_root(rstd[:, 2], ve[:, 2], ((ln2_ve, 1),), ln2_r)
            inverse_root(rboth[:, 1], ve[:, 5], ((ln2_ve, 2),), ln2_r)
            pool.wait_ge(slot_ready, 1)
            pool.wait_ge(cw_ready, 1)
            pool.wait_ge(rows_filled, 32)
            pool.wait_ge(row_copied, T)
            for t in range(T):
                for k in range(TOPK):
                    pool.indirect_dma_start(rows, bass.IndirectOffsetOnAxis(ap=slot_i[:, k, t:t + 1], axis=0),
                                            xr[:, t, :], None).then_inc(dispatched, 16)

            pool.wait_ge(acc_ready, 16)
            for j in range(TILES):
                par = j % 2
                pool.wait_ge(y_ready, j + 1)
                pool.wait_ge(tok_ready, j + 1)
                if j >= 1:
                    pool.wait_ge(y_added[1 - par], 16 * ((j + 1) // 2))
                pool.indirect_dma_start(acc, bass.IndirectOffsetOnAxis(ap=tok_i[:, par:par + 1], axis=0),
                                        y_sb[:, par, :], None, compute_op=ALU.add).then_inc(y_added[par], 16)

        @block.tensor
        def _(pe):
            def transpose(dst, src, idt):
                return pe.transpose(dst, src, idt)

            def cross_front_transposes(t, par, round_):
                pe.wait_ge(cross.xn_ready, t + 1)
                pe.wait_ge(cross.ctx_ready[par], 32 * (round_ + 1))
                after(pe, cross.tr_copied, t)
                for k in range(KC):
                    transpose(bank_tr[:, k * P:(k + 1) * P], xn[:, k * P:(k + 1) * P], ident[:])
                for k in range(KC):
                    last = transpose(bank_tr[:, (KC + k) * P:(KC + k + 1) * P],
                                     ctx_sb[:, par, k * P:(k + 1) * P], ident[:])
                last.then_inc(cross.tr_done, 1)

            def cross_front_products(t):
                pe.wait_ge(cross.tr_copied, t + 1)
                after(pe, cross.q_ready, t)
                after(pe, cross.k_ready, t)
                for w in range(2):
                    for f in range(KC):
                        for k in range(KC):
                            last = pe.matmul(bank_qk[:, (2 * w + f) * P:(2 * w + f + 1) * P],
                                             wproj[:, w, k, f * P:(f + 1) * P],
                                             xcT[:, (2 * w + k) * P:(2 * w + k + 1) * P],
                                             start=(k == 0), stop=(k == KC - 1))
                last.then_inc(cross.qk_done, 1)
                after(pe, cross.vbd_ready, t)
                for k in range(KC):
                    last = pe.matmul(bank_v[:, 0:D], xcT[:, (2 + k) * P:(3 + k) * P], wproj[:, 2, k, :],
                                     start=(k == 0), stop=(k == KC - 1))
                last.then_inc(cross.v_done, 1)

            def scores(a, t):
                pe.wait_ge(a.q_ready, t + 1)
                pe.wait_ge(a.kbd_ready, t + 1)
                for g in range(KC):
                    after(pe, a.shifted[g], t)
                    pe.matmul(bank_s[g][:, :], ident_bf[:], causal[:].unsqueeze(1).to_broadcast([P, HG, S]),
                              start=True, stop=False, skip_group_check=True)
                    for b in range(2):
                        last = pe.matmul(bank_s[g][S * b:S * b + S, :], qT[:, g, S * b:S * b + S],
                                         k_bd[:, g, b].rearrange("p h s -> p (h s)"),
                                         start=False, stop=True, skip_group_check=True)
                    last.then_inc(a.scores_done, 1)

            def probs_transposes(a, t):
                for g in range(2):
                    pe.wait_ge(a.exp_done, 2 * t + g + 1)
                    after(pe, a.ot_copied if g == 0 else a.x_done, t)
                    for j in range(4):
                        c = 4 * g + j
                        last = transpose(bank_p[g][:, j * P:(j + 1) * P],
                                         probs[:, 2 * c:2 * c + 2, :].rearrange("p h s -> p (h s)"), ident[:])
                    last.then_inc(a.pt_done[g], 1)

            def values(a, t, par):
                pe.wait_ge(a.vbd_ready, t + 1)
                pe.wait_ge(a.pt0_copied, t + 1)
                pe.wait_ge(a.pt1_copied, t + 1)
                after(pe, a.o_ready, t)
                for c in range(PAIRS):
                    for b in range(2):
                        last = pe.matmul(bank_o[S * b:S * b + S, c * VW:(c + 1) * VW],
                                         pT[:, c, S * b:S * b + S], v_bd[:, par, b, c, :],
                                         start=True, stop=True)
                last.then_inc(a.pv_done, 1)

            def cross_out(t):
                pe.wait_ge(cross.o_ready, t + 1)
                for k in range(KC):
                    last = transpose(bank_p[0][:, k * P:(k + 1) * P], o_sb[:, k * P:(k + 1) * P], ident[:])
                last.then_inc(cross.ot_done, 1)
                pe.wait_ge(cross.ot_copied, t + 1)
                for k in range(KC):
                    last = pe.matmul(bank_p[1][:, 0:D], oT[:, k, :], wproj[:, 3, k, :],
                                     start=(k == 0), stop=(k == KC - 1))
                last.then_inc(cross.out_done, 1)

            def own_front(t):
                pe.wait_ge(own.ints_ready, t + 1)
                after(pe, own.kbd_ready, t)
                tr = bank_tr[:, :].bitcast(BF16)
                for n in range(3):
                    for k in range(KC):
                        c = KC * n + k
                        last = transpose(tr[:, c * P:(c + 1) * P], zi[:, n, k * P:(k + 1) * P], ident_bf[:])
                last.then_inc(own.tr_done, 1)
                pe.wait_ge(own.tr_copied, t + 1)
                after(pe, own.q_ready, t)
                after(pe, own.k_ready, t)
                for f in range(KC):
                    for k in range(KC):
                        pe.matmul(bank_qk[:, f * P:(f + 1) * P], wtern[:, 0, k, f * P:(f + 1) * P],
                                  ziT[:, 0, k, :], start=(k == 0), stop=(k == KC - 1))
                for k in range(KC):
                    last = pe.matmul(bank_qk[:, D:2 * D], ziT[:, 1, k, :], wtern[:, 1, k, :],
                                     start=(k == 0), stop=(k == KC - 1))
                last.then_inc(own.qk_done, 1)
                after(pe, own.vbd_ready, t)
                for k in range(KC):
                    last = pe.matmul(bank_v[:, 0:D], ziT[:, 2, k, :], wtern[:, 2, k, :],
                                     start=(k == 0), stop=(k == KC - 1))
                last.then_inc(own.v_done, 1)
                pe.wait_ge(own.k_ready, t + 1)
                for k in range(KC):
                    last = transpose(bank_tr[:, k * P:(k + 1) * P],
                                     kT[:, :, :].rearrange("p a b -> p (a b)")[:, k * P:(k + 1) * P], ident[:])
                last.then_inc(own.kt_done, 1)

            def own_out(t):
                pe.wait_ge(own.oints_ready, t + 1)
                tr = bank_p[0][:, :].bitcast(BF16)
                for k in range(KC):
                    last = transpose(tr[:, k * P:(k + 1) * P], oi[:, k * P:(k + 1) * P], ident_bf[:])
                last.then_inc(own.ot_done, 1)
                pe.wait_ge(own.ot_copied, t + 1)
                for k in range(KC):
                    last = pe.matmul(bank_p[1][:, 0:D], oiT[:, k, :], wtern[:, 3, k, :],
                                     start=(k == 0), stop=(k == KC - 1))
                last.then_inc(own.out_done, 1)

            pe.wait_ge(const_ready, CONSTS)
            pe.wait_ge(rows_ready, 16 * 12)
            n = E * FC + 2 * KC
            transpose(bank_o[:, 0:n], bias_rows[:], ident[0:n, 0:n]).then_inc(bias_done, 1)
            pe.wait_ge(proj_ready, 64)
            cross_front_transposes(0, 0, 0)
            cross_front_products(0)
            pe.wait_ge(wabs_ready, 1)
            pe.wait_ge(bias_ready, 1)
            pe.matmul(bank_o[:, 0:4], ones[:], wabs[:], start=True, stop=True).then_inc(wtot_done, 1)
            pe.wait_ge(wint_ready, 1)
            for h in range(2):
                dst = bank_p[h][:, :].bitcast(BF16).rearrange("p (w c o) -> p w c o", w=2, c=KC)
                for w in range(2):
                    for oc in range(KC):
                        for cc in range(KC):
                            last = transpose(dst[:, w, cc, oc * P:(oc + 1) * P],
                                             wround[:, 2 * h + w, oc, cc * P:(cc + 1) * P], ident_bf[:])
            last.then_inc(wtr_done, 1)
            pe.wait_ge(wtr_copied, 1)

            def cross_step(t, par, round_, more=True):
                scores(cross, t)
                if more:
                    cross_front_transposes(t + 1, 1 - par, round_ + par)
                    cross_front_products(t + 1)
                probs_transposes(cross, t)
                values(cross, t, par)
                cross_out(t)

            cross_step(0, 0, 0)
            cross_step(1, 1, 0)
            with pe.Fori(1, T // 2 - 1) as r:
                cross_step(2 * r, 0, r)
                cross_step(2 * r + 1, 1, r)
            cross_step(T - 2, 0, T // 2 - 1)
            cross_step(T - 1, 1, T // 2 - 1, more=False)

            own_front(0)

            def own_step(t, par, more=True):
                scores(own, t)
                if more:
                    own_front(t + 1)
                probs_transposes(own, t)
                values(own, t, par)
                own_out(t)

            own_step(0, 0)
            own_step(1, 1)
            with pe.Fori(1, T // 2 - 1) as r:
                own_step(2 * r, 0)
                own_step(2 * r + 1, 1)
            own_step(T - 2, 0)
            own_step(T - 1, 1, more=False)

            def logits(t):
                pe.wait_ge(xr_ready, t + 1)
                after(pe, gtr_copied, t)
                for k in range(KC):
                    last = transpose(bank_tr[:, k * P:(k + 1) * P], xn[:, k * P:(k + 1) * P], ident[:])
                last.then_inc(gtr_done, 1)
                pe.wait_ge(gtr_copied, t + 1)
                for k in range(KC):
                    last = pe.matmul(bank_qk[:, at(t * E, E)], oT[:, k, :], gate_sb[:, k, :],
                                     start=(k == 0), stop=(k == KC - 1))
                last.then_inc(logit_done, 1)

            logits(0)
            with pe.Fori(1, T) as t:
                logits(t)

            pe.wait_ge(oh_ready, 1)
            pe.wait_ge(tables_ready, TABLES)
            flat = oh_bf[:, :, :].rearrange("p t e -> p (t e)")
            n = T * E
            pe.matmul(bank_qk[:, 0:n], before[:], flat, start=True, stop=False, skip_group_check=True)
            for s in range(1, T):
                pe.matmul(bank_qk[:, s * E:n], ones_bf[:], flat[:, 0:n - s * E],
                          start=False, stop=(s == T - 1), skip_group_check=True)
            for t in range(T):
                last = pe.matmul(bank_qk[:, n:n + E], ones_bf[:], flat[:, t * E:(t + 1) * E],
                                 start=False, stop=(t == T - 1), skip_group_check=True)
            last.then_inc(rank_done, 1)

            pe.wait_ge(tile_ready, 1)
            pe.wait_ge(w_ready, 16 * 16)

            def up(j, par, round_):
                pe.wait_ge(xg_ready[par], 16 * (round_ + 1))
                after(pe, e_tr_copied, j)
                for k in range(KC):
                    last = transpose(bank_tr[:, k * P:(k + 1) * P], xg[:, par, k * P:(k + 1) * P], ident[:])
                last.then_inc(e_tr_done, 1)
                e = pe.value_load(tile_e[0:1, at(j, 1)], min_val=0, max_val=E - 1)
                pe.wait_ge(e_tr_copied, j + 1)
                after(pe, h_ready, 2 * j)
                for half in range(2):
                    for k in range(KC):
                        last = pe.matmul(bank_s[half][:, :], xgT[:, k, :],
                                         w1_sb[:, at(e, 1), k, half * 512:(half + 1) * 512].rearrange("p e f -> p (e f)"),
                                         start=(k == 0), stop=(k == KC - 1))
                    last.then_inc(up_done, 1)

            def hidden(j):
                for g in range(2):
                    pe.wait_ge(h_ready, 2 * j + g + 1)
                    after(pe, gelu_done, 2 * j)
                    for c in range(4):
                        last = transpose(bank_p[g][:, c * P:(c + 1) * P],
                                         h_sb[:, (4 * g + c) * P:(4 * g + c + 1) * P], ident[:])
                    last.then_inc(ht_done[g], 1)

            def down(j):
                e = pe.value_load(tile_e[0:1, at(j, 1)], min_val=0, max_val=E - 1)
                after(pe, y_sum, j)
                for c in range(FC):
                    if c % 4 == 0:
                        pe.wait_ge(gelu_done, 2 * j + c // 4 + 1)
                    last = pe.matmul(bank_o[:, 0:D], gT[:, c, :],
                                     w2_sb[:, at(e, 1), c, :].rearrange("p e d -> p (e d)"),
                                     start=(c == 0), stop=(c == FC - 1))
                last.then_inc(down_done, 1)

            up(0, 0, 0)
            def two_tiles(r):
                for par in range(2):
                    hidden(2 * r + par)
                    up(2 * r + par + 1, 1 - par, r + par)
                    down(2 * r + par)

            two_tiles(0)
            with pe.Fori(1, TILES // 2) as r:
                two_tiles(r)
            hidden(TILES - 1)
            down(TILES - 1)

        @block.vector
        def _(dve):
            def norm_stats(a_sem, b_sem, count, src, dst, src_sem):
                dve.bn_stats(stats[:], src).then_inc(a_sem, 1)
                dve.wait_ge(a_sem, count)
                return dve.bn_aggr(dst, stats[:]).then_inc(b_sem, 1)

            dve.wait_ge(const_ready, CONSTS)
            dve.wait_ge(rows_ready, 16 * 12)
            dve.wait_ge(x_ready, 16)
            for t in range(T):
                norm_stats(x_stats, x_stats, 2 * t + 1, x_sb[:, t, :], mv[:, 0, t, :], None)
                dve.wait_ge(x_stats, 2 * t + 2)
            dve.tensor_scalar(ve[:, 0], mv[:, 0, :, 1], LN_EPS, None, ALU.add).then_inc(x_ve, 1)

            def cross_norm(t):
                dve.wait_ge(x_rstd, 1)
                after(dve, cross.tr_done, t)
                dve.tensor_scalar(xn[:], x_sb[:, at(t, 1), :].rearrange("p a d -> p (a d)"),
                                  mv[:, 0, at(t, 1), 0], rstd[:, 0, at(t, 1)],
                                  ALU.subtract, ALU.mult).then_inc(cross.xn_ready, 1)

            def key_blocks(a, t, src, src_sem):
                dve.wait_ge(src_sem, t + 1)
                after(dve, a.scores_done, 2 * t)
                for g in range(KC):
                    for b in range(2):
                        last = dve.tensor_tensor(
                            k_bd[:, g, b], src[:, g, S * b:S * b + S].unsqueeze(1).to_broadcast([P, HG, S]),
                            head_mask[:].unsqueeze(2).to_broadcast([P, HG, S]), ALU.mult)
                last.then_inc(a.kbd_ready, 1)

            def value_blocks(a, t, par, put):
                dve.wait_ge(a.v_done, t + 1)
                if not isinstance(t, int) or t >= 2:
                    dve.wait_ge(a.pv_done, t - 1)
                for b in range(2):
                    for odd in range(2):
                        src = bank_v[S * b:S * b + S, 0:D].rearrange("p (c o d) -> p c o d", o=2, d=HD)[:, :, odd, :]
                        dst = v_bd[S * odd:S * odd + S, par, b, :, HD * odd:HD * odd + HD]
                        last = put(dst, src, S * b, odd)
                last.then_inc(a.vbd_ready, 1)

            def cross_values(dst, src, row, odd):
                bias = bv_row[row:row + S, :].rearrange("p (c o d) -> p c o d", o=2, d=HD)[:, :, odd, :]
                return dve.tensor_tensor(dst, src, bias, ALU.add)

            def own_values(dst, src, row, odd):
                return dve.tensor_scalar(dst, src, deq[row:row + S, 2:3], None, ALU.mult)

            def shift(a, t):
                for g in range(2):
                    dve.wait_ge(a.scores_done, 2 * t + g + 1)
                    s = bank_s[g][:, :].rearrange("p (h s) -> p h s", s=S)
                    dve.tensor_reduce(rmax[:, HG * g:HG * g + HG], s, AX.X, ALU.max).then_inc(a.max_done, 1)
                    dve.wait_ge(a.max_done, 2 * t + g + 1)
                    after(dve, a.pt_done[g], t)
                    dve.tensor_tensor(probs[:, HG * g:HG * g + HG, :], s,
                                      rmax[:, HG * g:HG * g + HG].unsqueeze(2).to_broadcast([P, HG, S]),
                                      ALU.subtract).then_inc(a.shifted[g], 1)

            def copy_probs(a, t):
                dve.wait_ge(a.pt_done[1], t + 1)
                after(dve, a.pv_done, t)
                dve.tensor_copy(pT[:, 4:8, :].rearrange("p a b -> p (a b)"), bank_p[1][:]).then_inc(a.pt1_copied, 1)

            def normalise(a, t):
                o = bank_o[:, 0:PAIRS * VW].rearrange("p (c w) -> p c w", w=VW)
                dve.wait_ge(a.pv_done, t + 1)
                dve.reciprocal(rinv[:], o[:, :, 2 * HD:]).then_inc(a.rinv_ready, 1)
                dve.wait_ge(a.rinv_ready, t + 1)
                after(dve, a.ot_done, t)
                dve.tensor_tensor(o_sb[:, :].rearrange("p (c o d) -> p c o d", o=2, d=HD),
                                  o[:, :, 0:2 * HD].rearrange("p c (o d) -> p c o d", d=HD),
                                  rinv[:].unsqueeze(3).to_broadcast([P, PAIRS, 2, HD]),
                                  ALU.mult).then_inc(a.o_ready, 1)

            def next_stats(a, t, n):
                dve.wait_ge(x_ready, 16)
                dve.wait_ge(a.x_done, t + 1)
                dve.bn_stats(stats[:], x_sb[:, at(t, 1), :].rearrange("p a d -> p (a d)")).then_inc(a.stats_done, 1)
                dve.wait_ge(x_ready, 16)
                dve.wait_ge(a.stats_done, t + 1)
                dve.bn_aggr(mv_tile[:], stats[:]).then_inc(a.mv_done, 1)
                dve.wait_ge(a.mv_done, 2 * t + 1)
                dve.tensor_copy(mv[:, n, at(t, 1), :].rearrange("p a d -> p (a d)"), mv_tile[:]).then_inc(a.mv_done, 1)

            def cross_residual(t):
                dve.wait_ge(cross.out_done, t + 1)
                xt = x_sb[:, at(t, 1), :].rearrange("p a d -> p (a d)")
                dve.tensor_tensor(xt, bank_p[1][:, 0:D], xt, ALU.add).then_inc(cross.x_done, 1)
                next_stats(cross, t, 1)

            cross_norm(0)
            dve.wait_ge(bias_done, 1)
            dve.tensor_copy(bias_col[:], bank_o[:, 0:E * FC + 2 * KC]).then_inc(bias_ready, 1)
            key_blocks(cross, 0, kT, cross.k_ready)
            value_blocks(cross, 0, 0, cross_values)

            dve.wait_ge(raw_ready, 64)
            dve.tensor_reduce(wabs[:], wraw.rearrange("p w k d -> p w (k d)"), AX.X, ALU.add,
                              apply_absolute_value=True).then_inc(wabs_ready, 1)
            dve.wait_ge(wtot_done, 1)
            dve.tensor_scalar(wscale[:], bank_o[:, 0:4], 1.0 / (D * D), Q_EPS, ALU.mult, ALU.max).then_inc(wscale_ready, 1)
            dve.wait_ge(wscale_ready, 1)
            dve.reciprocal(wrecip[:], wscale[:]).then_inc(wscale_ready, 1)
            dve.tensor_tensor(qk_scale[:], wscale[:, 0:1], wscale[:, 1:2], ALU.mult).then_inc(wscale_ready, 1)
            dve.wait_ge(wrounded, 4)
            flat = wraw.rearrange("p w k d -> p (w k d)")
            dve.tensor_scalar(flat, flat, -ROUND, -1.0, ALU.add, ALU.max).then_inc(wscale_ready, 1)
            dve.wait_ge(wscale_ready, 4)
            dve.tensor_scalar(wround[:].rearrange("p w k d -> p (w k d)"), flat, 1.0, None,
                              ALU.min).then_inc(wint_ready, 1)
            dve.wait_ge(wtr_done, 1)
            for h in range(2):
                last = dve.tensor_copy(wtern[:, 2 * h:2 * h + 2].rearrange("p w k d -> p (w k d)"),
                                       bank_p[h][:, :].bitcast(BF16))
            last.then_inc(wtr_copied, 1)

            def add_bo(t):
                dve.wait_ge(cross.xn_ready, t + 1)
                xt = x_sb[:, at(t, 1), :].rearrange("p a d -> p (a d)")
                dve.tensor_tensor(xt, xt, bo_row[:], ALU.add).then_inc(bo_added, 1)

            def cross_step(t, par, more=True):
                if more:
                    cross_norm(t + 1)
                shift(cross, t)
                if more:
                    key_blocks(cross, t + 1, kT, cross.k_ready)
                    value_blocks(cross, t + 1, 1 - par, cross_values)
                add_bo(t)
                copy_probs(cross, t)
                normalise(cross, t)
                dve.wait_ge(bo_added, t + 1)
                cross_residual(t)

            cross_step(0, 0)
            cross_step(1, 1)
            with dve.Fori(1, T // 2 - 1) as r:
                cross_step(2 * r, 0)
                cross_step(2 * r + 1, 1)
            cross_step(T - 2, 0)
            cross_step(T - 1, 1, more=False)

            dve.wait_ge(cross.mv_done, 2 * T)
            dve.tensor_scalar(ve[:, 1], mv[:, 1, :, 1], LN_EPS, None, ALU.add).then_inc(ln1_ve, 1)
            dve.wait_ge(ln1_r, 1)
            dve.tensor_tensor(ve[:, 2], mv[:, 1, :, 1], rstd[:, 1], ALU.mult).then_inc(both1, 1)
            dve.wait_ge(both1, 1)
            dve.tensor_tensor(ve[:, 2], ve[:, 2], rstd[:, 1], ALU.mult).then_inc(both1, 1)
            dve.wait_ge(both1, 2)
            dve.tensor_scalar(ve[:, 3], ve[:, 2], RMS_EPS, None, ALU.add).then_inc(ln1_ve, 1)
            dve.wait_ge(ln1_r, 2)
            dve.tensor_tensor(rboth[:, 0], rboth[:, 0], rstd[:, 1], ALU.mult).then_inc(both1, 1)
            dve.wait_ge(both1, 3)

            dve.tensor_scalar(wfac[:, 0:1], qk_scale[:], SCALE, None, ALU.mult)
            dve.memset(wfac[:, 1:2], 1.0)
            dve.tensor_copy(wfac[:, 2:3], wscale[:, 2:3]).then_inc(both1, 1)
            dve.wait_ge(both1, 4)

            def tile_of(buf, t):
                return buf[:, at(t, 1), :].rearrange("p a d -> p (a d)")

            def own_norm(t, par):
                dve.tensor_scalar(xn[:], tile_of(x_sb, t), mv[:, 1, at(t, 1), 0], rboth[:, 0, at(t, 1)],
                                  ALU.subtract, ALU.mult).then_inc(own.xn_ready, 1)
                dve.wait_ge(own.xn_ready, t + 1)
                dve.tensor_tensor(z[:], xn[:].unsqueeze(1).to_broadcast([P, 3, D]), g_row[:, 0:3],
                                  ALU.mult).then_inc(own.z_ready, 1)
                dve.wait_ge(own.z_ready, t + 1)
                dve.tensor_reduce(amax[:], z[:], AX.X, ALU.max, apply_absolute_value=True).then_inc(own.amax_ready, 1)
                dve.wait_ge(own.amax_ready, 2 * t + 1)
                dve.tensor_scalar(amax[:], amax[:], Q_EPS, 1.0 / 127, ALU.max, ALU.mult).then_inc(own.amax_ready, 1)
                dve.wait_ge(own.amax_ready, 2 * t + 2)
                after(dve, own.rounded, t)
                dve.reciprocal(arecip[:], amax[:]).then_inc(own.qscale_ready, 1)
                if not isinstance(t, int) or t >= 2:
                    dve.wait_ge(own.exp_done, 2 * t - 2)
                    dve.wait_ge(own.k_ready, t - 1)
                dve.tensor_tensor(deq[:, par], amax[:], wfac[:], ALU.mult).then_inc(own.deq_ready, 1)

            def own_ints(t):
                dve.wait_ge(own.rounded, t + 1)
                after(dve, own.tr_done, t)
                dve.tensor_scalar(zi[:].rearrange("p n d -> p (n d)"), z[:].rearrange("p n d -> p (n d)"),
                                  -ROUND, 127.0, ALU.add, ALU.min).then_inc(own.ints_ready, 1)

            def own_values(par):
                def put(dst, src, row, odd):
                    return dve.tensor_scalar(dst, src, deq[row:row + S, par, 2:3], None, ALU.mult)
                return put

            def own_residual(t):
                dve.wait_ge(own.o_ready, t + 1)
                after(dve, own.orms_ready, t)
                dve.tensor_tensor_reduce(osq[:], o_sb[:], o_sb[:], 1.0 / D, RMS_EPS, ALU.mult, ALU.add,
                                         small[:, 0:1]).then_inc(own.sumsq_ready, 1)
                dve.wait_ge(own.orms_ready, t + 1)
                dve.scalar_tensor_tensor(o_sb[:], o_sb[:], small[:, 1:2], g_row[:, 3], ALU.mult,
                                         ALU.mult).then_inc(own.oz_ready, 1)
                dve.wait_ge(own.oz_ready, t + 1)
                dve.tensor_reduce(small[:, 2:3], o_sb[:], AX.X, ALU.max,
                                  apply_absolute_value=True).then_inc(own.omax_ready, 1)
                dve.wait_ge(own.omax_ready, 2 * t + 1)
                dve.tensor_scalar(small[:, 3:4], small[:, 2:3], Q_EPS, 1.0 / 127, ALU.max,
                                  ALU.mult).then_inc(own.omax_ready, 1)
                dve.wait_ge(own.omax_ready, 2 * t + 2)
                dve.reciprocal(small[:, 4:5], small[:, 3:4]).then_inc(own.oscale_ready, 1)
                dve.tensor_tensor(small[:, 5:6], small[:, 3:4], wscale[:, 3:4], ALU.mult)
                dve.wait_ge(own.oscale_ready, t + 1)
                dve.tensor_scalar(osq[:], o_sb[:], small[:, 4:5], ROUND, ALU.mult, ALU.add).then_inc(own.orounded, 1)
                dve.wait_ge(own.orounded, t + 1)
                after(dve, own.ot_done, t)
                dve.tensor_scalar(oi[:], osq[:], -ROUND, 127.0, ALU.add, ALU.min).then_inc(own.oints_ready, 1)
                dve.wait_ge(own.out_done, t + 1)
                dve.scalar_tensor_tensor(tile_of(x_sb, t), bank_p[1][:, 0:D], small[:, 5:6], tile_of(x_sb, t),
                                         ALU.mult, ALU.add).then_inc(own.x_done, 1)
                next_stats(own, t, 2)

            def key_blocks_own(t):
                key_blocks(own, t, bank_tr[:, 0:D].rearrange("p (k s) -> p k s", k=KC), own.kt_done)

            own_norm(0, 0)
            own_ints(0)
            key_blocks_own(0)
            value_blocks(own, 0, 0, own_values(0))

            def own_step(t, par, more=True):
                if more:
                    own_norm(t + 1, 1 - par)
                shift(own, t)
                if more:
                    own_ints(t + 1)
                    key_blocks_own(t + 1)
                    value_blocks(own, t + 1, 1 - par, own_values(1 - par))
                copy_probs(own, t)
                normalise(own, t)
                own_residual(t)

            own_step(0, 0)
            own_step(1, 1)
            with dve.Fori(1, T // 2 - 1) as r:
                own_step(2 * r, 0)
                own_step(2 * r + 1, 1)
            own_step(T - 2, 0)
            own_step(T - 1, 1, more=False)

            chained = [0]

            def link(ins):
                chained[0] += 1
                ins.then_inc(g_chain, 1)
                dve.wait_ge(g_chain, chained[0])

            dve.wait_ge(own.mv_done, 2 * T)
            dve.tensor_scalar(ve[:, 2], mv[:, 2, :, 1], LN_EPS, None, ALU.add).then_inc(ln2_ve, 1)
            dve.wait_ge(ln2_r, 1)
            link(dve.tensor_tensor(ve[:, 5], mv[:, 2, :, 1], rstd[:, 2], ALU.mult))
            link(dve.tensor_tensor(ve[:, 5], ve[:, 5], rstd[:, 2], ALU.mult))
            dve.tensor_scalar(ve[:, 5], ve[:, 5], LN_EPS, None, ALU.add).then_inc(ln2_ve, 1)
            link(dve.tensor_scalar(base_f[:, 0], rstd[:, 2], 1.0, None, ALU.add))
            dve.scalar_tensor_tensor(base_f[:, 1], mv[:, 2, :, 0], -1.0, rstd[:, 2], ALU.mult,
                                     ALU.mult).then_inc(both1, 1)
            dve.wait_ge(ln2_r, 2)
            link(dve.tensor_tensor(rboth[:, 1], rboth[:, 1], rstd[:, 2], ALU.mult))

            def expert_norm(t):
                after(dve, xr_ready, t)
                dve.scalar_tensor_tensor(osq[:], tile_of(x_sb, t), mv[:, 2, at(t, 1), 0], gamma_row[:],
                                         ALU.subtract, ALU.mult).then_inc(x_read, 1)
                dve.wait_ge(x_read, t + 1)
                after(dve, gtr_done, t)
                after(dve, row_copied, t)
                dve.scalar_tensor_tensor(xn[:], osq[:], rboth[:, 1, at(t, 1)], beta_row[:],
                                         ALU.mult, ALU.add).then_inc(xr_ready, 1)

            expert_norm(0)
            with dve.Fori(1, T) as t:
                expert_norm(t)

            def wide(a):
                return a.unsqueeze(2).to_broadcast([P, T, E])

            lg = bank_qk[:, 0:T * E].rearrange("p (t e) -> p t e", e=E)
            dve.wait_ge(logit_done, T)
            link(dve.tensor_reduce(gm[:, 0], lg, AX.X, ALU.max))
            dve.tensor_tensor(gp[:], lg, wide(gm[:, 0]), ALU.subtract).then_inc(max_ready, 1)
            dve.wait_ge(exp_ready, 1)
            link(dve.tensor_reduce(gm[:, 1], gp[:], AX.X, ALU.add))
            link(dve.reciprocal(gm[:, 0], gm[:, 1]))
            link(dve.tensor_tensor(gp[:], gp[:], wide(gm[:, 0]), ALU.mult))
            for k, p in enumerate((gp, gp2)):
                link(dve.tensor_reduce(gm[:, k], p[:], AX.X, ALU.max))
                link(dve.tensor_tensor(eq[:], p[:], wide(gm[:, k]), ALU.is_equal))
                link(dve.tensor_tensor(eq[:], eq[:], rev[:].unsqueeze(1).to_broadcast([P, T, E]), ALU.mult))
                link(dve.tensor_reduce(gm[:, 2], eq[:], AX.X, ALU.max))
                link(dve.tensor_tensor(oh[:, k], eq[:], wide(gm[:, 2]), ALU.is_equal))
                if k == 0:
                    link(dve.scalar_tensor_tensor(gp2[:].rearrange("p t e -> p (t e)"),
                                                  oh[:, 0].rearrange("p t e -> p (t e)"), -2.0,
                                                  gp[:].rearrange("p t e -> p (t e)"), ALU.mult, ALU.add))
            dve.tensor_tensor(oh_bf[:], oh[:, 0], oh[:, 1], ALU.add).then_inc(oh_ready, 1)
            link(dve.tensor_tensor(gm[:, 2], gm[:, 0], gm[:, 1], ALU.add))
            link(dve.reciprocal(gm[:, 3], gm[:, 2]))
            link(dve.tensor_tensor(gm[:, 0:2], gm[:, 0:2],
                                   gm[:, 3].unsqueeze(1).to_broadcast([P, 2, T]), ALU.mult))
            link(dve.tensor_tensor(gp[:], oh[:, 0], wide(gm[:, 0]), ALU.mult))
            link(dve.tensor_tensor(gp2[:], oh[:, 1], wide(gm[:, 1]), ALU.mult))
            dve.wait_ge(tables_ready, TABLES)
            dve.tensor_tensor(xr[:, :, D + 1:ROW], gp[:], gp2[:], ALU.add).then_inc(cw_ready, 1)
            dve.wait_ge(rank_done, 1)
            n = T * E
            link(dve.tensor_scalar(cnt_i[:, 0], bank_qk[:, n:n + E], P - 1.0, None, ALU.add))
            link(dve.tensor_scalar(cnt_i[:, 1], cnt_i[:, 0], 7, None, ALU.logical_shift_right))
            link(dve.tensor_copy(cnt[:, 0], cnt_i[:, 1]))
            link(dve.tensor_tensor_scan(cnt[:, 1], ones[:, 0:E], cnt[:, 0], 0.0, ALU.mult, ALU.add))
            link(dve.tensor_tensor(cnt[:, 2], cnt[:, 1], cnt[:, 0], ALU.subtract))
            link(dve.tensor_scalar(cnt[:, 2], cnt[:, 2], float(P), None, ALU.mult))
            link(dve.tensor_tensor(slots[:], lg, cnt[:, 2].unsqueeze(1).to_broadcast([P, T, E]), ALU.add))
            for k in range(TOPK):
                link(dve.tensor_tensor(eq[:], oh[:, k], slots[:], ALU.mult))
                link(dve.tensor_reduce(slot_f[:, k], eq[:], AX.X, ALU.add))
            dve.tensor_copy(slot_i[:], slot_f[:]).then_inc(slot_ready, 1)
            link(dve.tensor_tensor(tile_cmp[:], tile_no[:].unsqueeze(2).to_broadcast([P, TILES, E]),
                                   cnt[:, 1].unsqueeze(1).to_broadcast([P, TILES, E]), ALU.is_ge))
            link(dve.tensor_reduce(tile_f[:], tile_cmp[:], AX.X, ALU.add))
            dve.tensor_scalar(tile_e[:], tile_f[:], E - 1.0, None, ALU.min).then_inc(tile_ready, 1)

            def hidden(j):
                for g in range(2):
                    dve.wait_ge(up_done, 2 * j + g + 1)
                    after(dve, ht_done[g], j)
                    dve.tensor_copy(h_sb[:, g * 512:(g + 1) * 512], bank_s[g][:]).then_inc(h_ready, 1)

            def weighted(j, par, round_):
                e = dve.value_load(tile_e[0:1, at(j, 1)], min_val=0, max_val=E - 1)
                dve.wait_ge(xg_ready[par], 16 * (round_ + 1))
                after(dve, y_added[par], 16 * round_)
                dve.tensor_copy(tok_i[:, par:par + 1], xg[:, par, D:D + 1]).then_inc(tok_ready, 1)
                dve.wait_ge(down_done, j + 1)
                dve.tensor_tensor(y_sb[:, par, :], bank_o[:, 0:D],
                                  b2_row[:, at(e, 1), :].rearrange("p a d -> p (a d)"), ALU.add).then_inc(y_sum, 1)
                dve.wait_ge(y_sum, j + 1)
                dve.tensor_scalar(y_sb[:, par, :], y_sb[:, par, :], xg[:, par, bass.ds(e + D + 1, 1)], None,
                                  ALU.mult).then_inc(y_ready, 1)

            dve.wait_ge(tile_ready, 1)
            dve.wait_ge(b2_ready, 16)
            hidden(0)
            def two_tiles(r):
                for par in range(2):
                    hidden(2 * r + par + 1)
                    weighted(2 * r + par, par, r)

            two_tiles(0)
            with dve.Fori(1, TILES // 2) as r:
                two_tiles(r)
            weighted(TILES - 1, 0, TILES // 2)

        @block.scalar
        def _(act):
            for e in range(E):
                act.dma_start(w1_sb[:, e], w1[e].rearrange("(k p) f -> p k f", p=P)).then_inc(w_ready, 16)
                if e < E - 1:
                    act.dma_start(w2_sb[:, e], w2[e].rearrange("(c p) d -> p c d", p=P)).then_inc(w_ready, 16)

            def copy(dst, src):
                return act.activation(dst, src, ACT.Copy)

            def exps(a, t, scale):
                for g in range(2):
                    act.wait_ge(a.shifted[g], t + 1)
                    p = probs[:, HG * g:HG * g + HG, :].rearrange("p h s -> p (h s)")
                    act.activation(p, p, ACT.Exp, scale=scale).then_inc(a.exp_done, 1)

            def cross_front(t):
                act.wait_ge(cross.tr_done, t + 1)
                after(act, cross.v_done, t)
                copy(xcT[:], bank_tr[:]).then_inc(cross.tr_copied, 1)

            def cross_qk(t):
                act.wait_ge(cross.qk_done, t + 1)
                after(act, cross.scores_done, 2 * t)
                for f in range(KC):
                    last = act.activation(qT[:, f, :], bank_qk[:, f * P:(f + 1) * P], ACT.Identity,
                                          bias=bq_col[:, f:f + 1])
                last.then_inc(cross.q_ready, 1)
                after(act, cross.kbd_ready, t)
                for f in range(KC):
                    last = act.activation(kT[:, f, :], bank_qk[:, (KC + f) * P:(KC + f + 1) * P], ACT.Identity,
                                          bias=bk_col[:, f:f + 1])
                last.then_inc(cross.k_ready, 1)

            def copy_probs(a, t):
                act.wait_ge(a.pt_done[0], t + 1)
                after(act, a.pv_done, t)
                copy(pT[:, 0:4, :].rearrange("p a b -> p (a b)"), bank_p[0][:]).then_inc(a.pt0_copied, 1)

            def cross_out(t):
                act.wait_ge(cross.ot_done, t + 1)
                after(act, cross.out_done, t)
                copy(oT[:].rearrange("p a b -> p (a b)"), bank_p[0][:, 0:D]).then_inc(cross.ot_copied, 1)

            cross_front(0)
            act.wait_ge(bias_ready, 1)
            cross_qk(0)
            act.wait_ge(wscale_ready, 2)
            act.wait_ge(const_ready, CONSTS)
            for w in range(4):
                v = wraw[:, w].rearrange("p k d -> p (k d)")
                act.activation(v, v, ACT.Identity, scale=wrecip[:, w:w + 1], bias=round_col[:]).then_inc(wrounded, 1)

            def cross_step(t, more=True):
                if more:
                    cross_front(t + 1)
                exps(cross, t, SCALE)
                if more:
                    cross_qk(t + 1)
                copy_probs(cross, t)
                cross_out(t)

            cross_step(0)
            with act.Fori(1, T - 1) as t:
                cross_step(t)
            cross_step(T - 1, more=False)

            def own_round(t):
                act.wait_ge(own.qscale_ready, t + 1)
                for n in range(3):
                    last = act.activation(z[:, n], z[:, n], ACT.Identity, scale=arecip[:, n:n + 1], bias=round_col[:])
                last.then_inc(own.rounded, 1)

            def own_front(t, par):
                act.wait_ge(own.tr_done, t + 1)
                after(act, own.v_done, t)
                copy(ziT[:].rearrange("p a b c -> p (a b c)"),
                     bank_tr[:, :].bitcast(BF16)[:, 0:3 * D]).then_inc(own.tr_copied, 1)
                act.wait_ge(own.qk_done, t + 1)
                after(act, own.scores_done, 2 * t)
                copy(qT[:].rearrange("p a b -> p (a b)"), bank_qk[:, 0:D]).then_inc(own.q_ready, 1)
                after(act, own.kt_done, t)
                act.wait_ge(own.deq_ready, t + 1)
                act.activation(kT[:].rearrange("p a b -> p (a b)"), bank_qk[:, D:2 * D], ACT.Copy,
                               scale=deq[:, par, 1:2]).then_inc(own.k_ready, 1)

            def own_out(t):
                act.wait_ge(own.ot_done, t + 1)
                after(act, own.out_done, t)
                copy(oiT[:].rearrange("p a b -> p (a b)"),
                     bank_p[0][:, :].bitcast(BF16)[:, 0:D]).then_inc(own.ot_copied, 1)

            own_round(0)
            own_front(0, 0)

            def own_step(t, par, more=True):
                if more:
                    own_round(t + 1)
                exps(own, t, deq[:, par, 0:1])
                if more:
                    own_front(t + 1, 1 - par)
                copy_probs(own, t)
                own_out(t)

            own_step(0, 0)
            own_step(1, 1)
            with act.Fori(1, T // 2 - 1) as r:
                own_step(2 * r, 0)
                own_step(2 * r + 1, 1)
            own_step(T - 2, 0)
            own_step(T - 1, 1, more=False)

            act.wait_ge(both1, 5)
            def expert_rows(t):
                act.wait_ge(x_read, t + 1)
                xt = x_sb[:, at(t, 1), :].rearrange("p a d -> p (a d)")
                act.activation(xt, xt, ACT.Identity, scale=base_f[:, 0, at(t, 1)],
                               bias=base_f[:, 1, at(t, 1)]).then_inc(base_ready, 1)
                act.wait_ge(xr_ready, t + 1)
                copy(xr[:, at(t, 1), 0:D].rearrange("p a d -> p (a d)"), xn[:]).then_inc(row_copied, 1)
                act.wait_ge(gtr_done, t + 1)
                after(act, logit_done, t)
                copy(oT[:].rearrange("p a b -> p (a b)"), bank_tr[:, 0:D]).then_inc(gtr_copied, 1)

            expert_rows(0)
            with act.Fori(1, T) as t:
                expert_rows(t)
            act.wait_ge(max_ready, 1)
            act.activation(gp[:], gp[:], ACT.Exp).then_inc(exp_ready, 1)

            def rows_transposed(j):
                act.wait_ge(e_tr_done, j + 1)
                after(act, up_done, 2 * j)
                copy(xgT[:].rearrange("p a b -> p (a b)"), bank_tr[:, 0:D]).then_inc(e_tr_copied, 1)

            def gelus(j):
                e = act.value_load(tile_e[0:1, at(j, 1)], min_val=0, max_val=E - 1)
                after(act, down_done, j)
                for g in range(2):
                    act.wait_ge(ht_done[g], j + 1)
                    for c in range(4):
                        last = act.activation(gT[:, 4 * g + c, :], bank_p[g][:, c * P:(c + 1) * P], ACT.Gelu,
                                              bias=b1_col[:, bass.ds(e * FC + (4 * g + c), 1)])
                    last.then_inc(gelu_done, 1)

            act.wait_ge(tile_ready, 1)
            rows_transposed(0)
            gelus(0)
            rows_transposed(1)
            with act.Fori(1, TILES - 1) as j:
                gelus(j)
                rows_transposed(j + 1)
            gelus(TILES - 1)


_INS = ['x', 'ctx_1024', 'L0_xattn_Wq', 'L0_xattn_bq', 'L0_xattn_Wk', 'L0_xattn_bk', 'L0_xattn_Wv', 'L0_xattn_bv',
        'L0_xattn_Wo', 'L0_xattn_bo', 'L0_attn_wq', 'L0_attn_wk', 'L0_attn_wv', 'L0_attn_wo', 'L0_attn_gq',
        'L0_attn_gk', 'L0_attn_gv', 'L0_attn_go', 'L0_ffn_gate_w', 'L0_ffn_w1', 'L0_ffn_b1', 'L0_ffn_w2',
        'L0_ffn_b2', 'L0_ffn_gamma', 'L0_ffn_beta']


def kernel(**inputs):
    import concourse.bacc as bacc
    from concourse.bass_utils import run_bass_kernel_spmd

    nc = bacc.Bacc("TRN2", target_bir_lowering=False, num_devices=1)
    arrays, args = {}, []
    for name in _INS:
        a = np.ascontiguousarray(inputs[name])
        arrays[f"in_{name}"] = a
        args.append(nc.dram_tensor(f"in_{name}", a.shape, mybir.dt.from_np(a.dtype), kind="ExternalInput").ap())
    args.append(nc.dram_tensor("rows", (TILES * P, ROW), F32, kind="Internal").ap())
    args.append(nc.dram_tensor("acc", (TOK + P, D), F32, kind="Internal").ap())
    args.append(nc.dram_tensor("out", (B, S, D), F32, kind="ExternalOutput").ap())
    program(nc, *args)
    r = run_bass_kernel_spmd(nc, [arrays], core_ids=[0])
    return r.results[0]["out"]
```

```python
from contextlib import ExitStack

import numpy as np

import concourse.bass as bass
from concourse import mybir
from concourse.alu_op_type import AluOpType as ALU

ACT = mybir.ActivationFunctionType
AX = mybir.AxisListType
F32 = mybir.dt.float32
BF16 = mybir.dt.bfloat16
I32 = mybir.dt.int32

P = 128
B, S, D = 16, 64, 256
TOK = B * S
T = TOK // P
KC = D // P
H, HD = 16, 16
HG = P // HD
PAIRS = H // 2
VW = 2 * HD + 2
E, FF, TOPK = 8, 1024, 2
FC = FF // P
TILES = TOPK * T + E - 1
ROW = D + 1 + E
LN_EPS, RMS_EPS, Q_EPS = 1e-5, 1e-6, 1e-5
ROUND = 12582912.0
MASKED = -1e30
SCALE = HD ** -0.5


def at(start, size):
    return slice(start, start + size) if isinstance(start, int) else bass.ds(start, size)


def after(engine, semaphore, count):
    if not (isinstance(count, int) and count <= 0):
        engine.wait_ge(semaphore, count)


class Attention:

    def __init__(self, sem, name):
        self.xn_ready = sem(f"{name}_xn_ready")
        self.z_ready = sem(f"{name}_z_ready")
        self.amax_ready = sem(f"{name}_amax_ready")
        self.qscale_ready = sem(f"{name}_qscale_ready")
        self.deq_ready = sem(f"{name}_deq_ready")
        self.rounded = sem(f"{name}_rounded")
        self.ints_ready = sem(f"{name}_ints_ready")
        self.tr_done = sem(f"{name}_tr_done")
        self.tr_copied = sem(f"{name}_tr_copied")
        self.qk_done = sem(f"{name}_qk_done")
        self.v_done = sem(f"{name}_v_done")
        self.q_ready = sem(f"{name}_q_ready")
        self.k_ready = sem(f"{name}_k_ready")
        self.kt_done = sem(f"{name}_kt_done")
        self.kbd_low_ready = sem(f"{name}_kbd_low_ready")
        self.kbd_high_ready = sem(f"{name}_kbd_high_ready")
        self.vbd_ready = sem(f"{name}_vbd_ready")
        self.scores_done = sem(f"{name}_scores_done")
        self.max_done = sem(f"{name}_max_done")
        self.exp_done = sem(f"{name}_exp_done")
        self.pt0_copied = sem(f"{name}_pt0_copied")
        self.pt1_copied = sem(f"{name}_pt1_copied")
        self.pv_done = sem(f"{name}_pv_done")
        self.rinv_ready = sem(f"{name}_rinv_ready")
        self.o_ready = sem(f"{name}_o_ready")
        self.sumsq_ready = sem(f"{name}_sumsq_ready")
        self.orms_ready = sem(f"{name}_orms_ready")
        self.oz_ready = sem(f"{name}_oz_ready")
        self.omax_ready = sem(f"{name}_omax_ready")
        self.oscale_ready = sem(f"{name}_oscale_ready")
        self.orounded = sem(f"{name}_orounded")
        self.oints_ready = sem(f"{name}_oints_ready")
        self.ot_done = sem(f"{name}_ot_done")
        self.ot_copied = sem(f"{name}_ot_copied")
        self.out_done = sem(f"{name}_out_done")
        self.x_done = sem(f"{name}_x_done")
        self.stats_done = sem(f"{name}_stats_done")
        self.mv_done = sem(f"{name}_mv_done")
        self.ctx_ready = [sem(f"{name}_ctx_ready{k}") for k in range(2)]
        self.shifted = [sem(f"{name}_shifted{k}") for k in range(2)]
        self.pt_done = [sem(f"{name}_pt_done{k}") for k in range(2)]


def program(nc, x, ctx_in, xWq, xbq, xWk, xbk, xWv, xbv, xWo, xbo, awq, awk, awv, awo,
            agq, agk, agv, ago, gate_w, w1, b1, w2, b2, gamma, beta, rows, acc, out):
    x_rows = x.rearrange("b s d -> (b s) d")
    out_rows = out.rearrange("b s d -> (b s) d")

    with ExitStack() as stack:
        def sb(name, shape, dt=F32):
            return stack.enter_context(nc.sbuf_tensor(name, shape, dt))

        def bank(name):
            return stack.enter_context(nc.psum_tensor(name, [P, 512], F32))

        def sem(name):
            return stack.enter_context(nc.semaphore(name))

        w1_sb = sb("w1_sb", [P, E, KC, FF])
        w2_sb = sb("w2_sb", [P, E, FC, D])
        wraw = w2_sb[:, E - 1].rearrange("p (w k) d -> p w k d", k=KC)
        bias_rows = sb("bias_rows", [E * FC + 2 * KC, P])
        bias_col = sb("bias_col", [P, E * FC + 2 * KC])
        b1_col = bias_col[:, 0:E * FC]
        bq_col = bias_col[:, E * FC:E * FC + KC]
        bk_col = bias_col[:, E * FC + KC:E * FC + 2 * KC]
        wproj = sb("wproj", [P, 4, KC, D])
        wtern = sb("wtern", [P, 4, KC, D], BF16)
        wabs = sb("wabs", [P, 4])
        wscale = sb("wscale", [P, 4])
        wrecip = sb("wrecip", [P, 4])
        qk_scale = sb("qk_scale", [P, 1])
        bv_row = sb("bv_row", [P, D])
        bo_row = sb("bo_row", [P, D])
        g_row = sb("g_row", [P, 4, D])
        gamma_row = sb("gamma_row", [P, D])
        beta_row = sb("beta_row", [P, D])
        gate_sb = sb("gate_sb", [P, KC, E])
        ident = sb("ident", [P, P])
        ident_bf = sb("ident_bf", [P, P], BF16)
        ones_bf = sb("ones_bf", [P, P], BF16)
        ones = sb("ones", [P, P])
        before = sb("before", [P, P], BF16)
        odd_head = sb("odd_head", [P, 2])
        causal = sb("causal", [P, S], BF16)
        neg_half = sb("neg_half", [P, T])
        round_col = sb("round_col", [P, 1])
        head_mask = sb("head_mask", [P, HG])

        x_sb = sb("x_sb", [P, T, D])
        xr = sb("xr", [P, T, ROW])
        stats = sb("stats", [P, 6])
        mv_tile = sb("mv_tile", [P, 2])
        mv = sb("mv", [P, 3, T, 2])
        ve = sb("ve", [P, 6, T])
        rstd = sb("rstd", [P, 3, T])
        rboth = sb("rboth", [P, 2, T])
        ctx_sb = sb("ctx_sb", [P, 2, D])
        xn = sb("xn", [P, D])
        xcT = sb("xcT", [P, 4 * P])
        qT = sb("qT", [P, KC, P])
        kT = sb("kT", [P, KC, P])
        k_bd = sb("k_bd", [P, KC, 2, HG, S])
        v_bd = sb("v_bd", [P, 2, 2, PAIRS, VW])
        rmax = sb("rmax", [P, H])
        probs = sb("probs", [P, H, S])
        pT = sb("pT", [P, PAIRS, P])
        wround = pT[:].rearrange("p h s -> p (h s)").bitcast(BF16).rearrange("p (w k d) -> p w k d", w=4, k=KC)
        rinv = sb("rinv", [P, PAIRS, 2])
        o_sb = sb("o_sb", [P, D])
        oT = sb("oT", [P, KC, P])
        z = sb("z", [P, 3, D])
        zi = sb("zi", [P, 3, D], BF16)
        ziT = sb("ziT", [P, 3, KC, P], BF16)
        amax = sb("amax", [P, 3])
        arecip = sb("arecip", [P, 3])
        deq = sb("deq", [P, 2, 3])
        wfac = sb("wfac", [P, 3])
        osq = sb("osq", [P, D])
        base_f = sb("base_f", [P, 2, T])
        small = sb("small", [P, 8])
        oi = sb("oi", [P, D], BF16)
        oiT = sb("oiT", [P, KC, P], BF16)
        spare = [0]

        def reuse(*dims):
            n = int(np.prod(dims))
            a = wproj[:].rearrange("p w k d -> p (w k d)")[:, spare[0]:spare[0] + n]
            spare[0] += n
            names = "abc"[:len(dims)]
            return a if len(dims) == 1 else a.rearrange(
                f"p ({' '.join(names)}) -> p {' '.join(names)}", **dict(zip(names, dims)))

        b2_row = k_bd[:, :, :, :, :].rearrange("p a b c d -> p (a b c d)").rearrange("p (e d) -> p e d", e=E)
        fill = sb("fill", [P, ROW])
        gp = reuse(T, E)
        gp2 = reuse(T, E)
        eq = reuse(T, E)
        oh = reuse(2, T, E)
        oh_bf = sb("oh_bf", [P, T, E], BF16)
        rev = sb("rev", [P, E])
        gm = sb("gm", [P, 4, T])
        slots = reuse(T, E)
        slot_f = sb("slot_f", [P, 2, T])
        slot_i = sb("slot_i", [P, 2, T], I32)
        cnt = sb("cnt", [P, 4, E])
        cnt_i = sb("cnt_i", [P, 2, E], I32)
        tile_no = sb("tile_no", [P, TILES])
        tile_cmp = reuse(TILES, E)
        tile_f = sb("tile_f", [P, TILES])
        tile_e = sb("tile_e", [P, TILES], I32)
        xg = reuse(2, ROW)
        xgT = reuse(KC, P)
        h_sb = probs[:, :, :].rearrange("p h s -> p (h s)")
        gT = pT
        y_sb = reuse(2, D)
        tok_i = sb("tok_i", [P, 2], I32)
        meta = sb("meta", [P, 2, E])

        bank_tr, bank_qk, bank_v = bank("bank_tr"), bank("bank_qk"), bank("bank_v")
        bank_s = [bank("bank_s0"), bank("bank_s1")]
        bank_p = [bank("bank_p0"), bank("bank_p1")]
        bank_o = bank("bank_o")

        cross = Attention(sem, "cross")
        own = Attention(sem, "own")
        first_ready, biases_ready = sem("first_ready"), sem("biases_ready")
        x_ready, proj_ready, rows_ready, raw_ready, w_ready = (
            sem(n) for n in ("x_ready", "proj_ready", "rows_ready", "raw_ready", "w_ready"))
        const_ready, tables_ready = sem("const_ready"), sem("tables_ready")
        x_stats, x_ve, x_rstd = sem("x_stats"), sem("x_ve"), sem("x_rstd")
        bias_done, bias_ready = sem("bias_done"), sem("bias_ready")
        wabs_ready, wtot_done, wscale_ready, wrounded = (sem(n) for n in ("wabs_ready", "wtot_done", "wscale_ready", "wrounded"))
        wint_ready, wtr_done, wtr_copied = sem("wint_ready"), sem("wtr_done"), sem("wtr_copied")
        bo_added = sem("bo_added")
        ln1_ve, ln1_r, ln2_ve, ln2_r, both1 = (sem(n) for n in ("ln1_ve", "ln1_r", "ln2_ve", "ln2_r", "both1"))
        g_chain = sem("g_chain")
        base_ready, xr_ready, gtr_done, gtr_copied, logit_done = (
            sem(n) for n in ("base_ready", "xr_ready", "gtr_done", "gtr_copied", "logit_done"))
        max_ready, exp_ready, oh_ready, rank_done = (sem(n) for n in ("max_ready", "exp_ready", "oh_ready", "rank_done"))
        slot_ready, tile_ready, cw_ready = sem("slot_ready"), sem("tile_ready"), sem("cw_ready")
        b2_ready, dispatched, acc_ready = (sem(n) for n in ("b2_ready", "dispatched", "acc_ready"))
        xg_ready = [sem("xg_ready0"), sem("xg_ready1")]
        e_tr_done, e_tr_copied, up_done, h_ready, gelu_done, down_done, y_ready, meta_ready, y_sum = (
            sem(n) for n in ("e_tr_done", "e_tr_copied", "up_done", "h_ready", "gelu_done",
                             "down_done", "y_ready", "meta_ready", "y_sum"))
        y_added = [sem("y_added0"), sem("y_added1")]
        ht_done = [sem("ht_done0"), sem("ht_done1")]
        x_read, row_copied, rows_filled = sem("x_read"), sem("row_copied"), sem("rows_filled")
        out_stored = sem("out_stored")

        block = stack.enter_context(nc.Block())
        CONSTS, TABLES = 18, 8

        @block.sync
        def _(sp):
            def load_ctx(t, par):
                if not isinstance(t, int) or t >= 2:
                    sp.wait_ge(cross.tr_done, t - 1)
                for b in range(2):
                    src = ctx_in[at(2 * t + b, 1), 0:S, :].rearrange("b s d -> (b s) d")
                    sp.dma_start(ctx_sb[S * b:S * b + S, par, :], src).then_inc(cross.ctx_ready[par], 16)

            sp.dma_start(x_sb[:, 0], x_rows[0:P]).then_inc(first_ready, 16)
            load_ctx(0, 0)
            load_ctx(1, 1)
            for n, w in enumerate((xWq, xWk, xWv, xWo)):
                sp.dma_start(wproj[:, n], w.rearrange("(k p) o -> p k o", p=P)).then_inc(proj_ready, 16)
            sp.dma_start(x_sb[:, 1:T], x_rows[P:TOK].rearrange("(t p) d -> p t d", p=P)).then_inc(x_ready, 16)
            sp.dma_start(bias_rows[0:E * FC, :], b1.rearrange("e (c p) -> (e c) p", p=P)).then_inc(biases_ready, 16)
            for n, r in enumerate((xbq, xbk)):
                sp.dma_start(bias_rows[E * FC + KC * n:E * FC + KC * n + KC, :],
                             r.rearrange("(k p) -> k p", p=P)).then_inc(biases_ready, 16)
            for r, dst in ((xbv, bv_row[:]), (xbo, bo_row[:]), (agq, g_row[:, 0]), (agk, g_row[:, 1]),
                           (agv, g_row[:, 2]), (ago, g_row[:, 3]), (gamma, gamma_row[:]), (beta, beta_row[:])):
                sp.dma_start(dst, r.partition_broadcast(P)).then_inc(rows_ready, 16)
            sp.dma_start(gate_sb[:], gate_w.rearrange("(k p) e -> p k e", p=P)).then_inc(rows_ready, 16)
            for n, w in enumerate((awq, awk, awv, awo)):
                sp.dma_start(wraw[:, n], w.rearrange("(k p) c -> p k c", p=P)).then_inc(raw_ready, 16)
            with sp.Fori(1, T // 2) as r:
                load_ctx(2 * r, 0)
                load_ctx(2 * r + 1, 1)
            sp.wait_ge(tables_ready, 2)
            sp.dma_start(rows.rearrange("(j p) r -> p j r", p=P),
                         fill[:, :].unsqueeze(1).to_broadcast([P, TILES, ROW])).then_inc(rows_filled, 16)
            sp.dma_start(acc[TOK:TOK + P, :], fill[:, 0:D]).then_inc(rows_filled, 16)
            sp.wait_ge(wint_ready, 1)
            sp.dma_start(w2_sb[:, E - 1], w2[E - 1].rearrange("(c p) d -> p c d", p=P)).then_inc(w_ready, 16)
            sp.wait_ge(own.scores_done, 2 * T)
            sp.dma_start(b2_row, b2.partition_broadcast(P)).then_inc(b2_ready, 16)
            sp.wait_ge(base_ready, T)
            sp.dma_start(acc[0:TOK, :].rearrange("(t p) d -> p t d", p=P), x_sb[:]).then_inc(acc_ready, 16)

            def load_rows(j, par):
                if not isinstance(j, int) or j >= 2:
                    sp.wait_ge(e_tr_done, j - 1)
                    sp.wait_ge(meta_ready, j - 1)
                sp.dma_start(xg[:, par, :], rows[at(j * P, P), :]).then_inc(xg_ready[par], 16)

            sp.wait_ge(dispatched, 16 * TOPK * T)
            load_rows(0, 0)
            load_rows(1, 1)
            with sp.Fori(1, TILES // 2) as r:
                load_rows(2 * r, 0)
                load_rows(2 * r + 1, 1)
            load_rows(TILES - 1, 0)
            sp.wait_ge(y_added[0], 16 * (TILES - TILES // 2))
            sp.wait_ge(y_added[1], 16 * (TILES // 2))
            sp.dma_start(out_rows, acc[0:TOK, :]).then_inc(out_stored, 16)
            sp.wait_ge(out_stored, 16)

        @block.gpsimd
        def _(pool):
            made = [0]

            def const(ins):
                made[0] += 1
                ins.then_inc(const_ready, 1)
                pool.wait_ge(const_ready, made[0])

            const(pool.memset(ident[:], 0.0))
            const(pool.affine_select(out=ident[:], in_=ident[:], compare_op=ALU.not_equal, fill=1.0,
                                     base=0, pattern=[[-1, P]], channel_multiplier=1))
            const(pool.memset(neg_half[:], -0.5))
            const(pool.memset(head_mask[:], 1.0))
            const(pool.affine_select(out=head_mask[:], in_=head_mask[:], compare_op=ALU.is_ge, fill=0.0,
                                     base=0, pattern=[[-HD, HG]], channel_multiplier=1))
            const(pool.affine_select(out=head_mask[:], in_=head_mask[:], compare_op=ALU.is_ge, fill=0.0,
                                     base=HD - 1, pattern=[[HD, HG]], channel_multiplier=-1))
            const(pool.tensor_tensor(head_mask[:, 0:4], head_mask[:, 0:4], head_mask[:, 4:8], ALU.add))
            const(pool.tensor_tensor(odd_head[:], head_mask[:, 0:2], head_mask[:, 2:4], ALU.add))
            const(pool.memset(k_bd[:], 0.0))
            const(pool.memset(causal[:], 0.0))
            for b in range(2):
                half = causal[S * b:S * b + S]
                const(pool.affine_select(out=half, in_=half, compare_op=ALU.is_ge, fill=MASKED,
                                         base=0, pattern=[[-1, S]], channel_multiplier=1))
            const(pool.tensor_copy(ident_bf[:], ident[:]))
            const(pool.memset(v_bd[:], 0.0))
            const(pool.memset(v_bd[0:S, :, :, :, 2 * HD], 1.0))
            const(pool.memset(v_bd[S:P, :, :, :, 2 * HD + 1], 1.0))
            const(pool.memset(round_col[:], ROUND))
            const(pool.memset(ones[:], 1.0))
            assert made[0] == CONSTS

            def table(ins):
                made[1] += 1
                ins.then_inc(tables_ready, 1)
                pool.wait_ge(tables_ready, made[1])

            made.append(0)
            table(pool.memset(fill[:], 0.0))
            table(pool.iota(fill[:, D:D + 1], pattern=[[0, 1]], base=TOK, channel_multiplier=1,
                            allow_small_or_imprecise_dtypes=True))
            table(pool.memset(ones_bf[:], 1.0))
            table(pool.memset(before[:], 1.0))
            table(pool.affine_select(out=before[:], in_=before[:], compare_op=ALU.is_gt, fill=0.0,
                                     base=0, pattern=[[1, P]], channel_multiplier=-1))
            table(pool.iota(rev[:], pattern=[[-1, E]], base=E, channel_multiplier=0,
                            allow_small_or_imprecise_dtypes=True))
            table(pool.iota(tile_no[:], pattern=[[1, TILES]], base=0, channel_multiplier=0,
                            allow_small_or_imprecise_dtypes=True))
            table(pool.iota(xr[:, :, D:D + 1], pattern=[[P, T], [0, 1]], base=0, channel_multiplier=1,
                            allow_small_or_imprecise_dtypes=True))
            assert made[1] == TABLES

            def inverse_root(dst, src, waits, done):
                for s, v in waits:
                    pool.wait_ge(s, v)
                pool.tensor_tensor(dst, src, neg_half[:, 0:src.shape[-1]], ALU.pow).then_inc(done, 1)

            inverse_root(rstd[:, 0, 0:1], ve[:, 0, 0:1], ((x_ve, 1),), x_rstd)
            inverse_root(rstd[:, 0, 1:T], ve[:, 0, 1:T], ((x_ve, 2),), x_rstd)
            inverse_root(rstd[:, 1], ve[:, 1], ((ln1_ve, 1),), ln1_r)
            inverse_root(rboth[:, 0], ve[:, 3], ((ln1_ve, 2),), ln1_r)

            def own_gains(t):
                pool.wait_ge(own.xn_ready, t + 1)
                after(pool, own.ints_ready, t)
                pool.tensor_tensor(z[:], xn[:].unsqueeze(1).to_broadcast([P, 3, D]), g_row[:, 0:3],
                                   ALU.mult).then_inc(own.z_ready, 1)

            def own_mean_square(t):
                inverse_root(small[:, 1:2], small[:, 0:1], ((own.sumsq_ready, t + 1),), own.orms_ready)

            own_gains(0)
            own_gains(1)
            own_gains(2)
            with pool.Fori(1, T - 2) as t:
                own_mean_square(t - 1)
                own_gains(t + 2)
            for t in range(T - 3, T):
                own_mean_square(t)
            inverse_root(rstd[:, 2], ve[:, 2], ((ln2_ve, 1),), ln2_r)
            inverse_root(rboth[:, 1], ve[:, 5], ((ln2_ve, 2),), ln2_r)
            pool.wait_ge(slot_ready, 1)
            pool.wait_ge(cw_ready, 1)
            pool.wait_ge(rows_filled, 32)
            pool.wait_ge(row_copied, T)
            for t in range(T):
                for k in range(TOPK):
                    pool.indirect_dma_start(rows, bass.IndirectOffsetOnAxis(ap=slot_i[:, k, t:t + 1], axis=0),
                                            xr[:, t, :], None).then_inc(dispatched, 16)

            pool.wait_ge(acc_ready, 16)
            for j in range(TILES):
                par = j % 2
                pool.wait_ge(y_ready, j + 1)
                if j >= 1:
                    pool.wait_ge(y_added[1 - par], 16 * ((j + 1) // 2))
                pool.indirect_dma_start(acc, bass.IndirectOffsetOnAxis(ap=tok_i[:, par:par + 1], axis=0),
                                        y_sb[:, par, :], None, compute_op=ALU.add).then_inc(y_added[par], 16)

        @block.tensor
        def _(pe):
            def transpose(dst, src, idt):
                return pe.transpose(dst, src, idt)

            def cross_front_transposes(t, par, round_):
                pe.wait_ge(cross.xn_ready, t + 1)
                pe.wait_ge(cross.ctx_ready[par], 32 * (round_ + 1))
                after(pe, cross.tr_copied, t)
                for k in range(KC):
                    transpose(bank_tr[:, k * P:(k + 1) * P], xn[:, k * P:(k + 1) * P], ident[:])
                for k in range(KC):
                    last = transpose(bank_tr[:, (KC + k) * P:(KC + k + 1) * P],
                                     ctx_sb[:, par, k * P:(k + 1) * P], ident[:])
                last.then_inc(cross.tr_done, 1)

            def cross_queries_keys(t):
                pe.wait_ge(cross.tr_copied, t + 1)
                after(pe, cross.q_ready, t)
                after(pe, cross.k_ready, t)
                for w in range(2):
                    for f in range(KC):
                        for k in range(KC):
                            last = pe.matmul(bank_qk[:, (2 * w + f) * P:(2 * w + f + 1) * P],
                                             wproj[:, w, k, f * P:(f + 1) * P],
                                             xcT[:, (2 * w + k) * P:(2 * w + k + 1) * P],
                                             start=(k == 0), stop=(k == KC - 1))
                last.then_inc(cross.qk_done, 1)

            def cross_values(t):
                after(pe, cross.vbd_ready, t)
                for k in range(KC):
                    last = pe.matmul(bank_v[:, 0:D], xcT[:, (2 + k) * P:(3 + k) * P], wproj[:, 2, k, :],
                                     start=(k == 0), stop=(k == KC - 1))
                last.then_inc(cross.v_done, 1)

            def scores(a, t):
                pe.wait_ge(a.q_ready, t + 1)
                pe.wait_ge(a.kbd_low_ready, t + 1)
                pe.wait_ge(a.kbd_high_ready, t + 1)
                for g in range(KC):
                    after(pe, a.shifted[g], t)
                    pe.matmul(bank_s[g][:, :], ident_bf[:], causal[:].unsqueeze(1).to_broadcast([P, HG, S]),
                              start=True, stop=False, skip_group_check=True)
                    for b in range(2):
                        last = pe.matmul(bank_s[g][S * b:S * b + S, :], qT[:, g, S * b:S * b + S],
                                         k_bd[:, g, b].rearrange("p h s -> p (h s)"),
                                         start=False, stop=True, skip_group_check=True)
                    last.then_inc(a.scores_done, 1)

            def probs_transposes(a, t, g):
                pe.wait_ge(a.exp_done, 2 * t + g + 1)
                after(pe, a.pt0_copied if g == 0 else a.pt1_copied, t)
                for j in range(4):
                    c = 4 * g + j
                    last = transpose(bank_p[g][:, j * P:(j + 1) * P],
                                     probs[:, 2 * c:2 * c + 2, :].rearrange("p h s -> p (h s)"), ident[:])
                last.then_inc(a.pt_done[g], 1)

            def values(a, t, par):
                pe.wait_ge(a.vbd_ready, t + 1)
                pe.wait_ge(a.pt0_copied, t + 1)
                pe.wait_ge(a.pt1_copied, t + 1)
                after(pe, a.o_ready, t)
                for c in range(PAIRS):
                    for b in range(2):
                        last = pe.matmul(bank_o[S * b:S * b + S, c * VW:(c + 1) * VW],
                                         pT[:, c, S * b:S * b + S], v_bd[:, par, b, c, :],
                                         start=True, stop=True)
                last.then_inc(a.pv_done, 1)

            def cross_out_transposes(t):
                pe.wait_ge(cross.o_ready, t + 1)
                pe.wait_ge(cross.pt0_copied, t + 1)
                for k in range(KC):
                    last = transpose(bank_p[0][:, k * P:(k + 1) * P], o_sb[:, k * P:(k + 1) * P], ident[:])
                last.then_inc(cross.ot_done, 1)

            def cross_out(t):
                pe.wait_ge(cross.pt1_copied, t + 1)
                pe.wait_ge(cross.ot_copied, t + 1)
                for k in range(KC):
                    last = pe.matmul(bank_p[1][:, 0:D], oT[:, k, :], wproj[:, 3, k, :],
                                     start=(k == 0), stop=(k == KC - 1))
                last.then_inc(cross.out_done, 1)

            def own_front(t):
                pe.wait_ge(own.ints_ready, t + 1)
                after(pe, own.kbd_low_ready, t)
                after(pe, own.kbd_high_ready, t)
                tr = bank_tr[:, :].bitcast(BF16)
                for n in range(3):
                    for k in range(KC):
                        c = KC * n + k
                        last = transpose(tr[:, c * P:(c + 1) * P], zi[:, n, k * P:(k + 1) * P], ident_bf[:])
                last.then_inc(own.tr_done, 1)
                pe.wait_ge(own.tr_copied, t + 1)
                after(pe, own.q_ready, t)
                after(pe, own.k_ready, t)
                for k in range(KC):
                    last = pe.matmul(bank_qk[:, D:2 * D], ziT[:, 1, k, :], wtern[:, 1, k, :],
                                     start=(k == 0), stop=(k == KC - 1))
                for f in range(KC):
                    for k in range(KC):
                        last = pe.matmul(bank_qk[:, f * P:(f + 1) * P], wtern[:, 0, k, f * P:(f + 1) * P],
                                         ziT[:, 0, k, :], start=(k == 0), stop=(k == KC - 1))
                last.then_inc(own.qk_done, 1)
                after(pe, own.vbd_ready, t)
                for k in range(KC):
                    last = pe.matmul(bank_v[:, 0:D], ziT[:, 2, k, :], wtern[:, 2, k, :],
                                     start=(k == 0), stop=(k == KC - 1))
                last.then_inc(own.v_done, 1)

            def own_key_transposes(t):
                pe.wait_ge(own.k_ready, t + 1)
                for k in range(KC):
                    last = transpose(bank_tr[:, k * P:(k + 1) * P],
                                     kT[:, :, :].rearrange("p a b -> p (a b)")[:, k * P:(k + 1) * P], ident[:])
                last.then_inc(own.kt_done, 1)

            def own_out_transposes(t):
                pe.wait_ge(own.oints_ready, t + 1)
                after(pe, own.ot_copied, t)
                tr = bank_v[:, D:D + P].bitcast(BF16)
                for k in range(KC):
                    last = transpose(tr[:, k * P:(k + 1) * P], oi[:, k * P:(k + 1) * P], ident_bf[:])
                last.then_inc(own.ot_done, 1)

            def own_out(t):
                pe.wait_ge(own.ot_copied, t + 1)
                for k in range(KC):
                    last = pe.matmul(bank_p[1][:, 0:D], oiT[:, k, :], wtern[:, 3, k, :],
                                     start=(k == 0), stop=(k == KC - 1))
                last.then_inc(own.out_done, 1)

            pe.wait_ge(const_ready, CONSTS)
            pe.wait_ge(biases_ready, 16 * 3)
            n = E * FC + 2 * KC
            transpose(bank_o[:, 0:n], bias_rows[:], ident[0:n, 0:n]).then_inc(bias_done, 1)
            pe.wait_ge(proj_ready, 64)
            cross_front_transposes(0, 0, 0)
            cross_queries_keys(0)
            cross_values(0)
            pe.wait_ge(wabs_ready, 1)
            pe.wait_ge(bias_ready, 1)
            pe.matmul(bank_o[:, 0:4], ones[:], wabs[:], start=True, stop=True).then_inc(wtot_done, 1)

            def ternary_transposes():
                pe.wait_ge(wint_ready, 1)
                for h in range(2):
                    dst = bank_p[h][:, :].bitcast(BF16).rearrange("p (w c o) -> p w c o", w=2, c=KC)
                    for w in range(2):
                        for oc in range(KC):
                            for cc in range(KC):
                                last = transpose(dst[:, w, cc, oc * P:(oc + 1) * P],
                                                 wround[:, 2 * h + w, oc, cc * P:(cc + 1) * P], ident_bf[:])
                last.then_inc(wtr_done, 1)

            def cross_step(t, par, round_, first=False, more=True):
                scores(cross, t)
                if not first:
                    cross_out_transposes(t - 1)
                if more:
                    cross_front_transposes(t + 1, 1 - par, round_ + par)
                if first:
                    ternary_transposes()
                else:
                    cross_out(t - 1)
                if more:
                    cross_queries_keys(t + 1)
                if first:
                    pe.wait_ge(wtr_copied, 1)
                else:
                    pe.wait_ge(cross.ot_copied, t)
                probs_transposes(cross, t, 0)
                if not first:
                    pe.wait_ge(cross.x_done, t)
                probs_transposes(cross, t, 1)
                if more:
                    cross_values(t + 1)
                values(cross, t, par)

            cross_step(0, 0, 0, first=True)
            cross_step(1, 1, 0)
            with pe.Fori(1, T // 2 - 1) as r:
                cross_step(2 * r, 0, r)
                cross_step(2 * r + 1, 1, r)
            cross_step(T - 2, 0, T // 2 - 1)
            cross_step(T - 1, 1, T // 2 - 1, more=False)
            cross_out_transposes(T - 1)
            cross_out(T - 1)

            own_front(0)
            own_key_transposes(0)

            def own_step(t, par, first=False, more=True):
                scores(own, t)
                if more:
                    own_front(t + 1)
                probs_transposes(own, t, 0)
                if more:
                    own_key_transposes(t + 1)
                if first:
                    pe.wait_ge(cross.x_done, T)
                else:
                    after(pe, own.x_done, t - 1)
                probs_transposes(own, t, 1)
                if not first:
                    own_out_transposes(t - 1)
                values(own, t, par)
                if not first:
                    own_out(t - 1)

            own_step(0, 0, first=True)
            own_step(1, 1)
            with pe.Fori(1, T // 2 - 1) as r:
                own_step(2 * r, 0)
                own_step(2 * r + 1, 1)
            own_step(T - 2, 0)
            own_step(T - 1, 1, more=False)
            own_out_transposes(T - 1)
            pe.wait_ge(own.x_done, T - 1)
            own_out(T - 1)

            def logits(t):
                pe.wait_ge(xr_ready, t + 1)
                after(pe, gtr_copied, t)
                for k in range(KC):
                    last = transpose(bank_tr[:, k * P:(k + 1) * P], xn[:, k * P:(k + 1) * P], ident[:])
                last.then_inc(gtr_done, 1)
                pe.wait_ge(gtr_copied, t + 1)
                for k in range(KC):
                    last = pe.matmul(bank_qk[:, at(t * E, E)], oT[:, k, :], gate_sb[:, k, :],
                                     start=(k == 0), stop=(k == KC - 1))
                last.then_inc(logit_done, 1)

            logits(0)
            with pe.Fori(1, T) as t:
                logits(t)

            pe.wait_ge(oh_ready, 1)
            pe.wait_ge(tables_ready, TABLES)
            flat = oh_bf[:, :, :].rearrange("p t e -> p (t e)")
            n = T * E
            pe.matmul(bank_qk[:, 0:n], before[:], flat, start=True, stop=False, skip_group_check=True)
            for s in range(1, T):
                pe.matmul(bank_qk[:, s * E:n], ones_bf[:], flat[:, 0:n - s * E],
                          start=False, stop=(s == T - 1), skip_group_check=True)
            for t in range(T):
                last = pe.matmul(bank_qk[:, n:n + E], ones_bf[:], flat[:, t * E:(t + 1) * E],
                                 start=False, stop=(t == T - 1), skip_group_check=True)
            last.then_inc(rank_done, 1)

            pe.wait_ge(tile_ready, 1)
            pe.wait_ge(w_ready, 16 * 16)

            def rows_transposed(j, par, round_):
                pe.wait_ge(xg_ready[par], 16 * (round_ + 1))
                after(pe, e_tr_copied, j)
                for k in range(KC):
                    last = transpose(bank_tr[:, k * P:(k + 1) * P], xg[:, par, k * P:(k + 1) * P], ident[:])
                last.then_inc(e_tr_done, 1)

            def up(j):
                e = pe.value_load(tile_e[0:1, at(j, 1)], min_val=0, max_val=E - 1)
                pe.wait_ge(e_tr_copied, j + 1)
                after(pe, h_ready, 2 * j)
                for half in range(2):
                    for k in range(KC):
                        last = pe.matmul(bank_s[half][:, :], xgT[:, k, :],
                                         w1_sb[:, at(e, 1), k, half * 512:(half + 1) * 512].rearrange("p e f -> p (e f)"),
                                         start=(k == 0), stop=(k == KC - 1))
                    last.then_inc(up_done, 1)

            def hidden(j):
                for g in range(2):
                    pe.wait_ge(h_ready, 2 * j + g + 1)
                    after(pe, gelu_done, 2 * j)
                    for c in range(4):
                        last = transpose(bank_p[g][:, c * P:(c + 1) * P],
                                         h_sb[:, (4 * g + c) * P:(4 * g + c + 1) * P], ident[:])
                    last.then_inc(ht_done[g], 1)

            def down(j):
                e = pe.value_load(tile_e[0:1, at(j, 1)], min_val=0, max_val=E - 1)
                after(pe, y_sum, j)
                for c in range(FC):
                    if c % 4 == 0:
                        pe.wait_ge(gelu_done, 2 * j + c // 4 + 1)
                    last = pe.matmul(bank_o[:, 0:D], gT[:, c, :],
                                     w2_sb[:, at(e, 1), c, :].rearrange("p e d -> p (e d)"),
                                     start=(c == 0), stop=(c == FC - 1))
                last.then_inc(down_done, 1)

            rows_transposed(0, 0, 0)
            up(0)
            rows_transposed(1, 1, 0)

            def two_tiles(r, more=True):
                for par in range(2):
                    j = 2 * r + par
                    hidden(j)
                    up(j + 1)
                    if more or par == 0:
                        rows_transposed(j + 2, par, r + 1)
                    down(j)

            two_tiles(0)
            with pe.Fori(1, TILES // 2 - 1) as r:
                two_tiles(r)
            two_tiles(TILES // 2 - 1, more=False)
            hidden(TILES - 1)
            down(TILES - 1)

        @block.vector
        def _(dve):
            def norm_stats(a_sem, b_sem, count, src, dst, src_sem):
                dve.bn_stats(stats[:], src).then_inc(a_sem, 1)
                dve.wait_ge(a_sem, count)
                return dve.bn_aggr(dst, stats[:]).then_inc(b_sem, 1)

            def cross_norm(t):
                dve.wait_ge(x_rstd, 1 if isinstance(t, int) and t == 0 else 2)
                after(dve, cross.tr_done, t)
                dve.tensor_scalar(xn[:], x_sb[:, at(t, 1), :].rearrange("p a d -> p (a d)"),
                                  mv[:, 0, at(t, 1), 0], rstd[:, 0, at(t, 1)],
                                  ALU.subtract, ALU.mult).then_inc(cross.xn_ready, 1)

            def key_blocks(a, t):
                dve.wait_ge(a.k_ready, t + 1)
                after(dve, a.scores_done, 2 * t)
                for i in range(2):
                    rows_ = slice(32 * i, 32 * i + 32)
                    for g in range(KC):
                        last = dve.tensor_tensor(
                            k_bd[rows_, g, :, 2 * i:2 * i + 2, :],
                            kT[rows_, g, :].rearrange("p (b s) -> p b s", b=2).unsqueeze(2).to_broadcast([32, 2, 2, S]),
                            odd_head[rows_, :].unsqueeze(1).unsqueeze(3).to_broadcast([32, 2, 2, S]), ALU.mult)
                last.then_inc(a.kbd_low_ready, 1)

            def value_blocks(a, t, par, put):
                dve.wait_ge(a.v_done, t + 1)
                if not isinstance(t, int) or t >= 2:
                    dve.wait_ge(a.pv_done, t - 1)
                for b in range(2):
                    for odd in range(2):
                        src = bank_v[S * b:S * b + S, 0:D].rearrange("p (c o d) -> p c o d", o=2, d=HD)[:, :, odd, :]
                        dst = v_bd[S * odd:S * odd + S, par, b, :, HD * odd:HD * odd + HD]
                        last = put(dst, src, S * b, odd)
                last.then_inc(a.vbd_ready, 1)

            def cross_values(dst, src, row, odd):
                bias = bv_row[row:row + S, :].rearrange("p (c o d) -> p c o d", o=2, d=HD)[:, :, odd, :]
                return dve.tensor_tensor(dst, src, bias, ALU.add)

            def shift(a, t):
                for g in range(2):
                    dve.wait_ge(a.scores_done, 2 * t + g + 1)
                    s = bank_s[g][:, :].rearrange("p (h s) -> p h s", s=S)
                    dve.tensor_reduce(rmax[:, HG * g:HG * g + HG], s, AX.X, ALU.max).then_inc(a.max_done, 1)
                    dve.wait_ge(a.max_done, 2 * t + g + 1)
                    after(dve, a.pt_done[g], t)
                    dve.tensor_tensor(probs[:, HG * g:HG * g + HG, :], s,
                                      rmax[:, HG * g:HG * g + HG].unsqueeze(2).to_broadcast([P, HG, S]),
                                      ALU.subtract).then_inc(a.shifted[g], 1)

            def copy_probs(a, t):
                dve.wait_ge(a.pt_done[1], t + 1)
                after(dve, a.pv_done, t)
                dve.tensor_copy(pT[:, 4:8, :].rearrange("p a b -> p (a b)"), bank_p[1][:]).then_inc(a.pt1_copied, 1)

            def normalise(a, t):
                o = bank_o[:, 0:PAIRS * VW].rearrange("p (c w) -> p c w", w=VW)
                dve.wait_ge(a.pv_done, t + 1)
                dve.reciprocal(rinv[:], o[:, :, 2 * HD:]).then_inc(a.rinv_ready, 1)
                dve.wait_ge(a.rinv_ready, t + 1)
                after(dve, a.ot_done, t)
                dve.tensor_tensor(o_sb[:, :].rearrange("p (c o d) -> p c o d", o=2, d=HD),
                                  o[:, :, 0:2 * HD].rearrange("p c (o d) -> p c o d", d=HD),
                                  rinv[:].unsqueeze(3).to_broadcast([P, PAIRS, 2, HD]),
                                  ALU.mult).then_inc(a.o_ready, 1)

            def next_stats(a, t, n):
                dve.wait_ge(x_ready, 16)
                dve.wait_ge(a.x_done, t + 1)
                dve.bn_stats(stats[:], x_sb[:, at(t, 1), :].rearrange("p a d -> p (a d)")).then_inc(a.stats_done, 1)
                dve.wait_ge(x_ready, 16)
                dve.wait_ge(a.stats_done, t + 1)
                dve.bn_aggr(mv_tile[:], stats[:]).then_inc(a.mv_done, 1)
                dve.wait_ge(a.mv_done, 2 * t + 1)
                dve.tensor_copy(mv[:, n, at(t, 1), :].rearrange("p a d -> p (a d)"), mv_tile[:]).then_inc(a.mv_done, 1)

            def cross_residual(t):
                dve.wait_ge(bo_added, t + 1)
                dve.wait_ge(cross.out_done, t + 1)
                xt = x_sb[:, at(t, 1), :].rearrange("p a d -> p (a d)")
                dve.tensor_tensor(xt, bank_p[1][:, 0:D], xt, ALU.add).then_inc(cross.x_done, 1)

            dve.wait_ge(first_ready, 16)
            norm_stats(x_stats, x_stats, 1, x_sb[:, 0, :], mv[:, 0, 0, :], None)
            dve.wait_ge(x_stats, 2)
            dve.tensor_scalar(ve[:, 0, 0:1], mv[:, 0, 0:1, 1], LN_EPS, None, ALU.add).then_inc(x_ve, 1)
            cross_norm(0)
            dve.wait_ge(x_ready, 16)
            for t in range(1, T):
                norm_stats(x_stats, x_stats, 2 * t + 1, x_sb[:, t, :], mv[:, 0, t, :], None)
                dve.wait_ge(x_stats, 2 * t + 2)
            dve.tensor_scalar(ve[:, 0, 1:T], mv[:, 0, 1:T, 1], LN_EPS, None, ALU.add).then_inc(x_ve, 1)

            dve.wait_ge(bias_done, 1)
            dve.tensor_copy(bias_col[:], bank_o[:, 0:E * FC + 2 * KC]).then_inc(bias_ready, 1)

            dve.wait_ge(raw_ready, 64)
            dve.tensor_reduce(wabs[:], wraw.rearrange("p w k d -> p w (k d)"), AX.X, ALU.add,
                              apply_absolute_value=True).then_inc(wabs_ready, 1)
            dve.wait_ge(const_ready, CONSTS)
            key_blocks(cross, 0)
            dve.wait_ge(rows_ready, 16 * 9)
            value_blocks(cross, 0, 0, cross_values)
            dve.wait_ge(wtot_done, 1)
            dve.tensor_scalar(wscale[:], bank_o[:, 0:4], 1.0 / (D * D), Q_EPS, ALU.mult, ALU.max).then_inc(wscale_ready, 1)
            dve.wait_ge(wscale_ready, 1)
            dve.reciprocal(wrecip[:], wscale[:]).then_inc(wscale_ready, 1)
            dve.tensor_tensor(qk_scale[:], wscale[:, 0:1], wscale[:, 1:2], ALU.mult).then_inc(wscale_ready, 1)

            def ternary():
                dve.wait_ge(wrounded, 4)
                flat = wraw.rearrange("p w k d -> p (w k d)")
                dve.tensor_scalar(flat, flat, -ROUND, -1.0, ALU.add, ALU.max).then_inc(wscale_ready, 1)
                dve.wait_ge(wscale_ready, 4)
                dve.tensor_scalar(wround[:].rearrange("p w k d -> p (w k d)"), flat, 1.0, None,
                                  ALU.min).then_inc(wint_ready, 1)

            def ternary_columns():
                dve.wait_ge(wtr_done, 1)
                for h in range(2):
                    last = dve.tensor_copy(wtern[:, 2 * h:2 * h + 2].rearrange("p w k d -> p (w k d)"),
                                           bank_p[h][:, :].bitcast(BF16))
                last.then_inc(wtr_copied, 1)

            def add_bo(t):
                dve.wait_ge(cross.xn_ready, t + 1)
                xt = x_sb[:, at(t, 1), :].rearrange("p a d -> p (a d)")
                dve.tensor_tensor(xt, xt, bo_row[:], ALU.add).then_inc(bo_added, 1)

            def cross_step(t, par, first=False, more=True):
                if not first:
                    normalise(cross, t - 1)
                if more:
                    cross_norm(t + 1)
                if first:
                    ternary()
                shift(cross, t)
                if first:
                    ternary_columns()
                else:
                    cross_residual(t - 1)
                    next_stats(cross, t - 1, 1)
                add_bo(t)
                copy_probs(cross, t)
                if more:
                    key_blocks(cross, t + 1)
                    value_blocks(cross, t + 1, 1 - par, cross_values)

            cross_step(0, 0, first=True)
            cross_step(1, 1)
            with dve.Fori(1, T // 2 - 1) as r:
                cross_step(2 * r, 0)
                cross_step(2 * r + 1, 1)
            cross_step(T - 2, 0)
            cross_step(T - 1, 1, more=False)
            normalise(cross, T - 1)
            cross_residual(T - 1)
            next_stats(cross, T - 1, 1)

            dve.wait_ge(cross.mv_done, 2 * T)
            dve.tensor_scalar(ve[:, 1], mv[:, 1, :, 1], LN_EPS, None, ALU.add).then_inc(ln1_ve, 1)
            dve.wait_ge(ln1_r, 1)
            dve.tensor_tensor(ve[:, 2], mv[:, 1, :, 1], rstd[:, 1], ALU.mult).then_inc(both1, 1)
            dve.wait_ge(both1, 1)
            dve.tensor_tensor(ve[:, 2], ve[:, 2], rstd[:, 1], ALU.mult).then_inc(both1, 1)
            dve.wait_ge(both1, 2)
            dve.tensor_scalar(ve[:, 3], ve[:, 2], RMS_EPS, None, ALU.add).then_inc(ln1_ve, 1)
            dve.wait_ge(ln1_r, 2)
            dve.tensor_tensor(rboth[:, 0], rboth[:, 0], rstd[:, 1], ALU.mult).then_inc(both1, 1)
            dve.wait_ge(both1, 3)

            dve.tensor_scalar(wfac[:, 0:1], qk_scale[:], SCALE, None, ALU.mult)
            dve.memset(wfac[:, 1:2], 1.0)
            dve.tensor_copy(wfac[:, 2:3], wscale[:, 2:3]).then_inc(both1, 1)
            dve.wait_ge(both1, 4)

            def tile_of(buf, t):
                return buf[:, at(t, 1), :].rearrange("p a d -> p (a d)")

            def own_norm(t):
                after(dve, own.z_ready, t)
                dve.tensor_scalar(xn[:], tile_of(x_sb, t), mv[:, 1, at(t, 1), 0], rboth[:, 0, at(t, 1)],
                                  ALU.subtract, ALU.mult).then_inc(own.xn_ready, 1)

            def own_scales(t, par):
                dve.wait_ge(own.z_ready, t + 1)
                dve.tensor_reduce(amax[:], z[:], AX.X, ALU.max, apply_absolute_value=True).then_inc(own.amax_ready, 1)
                dve.wait_ge(own.amax_ready, 2 * t + 1)
                dve.tensor_scalar(amax[:], amax[:], Q_EPS, 1.0 / 127, ALU.max, ALU.mult).then_inc(own.amax_ready, 1)
                dve.wait_ge(own.amax_ready, 2 * t + 2)
                after(dve, own.rounded, t)
                dve.reciprocal(arecip[:], amax[:]).then_inc(own.qscale_ready, 1)
                if not isinstance(t, int) or t >= 2:
                    dve.wait_ge(own.exp_done, 2 * t - 2)
                    dve.wait_ge(own.k_ready, t - 1)
                    dve.wait_ge(own.vbd_ready, t - 1)
                dve.tensor_tensor(deq[:, par], amax[:], wfac[:], ALU.mult).then_inc(own.deq_ready, 1)

            def own_ints(t):
                dve.wait_ge(own.rounded, t + 1)
                after(dve, own.tr_done, t)
                dve.tensor_scalar(zi[:].rearrange("p n d -> p (n d)"), z[:].rearrange("p n d -> p (n d)"),
                                  -ROUND, 127.0, ALU.add, ALU.min).then_inc(own.ints_ready, 1)

            def own_square(t):
                dve.wait_ge(own.o_ready, t + 1)
                after(dve, own.orms_ready, t)
                dve.tensor_tensor_reduce(osq[:], o_sb[:], o_sb[:], 1.0 / D, RMS_EPS, ALU.mult, ALU.add,
                                         small[:, 0:1]).then_inc(own.sumsq_ready, 1)

            def own_out_ints(t):
                dve.wait_ge(own.orms_ready, t + 1)
                dve.scalar_tensor_tensor(o_sb[:], o_sb[:], small[:, 1:2], g_row[:, 3], ALU.mult,
                                         ALU.mult).then_inc(own.oz_ready, 1)
                dve.wait_ge(own.oz_ready, t + 1)
                dve.tensor_reduce(small[:, 2:3], o_sb[:], AX.X, ALU.max,
                                  apply_absolute_value=True).then_inc(own.omax_ready, 1)
                dve.wait_ge(own.omax_ready, 2 * t + 1)
                dve.tensor_scalar(small[:, 3:4], small[:, 2:3], Q_EPS, 1.0 / 127, ALU.max,
                                  ALU.mult).then_inc(own.omax_ready, 1)
                dve.wait_ge(own.omax_ready, 2 * t + 2)
                dve.reciprocal(small[:, 4:5], small[:, 3:4]).then_inc(own.oscale_ready, 1)
                after(dve, own.x_done, t)
                dve.tensor_tensor(small[:, 5:6], small[:, 3:4], wscale[:, 3:4], ALU.mult)
                dve.wait_ge(own.oscale_ready, t + 1)
                dve.tensor_scalar(osq[:], o_sb[:], small[:, 4:5], ROUND, ALU.mult, ALU.add).then_inc(own.orounded, 1)
                dve.wait_ge(own.orounded, t + 1)
                after(dve, own.ot_done, t)
                dve.tensor_scalar(oi[:], osq[:], -ROUND, 127.0, ALU.add, ALU.min).then_inc(own.oints_ready, 1)

            def own_residual(t):
                dve.wait_ge(own.out_done, t + 1)
                dve.scalar_tensor_tensor(tile_of(x_sb, t), bank_p[1][:, 0:D], small[:, 5:6], tile_of(x_sb, t),
                                         ALU.mult, ALU.add).then_inc(own.x_done, 1)

            for u in range(2):
                own_norm(u)
                own_scales(u, u)
                own_ints(u)

            def own_step(t, par, back=2, ahead=True):
                if back >= 1:
                    normalise(own, t - 1)
                    own_square(t - 1)
                if ahead:
                    own_norm(t + 2)
                if back >= 2:
                    own_residual(t - 2)
                shift(own, t)
                if back >= 1:
                    own_out_ints(t - 1)
                if ahead:
                    own_scales(t + 2, par)
                copy_probs(own, t)
                if back >= 2:
                    next_stats(own, t - 2, 2)
                if ahead:
                    own_ints(t + 2)

            own_step(0, 0, back=0)
            own_step(1, 1, back=1)
            with dve.Fori(1, T // 2 - 1) as r:
                own_step(2 * r, 0)
                own_step(2 * r + 1, 1)
            own_step(T - 2, 0, ahead=False)
            own_step(T - 1, 1, ahead=False)
            normalise(own, T - 1)
            own_square(T - 1)
            own_residual(T - 2)
            own_out_ints(T - 1)
            next_stats(own, T - 2, 2)
            own_residual(T - 1)
            next_stats(own, T - 1, 2)

            chained = [0]

            def link(ins):
                chained[0] += 1
                ins.then_inc(g_chain, 1)
                dve.wait_ge(g_chain, chained[0])

            dve.wait_ge(own.mv_done, 2 * T)
            dve.tensor_scalar(ve[:, 2], mv[:, 2, :, 1], LN_EPS, None, ALU.add).then_inc(ln2_ve, 1)
            dve.wait_ge(ln2_r, 1)
            link(dve.tensor_tensor(ve[:, 5], mv[:, 2, :, 1], rstd[:, 2], ALU.mult))
            link(dve.tensor_tensor(ve[:, 5], ve[:, 5], rstd[:, 2], ALU.mult))
            dve.tensor_scalar(ve[:, 5], ve[:, 5], LN_EPS, None, ALU.add).then_inc(ln2_ve, 1)
            link(dve.tensor_scalar(base_f[:, 0], rstd[:, 2], 1.0, None, ALU.add))
            dve.scalar_tensor_tensor(base_f[:, 1], mv[:, 2, :, 0], -1.0, rstd[:, 2], ALU.mult,
                                     ALU.mult).then_inc(both1, 1)
            dve.wait_ge(ln2_r, 2)
            link(dve.tensor_tensor(rboth[:, 1], rboth[:, 1], rstd[:, 2], ALU.mult))

            def expert_norm(t):
                after(dve, xr_ready, t)
                dve.scalar_tensor_tensor(osq[:], tile_of(x_sb, t), mv[:, 2, at(t, 1), 0], gamma_row[:],
                                         ALU.subtract, ALU.mult).then_inc(x_read, 1)
                dve.wait_ge(x_read, t + 1)
                after(dve, gtr_done, t)
                after(dve, row_copied, t)
                dve.scalar_tensor_tensor(xn[:], osq[:], rboth[:, 1, at(t, 1)], beta_row[:],
                                         ALU.mult, ALU.add).then_inc(xr_ready, 1)

            expert_norm(0)
            with dve.Fori(1, T) as t:
                expert_norm(t)

            def wide(a):
                return a.unsqueeze(2).to_broadcast([P, T, E])

            lg = bank_qk[:, 0:T * E].rearrange("p (t e) -> p t e", e=E)
            dve.wait_ge(logit_done, T)
            link(dve.tensor_reduce(gm[:, 0], lg, AX.X, ALU.max))
            dve.tensor_tensor(gp[:], lg, wide(gm[:, 0]), ALU.subtract).then_inc(max_ready, 1)
            dve.wait_ge(exp_ready, 1)
            link(dve.tensor_reduce(gm[:, 1], gp[:], AX.X, ALU.add))
            link(dve.reciprocal(gm[:, 0], gm[:, 1]))
            link(dve.tensor_tensor(gp[:], gp[:], wide(gm[:, 0]), ALU.mult))
            for k, p in enumerate((gp, gp2)):
                link(dve.tensor_reduce(gm[:, k], p[:], AX.X, ALU.max))
                link(dve.tensor_tensor(eq[:], p[:], wide(gm[:, k]), ALU.is_equal))
                link(dve.tensor_tensor(eq[:], eq[:], rev[:].unsqueeze(1).to_broadcast([P, T, E]), ALU.mult))
                link(dve.tensor_reduce(gm[:, 2], eq[:], AX.X, ALU.max))
                link(dve.tensor_tensor(oh[:, k], eq[:], wide(gm[:, 2]), ALU.is_equal))
                if k == 0:
                    link(dve.scalar_tensor_tensor(gp2[:].rearrange("p t e -> p (t e)"),
                                                  oh[:, 0].rearrange("p t e -> p (t e)"), -2.0,
                                                  gp[:].rearrange("p t e -> p (t e)"), ALU.mult, ALU.add))
            dve.tensor_tensor(oh_bf[:], oh[:, 0], oh[:, 1], ALU.add).then_inc(oh_ready, 1)
            link(dve.tensor_tensor(gm[:, 2], gm[:, 0], gm[:, 1], ALU.add))
            link(dve.reciprocal(gm[:, 3], gm[:, 2]))
            link(dve.tensor_tensor(gm[:, 0:2], gm[:, 0:2],
                                   gm[:, 3].unsqueeze(1).to_broadcast([P, 2, T]), ALU.mult))
            link(dve.tensor_tensor(gp[:], oh[:, 0], wide(gm[:, 0]), ALU.mult))
            link(dve.tensor_tensor(gp2[:], oh[:, 1], wide(gm[:, 1]), ALU.mult))
            dve.wait_ge(tables_ready, TABLES)
            dve.tensor_tensor(xr[:, :, D + 1:ROW], gp[:], gp2[:], ALU.add).then_inc(cw_ready, 1)
            dve.wait_ge(rank_done, 1)
            n = T * E
            link(dve.tensor_scalar(cnt_i[:, 0], bank_qk[:, n:n + E], P - 1.0, None, ALU.add))
            link(dve.tensor_scalar(cnt_i[:, 1], cnt_i[:, 0], 7, None, ALU.logical_shift_right))
            link(dve.tensor_copy(cnt[:, 0], cnt_i[:, 1]))
            link(dve.tensor_tensor_scan(cnt[:, 1], ones[:, 0:E], cnt[:, 0], 0.0, ALU.mult, ALU.add))
            link(dve.tensor_tensor(cnt[:, 2], cnt[:, 1], cnt[:, 0], ALU.subtract))
            link(dve.tensor_scalar(cnt[:, 2], cnt[:, 2], float(P), None, ALU.mult))
            link(dve.tensor_tensor(slots[:], lg, cnt[:, 2].unsqueeze(1).to_broadcast([P, T, E]), ALU.add))
            for k in range(TOPK):
                link(dve.tensor_tensor(eq[:], oh[:, k], slots[:], ALU.mult))
                link(dve.tensor_reduce(slot_f[:, k], eq[:], AX.X, ALU.add))
            dve.tensor_copy(slot_i[:], slot_f[:]).then_inc(slot_ready, 1)
            link(dve.tensor_tensor(tile_cmp[:], tile_no[:].unsqueeze(2).to_broadcast([P, TILES, E]),
                                   cnt[:, 1].unsqueeze(1).to_broadcast([P, TILES, E]), ALU.is_ge))
            link(dve.tensor_reduce(tile_f[:], tile_cmp[:], AX.X, ALU.add))
            dve.tensor_scalar(tile_e[:], tile_f[:], E - 1.0, None, ALU.min).then_inc(tile_ready, 1)

            def hidden(j):
                for g in range(2):
                    dve.wait_ge(up_done, 2 * j + g + 1)
                    after(dve, ht_done[g], j)
                    dve.tensor_copy(h_sb[:, g * 512:(g + 1) * 512], bank_s[g][:]).then_inc(h_ready, 1)

            def rows_transposed(j):
                dve.wait_ge(e_tr_done, j + 1)
                after(dve, up_done, 2 * j)
                dve.tensor_copy(xgT[:].rearrange("p a b -> p (a b)"), bank_tr[:, 0:D]).then_inc(e_tr_copied, 1)

            def keep_meta(j, par, round_):
                dve.wait_ge(xg_ready[par], 16 * (round_ + 1))
                after(dve, y_ready, j - 1)
                dve.tensor_copy(meta[:, par], xg[:, par, D + 1:ROW])
                after(dve, y_added[par], 16 * round_)
                dve.tensor_copy(tok_i[:, par:par + 1], xg[:, par, D:D + 1]).then_inc(meta_ready, 1)

            def weighted(j, par, round_):
                e = dve.value_load(tile_e[0:1, at(j, 1)], min_val=0, max_val=E - 1)
                after(dve, y_added[par], 16 * round_)
                dve.wait_ge(down_done, j + 1)
                dve.tensor_tensor(y_sb[:, par, :], bank_o[:, 0:D],
                                  b2_row[:, at(e, 1), :].rearrange("p a d -> p (a d)"), ALU.add).then_inc(y_sum, 1)
                dve.wait_ge(y_sum, j + 1)
                dve.wait_ge(meta_ready, j + 1)
                dve.tensor_scalar(y_sb[:, par, :], y_sb[:, par, :], meta[:, par, bass.ds(e, 1)], None,
                                  ALU.mult).then_inc(y_ready, 1)

            dve.wait_ge(tile_ready, 1)
            dve.wait_ge(b2_ready, 16)
            rows_transposed(0)
            keep_meta(0, 0, 0)
            hidden(0)
            rows_transposed(1)
            keep_meta(1, 1, 0)

            def two_tiles(r, more=True):
                for par in range(2):
                    j = 2 * r + par
                    hidden(j + 1)
                    if more or par == 0:
                        rows_transposed(j + 2)
                    weighted(j, par, r)
                    if more or par == 0:
                        keep_meta(j + 2, par, r + 1)

            two_tiles(0)
            with dve.Fori(1, TILES // 2 - 1) as r:
                two_tiles(r)
            two_tiles(TILES // 2 - 1, more=False)
            weighted(TILES - 1, 0, TILES // 2)

        @block.scalar
        def _(act):
            def copy(dst, src):
                return act.activation(dst, src, ACT.Copy)

            def load_expert(e):
                act.dma_start(w1_sb[:, at(e, 1)], w1[at(e, 1)].rearrange("e (k p) f -> p e k f", p=P)).then_inc(w_ready, 16)
                if not isinstance(e, int) or e < E - 1:
                    act.dma_start(w2_sb[:, at(e, 1)],
                                  w2[at(e, 1)].rearrange("e (c p) d -> p e c d", p=P)).then_inc(w_ready, 16)

            def exps(a, t, g, scale):
                act.wait_ge(a.shifted[g], t + 1)
                p = probs[:, HG * g:HG * g + HG, :].rearrange("p h s -> p (h s)")
                act.activation(p, p, ACT.Exp, scale=scale).then_inc(a.exp_done, 1)

            def key_blocks(a, t, src, src_sem):
                act.wait_ge(src_sem, t + 1)
                after(act, a.scores_done, 2 * t)
                for i in range(0 if a is own else 2, 4):
                    rows_ = slice(32 * i, 32 * i + 32)
                    for odd in range(2):
                        last = act.activation(k_bd[rows_, :, :, 2 * i + odd, :],
                                              src[rows_].rearrange("p k (b s) -> p k b s", b=2), ACT.Copy,
                                              scale=odd_head[rows_, odd:odd + 1])
                        if a is own and i == 1 and odd == 1:
                            last.then_inc(a.kbd_low_ready, 1)
                last.then_inc(a.kbd_high_ready, 1)

            def cross_front(t):
                act.wait_ge(cross.tr_done, t + 1)
                after(act, cross.v_done, t)
                copy(xcT[:], bank_tr[:]).then_inc(cross.tr_copied, 1)

            def cross_qk(t):
                act.wait_ge(cross.qk_done, t + 1)
                after(act, cross.scores_done, 2 * t)
                after(act, cross.kbd_low_ready, t)
                after(act, cross.kbd_high_ready, t)
                for f in range(KC):
                    last = act.activation(kT[:, f, :], bank_qk[:, (KC + f) * P:(KC + f + 1) * P], ACT.Identity,
                                          bias=bk_col[:, f:f + 1])
                last.then_inc(cross.k_ready, 1)
                for f in range(KC):
                    last = act.activation(qT[:, f, :], bank_qk[:, f * P:(f + 1) * P], ACT.Identity,
                                          bias=bq_col[:, f:f + 1])
                last.then_inc(cross.q_ready, 1)

            def copy_probs(a, t):
                act.wait_ge(a.pt_done[0], t + 1)
                after(act, a.pv_done, t)
                copy(pT[:, 0:4, :].rearrange("p a b -> p (a b)"), bank_p[0][:]).then_inc(a.pt0_copied, 1)

            def cross_out(t):
                act.wait_ge(cross.ot_done, t + 1)
                after(act, cross.out_done, t)
                copy(oT[:].rearrange("p a b -> p (a b)"), bank_p[0][:, 0:D]).then_inc(cross.ot_copied, 1)

            act.wait_ge(const_ready, CONSTS)
            cross_front(0)
            act.wait_ge(bias_ready, 1)
            cross_qk(0)
            key_blocks(cross, 0, kT, cross.k_ready)
            act.wait_ge(wscale_ready, 2)
            for w in range(4):
                v = wraw[:, w].rearrange("p k d -> p (k d)")
                act.activation(v, v, ACT.Identity, scale=wrecip[:, w:w + 1], bias=round_col[:]).then_inc(wrounded, 1)

            assert T == E

            def cross_step(t, first=False, more=True):
                load_expert(t)
                if not first:
                    cross_out(t - 1)
                if more:
                    cross_front(t + 1)
                exps(cross, t, 0, SCALE)
                exps(cross, t, 1, SCALE)
                if more:
                    cross_qk(t + 1)
                if first:
                    act.wait_ge(wtr_done, 1)
                copy_probs(cross, t)
                if more:
                    key_blocks(cross, t + 1, kT, cross.k_ready)

            cross_step(0, first=True)
            with act.Fori(1, T - 1) as t:
                cross_step(t)
            cross_step(T - 1, more=False)
            cross_out(T - 1)

            def own_round(t):
                act.wait_ge(own.qscale_ready, t + 1)
                for n in range(3):
                    last = act.activation(z[:, n], z[:, n], ACT.Identity, scale=arecip[:, n:n + 1], bias=round_col[:])
                last.then_inc(own.rounded, 1)

            def own_columns(t):
                act.wait_ge(own.tr_done, t + 1)
                after(act, own.v_done, t)
                copy(ziT[:].rearrange("p a b c -> p (a b c)"),
                     bank_tr[:, :].bitcast(BF16)[:, 0:3 * D]).then_inc(own.tr_copied, 1)

            def own_keys(t, par):
                act.wait_ge(own.qk_done, t + 1)
                after(act, own.kt_done, t)
                act.wait_ge(own.deq_ready, t + 1)
                act.activation(kT[:].rearrange("p a b -> p (a b)"), bank_qk[:, D:2 * D], ACT.Copy,
                               scale=deq[:, par, 1:2]).then_inc(own.k_ready, 1)

            def own_queries(t):
                act.wait_ge(own.qk_done, t + 1)
                after(act, own.scores_done, 2 * t)
                copy(qT[:].rearrange("p a b -> p (a b)"), bank_qk[:, 0:D]).then_inc(own.q_ready, 1)

            def own_key_blocks(t):
                key_blocks(own, t, bank_tr[:, 0:D].rearrange("p (k s) -> p k s", k=KC), own.kt_done)

            def own_value_blocks(t, par):
                act.wait_ge(own.v_done, t + 1)
                if not isinstance(t, int) or t >= 2:
                    act.wait_ge(own.pv_done, t - 1)
                for b in range(2):
                    for odd in range(2):
                        src = bank_v[S * b:S * b + S, 0:D].rearrange("p (c o d) -> p c o d", o=2, d=HD)[:, :, odd, :]
                        dst = v_bd[S * odd:S * odd + S, par, b, :, HD * odd:HD * odd + HD]
                        last = act.activation(dst, src, ACT.Copy, scale=deq[S * b:S * b + S, par, 2:3])
                last.then_inc(own.vbd_ready, 1)

            def own_out(t):
                act.wait_ge(own.ot_done, t + 1)
                after(act, own.out_done, t)
                copy(oiT[:].rearrange("p a b -> p (a b)"),
                     bank_v[:, D:D + P].bitcast(BF16)).then_inc(own.ot_copied, 1)

            own_round(0)
            own_columns(0)
            own_keys(0, 0)
            own_queries(0)
            own_round(1)
            own_key_blocks(0)
            own_value_blocks(0, 0)

            def own_step(t, par, first=False, more=True, ahead=True):
                if more:
                    own_columns(t + 1)
                exps(own, t, 0, deq[:, par, 0:1])
                if more:
                    own_keys(t + 1, 1 - par)
                exps(own, t, 1, deq[:, par, 0:1])
                if more:
                    own_queries(t + 1)
                copy_probs(own, t)
                if not first:
                    own_out(t - 1)
                if more:
                    own_key_blocks(t + 1)
                    own_value_blocks(t + 1, 1 - par)
                if ahead:
                    own_round(t + 2)

            own_step(0, 0, first=True)
            own_step(1, 1)
            with act.Fori(1, T // 2 - 1) as r:
                own_step(2 * r, 0)
                own_step(2 * r + 1, 1)
            own_step(T - 2, 0, ahead=False)
            own_step(T - 1, 1, more=False, ahead=False)
            own_out(T - 1)

            act.wait_ge(both1, 5)
            def expert_rows(t):
                act.wait_ge(x_read, t + 1)
                xt = x_sb[:, at(t, 1), :].rearrange("p a d -> p (a d)")
                act.activation(xt, xt, ACT.Identity, scale=base_f[:, 0, at(t, 1)],
                               bias=base_f[:, 1, at(t, 1)]).then_inc(base_ready, 1)
                act.wait_ge(xr_ready, t + 1)
                copy(xr[:, at(t, 1), 0:D].rearrange("p a d -> p (a d)"), xn[:]).then_inc(row_copied, 1)
                act.wait_ge(gtr_done, t + 1)
                after(act, logit_done, t)
                copy(oT[:].rearrange("p a b -> p (a b)"), bank_tr[:, 0:D]).then_inc(gtr_copied, 1)

            expert_rows(0)
            with act.Fori(1, T) as t:
                expert_rows(t)
            act.wait_ge(max_ready, 1)
            act.activation(gp[:], gp[:], ACT.Exp).then_inc(exp_ready, 1)

            def gelus(j):
                e = act.value_load(tile_e[0:1, at(j, 1)], min_val=0, max_val=E - 1)
                after(act, down_done, j)
                for g in range(2):
                    act.wait_ge(ht_done[g], j + 1)
                    for c in range(4):
                        last = act.activation(gT[:, 4 * g + c, :], bank_p[g][:, c * P:(c + 1) * P], ACT.Gelu,
                                              bias=b1_col[:, bass.ds(e * FC + (4 * g + c), 1)])
                    last.then_inc(gelu_done, 1)

            act.wait_ge(tile_ready, 1)
            gelus(0)
            with act.Fori(1, TILES) as j:
                gelus(j)


_INS = ['x', 'ctx_1024', 'L0_xattn_Wq', 'L0_xattn_bq', 'L0_xattn_Wk', 'L0_xattn_bk', 'L0_xattn_Wv', 'L0_xattn_bv',
        'L0_xattn_Wo', 'L0_xattn_bo', 'L0_attn_wq', 'L0_attn_wk', 'L0_attn_wv', 'L0_attn_wo', 'L0_attn_gq',
        'L0_attn_gk', 'L0_attn_gv', 'L0_attn_go', 'L0_ffn_gate_w', 'L0_ffn_w1', 'L0_ffn_b1', 'L0_ffn_w2',
        'L0_ffn_b2', 'L0_ffn_gamma', 'L0_ffn_beta']


def kernel(**inputs):
    import concourse.bacc as bacc
    from concourse.bass_utils import run_bass_kernel_spmd

    nc = bacc.Bacc("TRN2", target_bir_lowering=False, num_devices=1)
    arrays, args = {}, []
    for name in _INS:
        a = np.ascontiguousarray(inputs[name])
        arrays[f"in_{name}"] = a
        args.append(nc.dram_tensor(f"in_{name}", a.shape, mybir.dt.from_np(a.dtype), kind="ExternalInput").ap())
    args.append(nc.dram_tensor("rows", (TILES * P, ROW), F32, kind="Internal").ap())
    args.append(nc.dram_tensor("acc", (TOK + P, D), F32, kind="Internal").ap())
    args.append(nc.dram_tensor("out", (B, S, D), F32, kind="ExternalOutput").ap())
    program(nc, *args)
    r = run_bass_kernel_spmd(nc, [arrays], core_ids=[0])
    return r.results[0]["out"]
```

```python
from contextlib import ExitStack

import numpy as np

import concourse.bass as bass
from concourse import mybir
from concourse.alu_op_type import AluOpType as ALU

ACT = mybir.ActivationFunctionType
AX = mybir.AxisListType
F32 = mybir.dt.float32
BF16 = mybir.dt.bfloat16
F16 = mybir.dt.float16
I32 = mybir.dt.int32

P = 128
B, S, D = 16, 64, 256
TOK = B * S
T = TOK // P
KC = D // P
H, HD = 16, 16
HG = P // HD
PAIRS = H // 2
VW = 2 * HD + 2
E, FF, TOPK = 8, 1024, 2
FC = FF // P
TILES = TOPK * T + E - 1
ROW = D + E
LN_EPS, RMS_EPS, Q_EPS = 1e-5, 1e-6, 1e-5
OWN_LOW = 1
ROUND = 12582912.0
MASKED = -1e30
SCALE = HD ** -0.5


def at(start, size):
    return slice(start, start + size) if isinstance(start, int) else bass.ds(start, size)


def after(engine, semaphore, count):
    if not (isinstance(count, int) and count <= 0):
        engine.wait_ge(semaphore, count)


class Attention:

    def __init__(self, sem, name):
        self.xn_ready = sem(f"{name}_xn_ready")
        self.tr_done = sem(f"{name}_tr_done")
        self.tr_copied = sem(f"{name}_tr_copied")
        self.qk_done = sem(f"{name}_qk_done")
        self.v_done = sem(f"{name}_v_done")
        self.q_ready = sem(f"{name}_q_ready")
        self.k_ready = sem(f"{name}_k_ready")
        self.kbd_low_ready = sem(f"{name}_kbd_low_ready")
        self.kbd_high_ready = sem(f"{name}_kbd_high_ready")
        self.vbd_ready = sem(f"{name}_vbd_ready")
        self.scores_done = sem(f"{name}_scores_done")
        self.max_done = sem(f"{name}_max_done")
        self.exp_done = sem(f"{name}_exp_done")
        self.pt0_copied = sem(f"{name}_pt0_copied")
        self.pt1_copied = sem(f"{name}_pt1_copied")
        self.pv_done = sem(f"{name}_pv_done")
        self.rinv_ready = sem(f"{name}_rinv_ready")
        self.o_ready = sem(f"{name}_o_ready")
        self.ot_done = sem(f"{name}_ot_done")
        self.ot_copied = sem(f"{name}_ot_copied")
        self.out_done = sem(f"{name}_out_done")
        self.x_done = sem(f"{name}_x_done")
        self.stats_done = sem(f"{name}_stats_done")
        self.mv_done = sem(f"{name}_mv_done")
        self.shifted = [sem(f"{name}_shifted{k}") for k in range(2)]
        self.pt_done = [sem(f"{name}_pt_done{k}") for k in range(2)]


class QuantisedAttention(Attention):

    def __init__(self, sem, name):
        super().__init__(sem, name)
        self.z_ready = sem(f"{name}_z_ready")
        self.amax_ready = sem(f"{name}_amax_ready")
        self.qscale_ready = sem(f"{name}_qscale_ready")
        self.deq_ready = sem(f"{name}_deq_ready")
        self.rounded = sem(f"{name}_rounded")
        self.ints_ready = sem(f"{name}_ints_ready")
        self.kt_done = sem(f"{name}_kt_done")
        self.sumsq_ready = sem(f"{name}_sumsq_ready")
        self.orms_ready = sem(f"{name}_orms_ready")
        self.oz_ready = sem(f"{name}_oz_ready")
        self.omax_ready = sem(f"{name}_omax_ready")
        self.oscale_ready = sem(f"{name}_oscale_ready")
        self.orounded = sem(f"{name}_orounded")
        self.oints_ready = sem(f"{name}_oints_ready")


def program(nc, x, ctx_in, xWq, xbq, xWk, xbk, xWv, xbv, xWo, xbo, awq, awk, awv, awo,
            agq, agk, agv, ago, gate_w, w1, b1, w2, b2, gamma, beta, rows, out):
    x_rows = x.rearrange("b s d -> (b s) d")
    out_rows = out.rearrange("b s d -> (b s) d")

    with ExitStack() as stack:
        def sb(name, shape, dt=F32):
            return stack.enter_context(nc.sbuf_tensor(name, shape, dt))

        def bank(name):
            return stack.enter_context(nc.psum_tensor(name, [P, 512], F32))

        def sem(name):
            return stack.enter_context(nc.semaphore(name))

        w1_sb = sb("w1_sb", [P, E, KC, FF])
        w2_sb = sb("w2_sb", [P, E, FC, D])
        wraw = w2_sb[:, E - 1].rearrange("p (w k) d -> p w k d", k=KC)
        bias_rows = sb("bias_rows", [E * FC + 2 * KC, P])
        bias_col = sb("bias_col", [P, E * FC + 2 * KC])
        b1_col = bias_col[:, 0:E * FC]
        bq_col = bias_col[:, E * FC:E * FC + KC]
        bk_col = bias_col[:, E * FC + KC:E * FC + 2 * KC]
        wproj = sb("wproj", [P, 4, KC, D])
        wtern = sb("wtern", [P, 4, KC, D], BF16)
        wabs = sb("wabs", [P, 4])
        wscale = sb("wscale", [P, 4])
        wrecip = sb("wrecip", [P, 4])
        qk_scale = sb("qk_scale", [P, 1])
        bv_row = sb("bv_row", [P, D])
        bo_row = sb("bo_row", [P, D])
        g_row = sb("g_row", [P, 4, D])
        gamma_row = sb("gamma_row", [P, D])
        beta_row = sb("beta_row", [P, D])
        gate_sb = sb("gate_sb", [P, KC, E])
        ident = sb("ident", [P, P])
        ident_bf = sb("ident_bf", [P, P], BF16)
        ones_bf = sb("ones_bf", [P, P], BF16)
        ones = sb("ones", [P, P])
        before = sb("before", [P, P], BF16)
        odd_head = sb("odd_head", [P, 2])
        causal = sb("causal", [P, S], BF16)
        neg_half = sb("neg_half", [P, 2, T])
        warm = sb("warm", [P, 1])
        round_col = sb("round_col", [P, 1])
        head_mask = sb("head_mask", [P, HG])

        x_sb = sb("x_sb", [P, T, D])
        xr = sb("xr", [P, T, ROW])
        stats = sb("stats", [P, 6])
        mv_tile = sb("mv_tile", [P, 2])
        mv = sb("mv", [P, 3, T, 2])
        ve = sb("ve", [P, 4, T])
        rstd = sb("rstd", [P, 1, T])
        rboth = sb("rboth", [P, 1, T])
        r2 = sb("r2", [P, 2, T])
        ctx_sb = sb("ctx_sb", [P, 2, D])
        xn = sb("xn", [P, D])
        xcT = sb("xcT", [P, 4 * P])
        qT = sb("qT", [P, KC, P])
        kT = sb("kT", [P, KC, P])
        k_bd = sb("k_bd", [P, KC, 2, HG, S])
        v_bd = sb("v_bd", [P, 2, 2, PAIRS, VW])
        rmax = sb("rmax", [P, H])
        probs = sb("probs", [P, H, S])
        pT = sb("pT", [P, PAIRS, P])
        wround = xr[:, 0:4, 0:D].bitcast(BF16)
        rinv = sb("rinv", [P, PAIRS, 2])
        o_sb = sb("o_sb", [P, D])
        oT = sb("oT", [P, KC, P])
        z = sb("z", [P, 3, D])
        zi = sb("zi", [P, 3, D], BF16)
        ziT = sb("ziT", [P, 3, KC, P], BF16)
        amax = sb("amax", [P, 3])
        arecip = sb("arecip", [P, 3])
        deq = sb("deq", [P, 2, 3])
        wfac = sb("wfac", [P, 3])
        osq = sb("osq", [P, D])
        base_f = sb("base_f", [P, 2, T])
        centred = (osq[:], z[:, 2])
        small = sb("small", [P, 8])
        oi = sb("oi", [P, D], BF16)
        oiT = sb("oiT", [P, KC, P], BF16)
        spare = [0]

        def reuse(*dims):
            n = int(np.prod(dims))
            a = wproj[:].rearrange("p w k d -> p (w k d)")[:, spare[0]:spare[0] + n]
            spare[0] += n
            names = "abc"[:len(dims)]
            return a if len(dims) == 1 else a.rearrange(
                f"p ({' '.join(names)}) -> p {' '.join(names)}", **dict(zip(names, dims)))

        b2_row = k_bd[:, :, :, :, :].rearrange("p a b c d -> p (a b c d)").rearrange("p (e d) -> p e d", e=E)
        gp = reuse(T, E)
        gp2 = reuse(T, E)
        eq = reuse(T, E)
        oh = reuse(2, T, E)
        oh_bf = sb("oh_bf", [P, T, E], BF16)
        rev = sb("rev", [P, E])
        gm = sb("gm", [P, 4, T])
        slots = reuse(T, E)
        slot_f = sb("slot_f", [P, 2, T])
        slot_i = sb("slot_i", [P, 2, T], I32)
        cnt = sb("cnt", [P, 4, E])
        cnt_i = sb("cnt_i", [P, 2, E], I32)
        tile_no = sb("tile_no", [P, TILES], F16)
        tile_cmp = reuse(TILES, E)
        tile_f = sb("tile_f", [P, TILES])
        tile_e = sb("tile_e", [P, TILES], I32)
        xg = reuse(2, ROW)
        xgT = reuse(KC, P)
        h_sb = probs[:, :, :].rearrange("p h s -> p (h s)")
        gT = pT
        y_sb = reuse(2, D)
        place_no, token_1, beyond = sb("place_no", [P, P], F16), sb("token_1", [P, T], F16), sb("beyond", [P, 1])
        slot_tile = sb("slot_tile", [P, 2, T], F16)
        tile_eq = z[:].rearrange("p n d -> p (n d)").bitcast(F16)[:, 0:TOPK * T * TILES].rearrange("p (n j) -> p n j", j=TILES)
        tile_oh = osq[:].bitcast(F16)[:, 0:TOPK * T * TILES].rearrange("p (n j) -> p n j", j=TILES)
        place_oh = probs[:].rearrange("p h s -> p (h s)").bitcast(F16).rearrange("p (n s) -> p n s", s=P)
        source_i, target_i = sb("source_i", [P, TILES], I32), sb("target_i", [P, TILES], I32)
        meta = sb("meta", [P, 2, E])

        bank_tr, bank_qk, bank_v = bank("bank_tr"), bank("bank_qk"), bank("bank_v")
        bank_s = [bank("bank_s0"), bank("bank_s1")]
        bank_p = [bank("bank_p0"), bank("bank_p1")]
        bank_o = bank("bank_o")

        cross = Attention(sem, "cross")
        ctx_ready = [sem("ctx_ready0"), sem("ctx_ready1")]
        own = QuantisedAttention(sem, "own")
        second_ready = sem("second_ready")
        first_ready, biases_ready, bv_ready = sem("first_ready"), sem("biases_ready"), sem("bv_ready")
        x_ready, proj_ready, rows_ready, raw_ready, w_ready = (
            sem(n) for n in ("x_ready", "proj_ready", "rows_ready", "raw_ready", "w_ready"))
        const_ready, tables_ready = sem("const_ready"), sem("tables_ready")
        x_stats, x_ve, x_rstd = sem("x_stats"), sem("x_ve"), sem("x_rstd")
        bias_done, bias_ready = sem("bias_done"), sem("bias_ready")
        wabs_ready, wtot_done, wscale_ready, wrounded = (sem(n) for n in ("wabs_ready", "wtot_done", "wscale_ready", "wrounded"))
        wclip_ready, wtr_done, wtr_copied = sem("wclip_ready"), sem("wtr_done"), sem("wtr_copied")
        bo_added = sem("bo_added")
        ln1_ve, ln1_r, ln2_ve, ln2_r, both1 = (sem(n) for n in ("ln1_ve", "ln1_r", "ln2_ve", "ln2_r", "both1"))
        c_chain, g_pair, slot_tile_ready, tile_eq_ready = (
            sem(n) for n in ("c_chain", "g_pair", "slot_tile_ready", "tile_eq_ready"))
        g_chain, base_f_ready = sem("g_chain"), sem("base_f_ready")
        base_ready, xr_ready, gtr_done, gtr_copied, logit_done = (
            sem(n) for n in ("base_ready", "xr_ready", "gtr_done", "gtr_copied", "logit_done"))
        max_ready, exp_ready, oh_ready, rank_done = (sem(n) for n in ("max_ready", "exp_ready", "oh_ready", "rank_done"))
        tile_ready, cw_ready, source_ready = sem("tile_ready"), sem("cw_ready"), sem("source_ready")
        tile_tokens_ready, places_ready, inverse_done = (
            sem(n) for n in ("tile_tokens_ready", "places_ready", "inverse_done"))
        b2_ready, base_stored, rows_stored = (sem(n) for n in ("b2_ready", "base_stored", "rows_stored"))
        xg_ready = [sem("xg_ready0"), sem("xg_ready1")]
        e_tr_done, e_tr_copied, up_done, h_ready, gelu_done, down_done, y_ready, meta_ready, y_sum = (
            sem(n) for n in ("e_tr_done", "e_tr_copied", "up_done", "h_ready", "gelu_done",
                             "down_done", "y_ready", "meta_ready", "y_sum"))
        y_added = [sem("y_added0"), sem("y_added1")]
        ht_done = [sem("ht_done0"), sem("ht_done1")]
        x_read, row_copied = sem("x_read"), sem("row_copied")

        block = stack.enter_context(nc.Block())
        CONSTS, TABLES = 18, 8

        @block.sync
        def _(sp):
            def load_ctx(t, par):
                if not isinstance(t, int) or t >= 2:
                    sp.wait_ge(cross.tr_done, t - 1)
                for b in range(2):
                    src = ctx_in[at(2 * t + b, 1), 0:S, :].rearrange("b s d -> (b s) d")
                    sp.dma_start(ctx_sb[S * b:S * b + S, par, :], src).then_inc(ctx_ready[par], 16)

            sp.dma_start(x_sb[:, 0], x_rows[0:P]).then_inc(first_ready, 16)
            load_ctx(0, 0)
            sp.dma_start(bias_rows[0:E * FC, :], b1.rearrange("e (c p) -> (e c) p", p=P)).then_inc(biases_ready, 16)
            for n, r in enumerate((xbq, xbk)):
                sp.dma_start(bias_rows[E * FC + KC * n:E * FC + KC * n + KC, :],
                             r.rearrange("(k p) -> k p", p=P)).then_inc(biases_ready, 16)
            sp.dma_start(x_sb[:, 1:3], x_rows[P:3 * P].rearrange("(t p) d -> p t d", p=P)).then_inc(second_ready, 16)
            load_ctx(1, 1)
            sp.dma_start(bv_row[:], xbv.partition_broadcast(P)).then_inc(bv_ready, 16)
            sp.dma_start(x_sb[:, 3:T], x_rows[3 * P:TOK].rearrange("(t p) d -> p t d", p=P)).then_inc(x_ready, 16)
            for r, dst in ((xbo, bo_row[:]), (agq, g_row[:, 0]), (agk, g_row[:, 1]),
                           (agv, g_row[:, 2]), (ago, g_row[:, 3]), (gamma, gamma_row[:]), (beta, beta_row[:])):
                sp.dma_start(dst, r.partition_broadcast(P)).then_inc(rows_ready, 16)
            sp.dma_start(gate_sb[:], gate_w.rearrange("(k p) e -> p k e", p=P)).then_inc(rows_ready, 16)
            for n, w in enumerate((awq, awk, awv, awo)):
                sp.dma_start(wraw[:, n], w.rearrange("(k p) c -> p k c", p=P)).then_inc(raw_ready, 16)
            with sp.Fori(1, T // 2) as r:
                load_ctx(2 * r, 0)
                load_ctx(2 * r + 1, 1)
            sp.wait_ge(wclip_ready, 8)
            sp.dma_start(w2_sb[:, E - 1], w2[E - 1].rearrange("(c p) d -> p c d", p=P)).then_inc(w_ready, 16)
            sp.wait_ge(own.scores_done, 2 * T)
            sp.dma_start(b2_row, b2.partition_broadcast(P)).then_inc(b2_ready, 16)
            sp.wait_ge(row_copied, T)
            sp.wait_ge(cw_ready, 1)
            sp.dma_start(rows.rearrange("(t p) r -> p t r", p=P), xr[:]).then_inc(rows_stored, 16)
            sp.wait_ge(base_ready, T)
            sp.dma_start(out_rows.rearrange("(t p) d -> p t d", p=P), x_sb[:]).then_inc(base_stored, 16)
            sp.wait_ge(base_stored, 16)
            sp.wait_ge(y_added[0], 16 * (TILES - TILES // 2))
            sp.wait_ge(y_added[1], 16 * (TILES // 2))

        @block.gpsimd
        def _(pool):
            made = [0]

            def const(ins):
                made[0] += 1
                ins.then_inc(const_ready, 1)
                pool.wait_ge(const_ready, made[0])

            def inverse_root(dst, src, waits, done):
                for s, v in waits:
                    pool.wait_ge(s, v)
                half = neg_half[:, 0, 0:src.shape[-1]] if len(src.shape) == 2 else neg_half[:, :, 0:src.shape[-1]]
                pool.tensor_tensor(dst, src, half, ALU.pow).then_inc(done, 1)

            const(pool.memset(ident[:], 0.0))
            const(pool.affine_select(out=ident[:], in_=ident[:], compare_op=ALU.not_equal, fill=1.0,
                                     base=0, pattern=[[-1, P]], channel_multiplier=1))
            const(pool.memset(neg_half[:], -0.5))
            inverse_root(rstd[:, 0, 0:1], ve[:, 0, 0:1], ((x_ve, 1),), x_rstd)
            const(pool.memset(head_mask[:], 1.0))
            const(pool.affine_select(out=head_mask[:], in_=head_mask[:], compare_op=ALU.is_ge, fill=0.0,
                                     base=0, pattern=[[-HD, HG]], channel_multiplier=1))
            const(pool.affine_select(out=head_mask[:], in_=head_mask[:], compare_op=ALU.is_ge, fill=0.0,
                                     base=HD - 1, pattern=[[HD, HG]], channel_multiplier=-1))
            const(pool.tensor_tensor(head_mask[:, 0:4], head_mask[:, 0:4], head_mask[:, 4:8], ALU.add))
            const(pool.tensor_tensor(odd_head[:], head_mask[:, 0:2], head_mask[:, 2:4], ALU.add))
            const(pool.memset(k_bd[:], 0.0))
            const(pool.memset(causal[:], 0.0))
            for b in range(2):
                half = causal[S * b:S * b + S]
                const(pool.affine_select(out=half, in_=half, compare_op=ALU.is_ge, fill=MASKED,
                                         base=0, pattern=[[-1, S]], channel_multiplier=1))
            const(pool.tensor_copy(ident_bf[:], ident[:]))
            const(pool.memset(v_bd[:], 0.0))
            const(pool.memset(v_bd[0:S, :, :, :, 2 * HD], 1.0))
            const(pool.memset(v_bd[S:P, :, :, :, 2 * HD + 1], 1.0))
            const(pool.memset(round_col[:], ROUND))
            const(pool.memset(ones[:], 1.0))
            assert made[0] == CONSTS

            def table(ins):
                made[1] += 1
                ins.then_inc(tables_ready, 1)
                pool.wait_ge(tables_ready, made[1])

            made.append(0)
            table(pool.memset(ones_bf[:], 1.0))
            table(pool.memset(before[:], 1.0))
            table(pool.affine_select(out=before[:], in_=before[:], compare_op=ALU.is_gt, fill=0.0,
                                     base=0, pattern=[[1, P]], channel_multiplier=-1))
            table(pool.iota(rev[:], pattern=[[-1, E]], base=E, channel_multiplier=0,
                            allow_small_or_imprecise_dtypes=True))
            table(pool.iota(tile_no[:], pattern=[[1, TILES]], base=0, channel_multiplier=0,
                            allow_small_or_imprecise_dtypes=True))
            table(pool.iota(place_no[:], pattern=[[1, P]], base=0, channel_multiplier=0,
                            allow_small_or_imprecise_dtypes=True))
            table(pool.iota(token_1[:], pattern=[[P, T]], base=1, channel_multiplier=1,
                            allow_small_or_imprecise_dtypes=True))
            table(pool.iota(beyond[:], pattern=[[0, 1]], base=TOK + 1, channel_multiplier=1,
                            allow_small_or_imprecise_dtypes=True))
            assert made[1] == TABLES

            inverse_root(rstd[:, 0, 1:3], ve[:, 0, 1:3], ((x_ve, 2),), x_rstd)
            inverse_root(rstd[:, 0, 3:T], ve[:, 0, 3:T], ((x_ve, 3),), x_rstd)
            pool.wait_ge(wrounded, 4)
            for w in range(4):
                v = wraw[:, w].rearrange("p k d -> p (k d)")
                pool.tensor_scalar(v, v, -ROUND, -1.0, ALU.add, ALU.max).then_inc(wclip_ready, 1)
                pool.wait_ge(wclip_ready, 2 * w + 1)
                pool.tensor_scalar(wround[:, w], v, 1.0, None, ALU.min).then_inc(wclip_ready, 1)
                pool.wait_ge(wclip_ready, 2 * w + 2)
            inverse_root(rboth[:, 0, 0:T - 2], ve[:, 1, 0:T - 2], ((ln1_ve, 1),), ln1_r)

            def own_gains(t):
                pool.wait_ge(own.xn_ready, t + 1)
                after(pool, own.ints_ready, t)
                pool.tensor_tensor(z[:], xn[:].unsqueeze(1).to_broadcast([P, 3, D]), g_row[:, 0:3],
                                   ALU.mult).then_inc(own.z_ready, 1)

            def own_mean_square(t):
                inverse_root(small[:, 1:2], small[:, 0:1], ((own.sumsq_ready, t + 1),), own.orms_ready)

            own_gains(0)
            own_gains(1)
            inverse_root(rboth[:, 0, T - 2:T], ve[:, 1, T - 2:T], ((ln1_ve, 2),), ln1_r)
            own_gains(2)
            with pool.Fori(1, T - 2) as t:
                own_mean_square(t - 1)
                own_gains(t + 2)
            own_mean_square(T - 3)
            inverse_root(r2[:, :, 0:T - 3], ve[:, 2:4, 0:T - 3], ((ln2_ve, 1),), ln2_r)
            own_mean_square(T - 2)
            own_mean_square(T - 1)
            inverse_root(r2[:, :, T - 3:T], ve[:, 2:4, T - 3:T], ((ln2_ve, 2),), ln2_r)
            def gather(j):
                par = j % 2
                if j >= 2:
                    pool.wait_ge(e_tr_done, j - 1)
                    pool.wait_ge(meta_ready, j - 1)
                pool.indirect_dma_start(xg[:, par, :], None, rows,
                                        bass.IndirectOffsetOnAxis(ap=source_i[:, j:j + 1], axis=0),
                                        compute_op=ALU.bypass).then_inc(xg_ready[par], 16)

            pool.wait_ge(tile_eq_ready, 1)
            for k in range(TOPK):
                last = pool.tensor_tensor(tile_oh[:, k * T:(k + 1) * T, :], tile_eq[:, k * T:(k + 1) * T, :],
                                          token_1[:].unsqueeze(2).to_broadcast([P, T, TILES]), ALU.mult)
                last.then_inc(tile_tokens_ready, 1)
            pool.wait_ge(source_ready, 1)
            pool.wait_ge(rows_stored, 16)
            for j in range(4):
                gather(j)
            pool.wait_ge(base_stored, 16)
            for j in range(TILES):
                par = j % 2
                pool.wait_ge(y_ready, j + 1)
                if j >= 1:
                    pool.wait_ge(y_added[1 - par], 16 * ((j + 1) // 2))
                pool.indirect_dma_start(out_rows, bass.IndirectOffsetOnAxis(ap=target_i[:, j:j + 1], axis=0),
                                        y_sb[:, par, :], None, bounds_check=TOK - 1, oob_is_err=False,
                                        compute_op=ALU.add).then_inc(y_added[par], 16)
                if j + 4 < TILES:
                    gather(j + 4)

        @block.tensor
        def _(pe):
            def transpose(dst, src, idt):
                return pe.transpose(dst, src, idt)

            def cross_front_transposes(t, par, round_):
                pe.wait_ge(cross.xn_ready, t + 1)
                pe.wait_ge(ctx_ready[par], 32 * (round_ + 1))
                after(pe, cross.tr_copied, t)
                for k in range(KC):
                    transpose(bank_tr[:, k * P:(k + 1) * P], xn[:, k * P:(k + 1) * P], ident[:])
                for k in range(KC):
                    last = transpose(bank_tr[:, (KC + k) * P:(KC + k + 1) * P],
                                     ctx_sb[:, par, k * P:(k + 1) * P], ident[:])
                last.then_inc(cross.tr_done, 1)

            def cross_queries_keys(t):
                pe.wait_ge(cross.tr_copied, t + 1)
                after(pe, cross.q_ready, t)
                after(pe, cross.k_ready, t)
                for w in range(2):
                    for f in range(KC):
                        for k in range(KC):
                            last = pe.matmul(bank_qk[:, (2 * w + f) * P:(2 * w + f + 1) * P],
                                             wproj[:, w, k, f * P:(f + 1) * P],
                                             xcT[:, (2 * w + k) * P:(2 * w + k + 1) * P],
                                             start=(k == 0), stop=(k == KC - 1))
                last.then_inc(cross.qk_done, 1)

            def cross_values(t):
                after(pe, cross.vbd_ready, t)
                for k in range(KC):
                    last = pe.matmul(bank_v[:, 0:D], xcT[:, (2 + k) * P:(3 + k) * P], wproj[:, 2, k, :],
                                     start=(k == 0), stop=(k == KC - 1))
                last.then_inc(cross.v_done, 1)

            def scores(a, t):
                pe.wait_ge(a.q_ready, t + 1)
                pe.wait_ge(a.kbd_low_ready, t + 1)
                pe.wait_ge(a.kbd_high_ready, t + 1)
                for g in range(KC):
                    after(pe, a.shifted[g], t)
                    pe.matmul(bank_s[g][:, :], ident_bf[:], causal[:].unsqueeze(1).to_broadcast([P, HG, S]),
                              start=True, stop=False, skip_group_check=True)
                    for b in range(2):
                        last = pe.matmul(bank_s[g][S * b:S * b + S, :], qT[:, g, S * b:S * b + S],
                                         k_bd[:, g, b].rearrange("p h s -> p (h s)"),
                                         start=False, stop=True, skip_group_check=True)
                    last.then_inc(a.scores_done, 1)

            def probs_transposes(a, t, g):
                pe.wait_ge(a.exp_done, 2 * t + g + 1)
                after(pe, a.pt0_copied if g == 0 else a.pt1_copied, t)
                for j in range(4):
                    c = 4 * g + j
                    last = transpose(bank_p[g][:, j * P:(j + 1) * P],
                                     probs[:, 2 * c:2 * c + 2, :].rearrange("p h s -> p (h s)"), ident[:])
                last.then_inc(a.pt_done[g], 1)

            def values(a, t, par):
                pe.wait_ge(a.vbd_ready, t + 1)
                pe.wait_ge(a.pt0_copied, t + 1)
                pe.wait_ge(a.pt1_copied, t + 1)
                after(pe, a.o_ready, t)
                for c in range(PAIRS):
                    for b in range(2):
                        last = pe.matmul(bank_o[S * b:S * b + S, c * VW:(c + 1) * VW],
                                         pT[:, c, S * b:S * b + S], v_bd[:, par, b, c, :],
                                         start=True, stop=True)
                last.then_inc(a.pv_done, 1)

            def cross_out_transposes(t):
                pe.wait_ge(cross.o_ready, t + 1)
                pe.wait_ge(cross.pt0_copied, t + 1)
                for k in range(KC):
                    last = transpose(bank_p[0][:, k * P:(k + 1) * P], o_sb[:, k * P:(k + 1) * P], ident[:])
                last.then_inc(cross.ot_done, 1)

            def cross_out(t):
                pe.wait_ge(cross.pt1_copied, t + 1)
                pe.wait_ge(cross.ot_copied, t + 1)
                for k in range(KC):
                    last = pe.matmul(bank_p[1][:, 0:D], oT[:, k, :], wproj[:, 3, k, :],
                                     start=(k == 0), stop=(k == KC - 1))
                last.then_inc(cross.out_done, 1)

            def own_front(t):
                pe.wait_ge(own.ints_ready, t + 1)
                after(pe, own.kbd_low_ready, t)
                after(pe, own.kbd_high_ready, t)
                tr = bank_tr[:, :].bitcast(BF16)
                for n in range(3):
                    for k in range(KC):
                        c = KC * n + k
                        last = transpose(tr[:, c * P:(c + 1) * P], zi[:, n, k * P:(k + 1) * P], ident_bf[:])
                last.then_inc(own.tr_done, 1)
                pe.wait_ge(own.tr_copied, t + 1)
                after(pe, own.q_ready, t)
                after(pe, own.k_ready, t)
                for k in range(KC):
                    last = pe.matmul(bank_qk[:, D:2 * D], ziT[:, 1, k, :], wtern[:, 1, k, :],
                                     start=(k == 0), stop=(k == KC - 1))
                for f in range(KC):
                    for k in range(KC):
                        last = pe.matmul(bank_qk[:, f * P:(f + 1) * P], wtern[:, 0, k, f * P:(f + 1) * P],
                                         ziT[:, 0, k, :], start=(k == 0), stop=(k == KC - 1))
                last.then_inc(own.qk_done, 1)
                after(pe, own.vbd_ready, t)
                for k in range(KC):
                    last = pe.matmul(bank_v[:, 0:D], ziT[:, 2, k, :], wtern[:, 2, k, :],
                                     start=(k == 0), stop=(k == KC - 1))
                last.then_inc(own.v_done, 1)

            def own_key_transposes(t):
                pe.wait_ge(own.k_ready, t + 1)
                for k in range(KC):
                    last = transpose(bank_tr[:, k * P:(k + 1) * P],
                                     kT[:, :, :].rearrange("p a b -> p (a b)")[:, k * P:(k + 1) * P], ident[:])
                for k in range(KC):
                    last = transpose(bank_v[:, D + k * P:D + (k + 1) * P],
                                     kT[:, :, :].rearrange("p a b -> p (a b)")[:, k * P:(k + 1) * P], ident[:])
                last.then_inc(own.kt_done, 1)

            def own_out_transposes(t):
                pe.wait_ge(own.oints_ready, t + 1)
                tr = bank_p[0][:, 0:P].bitcast(BF16)
                for k in range(KC):
                    last = transpose(tr[:, k * P:(k + 1) * P], oi[:, k * P:(k + 1) * P], ident_bf[:])
                last.then_inc(own.ot_done, 1)

            def own_out(t):
                pe.wait_ge(own.ot_copied, t + 1)
                for k in range(KC):
                    last = pe.matmul(bank_p[1][:, 0:D], oiT[:, k, :], wtern[:, 3, k, :],
                                     start=(k == 0), stop=(k == KC - 1))
                last.then_inc(own.out_done, 1)

            pe.wait_ge(const_ready, 2)
            cross_front_transposes(0, 0, 0)
            pe.wait_ge(biases_ready, 16 * 3)
            n = E * FC + 2 * KC
            transpose(bank_o[:, 0:n], bias_rows[:], ident[0:n, 0:n]).then_inc(bias_done, 1)
            pe.wait_ge(proj_ready, 64)
            cross_queries_keys(0)
            cross_values(0)
            pe.wait_ge(const_ready, CONSTS)

            def ternary_transposes(h):
                pe.wait_ge(wclip_ready, 8)
                dst = bank_o[:, :].bitcast(BF16).rearrange("p (w c o) -> p w c o", w=2, c=KC)
                for w in range(2):
                    for oc in range(KC):
                        for cc in range(KC):
                            c = oc * D + cc * P
                            last = transpose(dst[:, w, cc, oc * P:(oc + 1) * P],
                                             wround[:, 2 * h + w, c:c + P], ident_bf[:])
                last.then_inc(wtr_done, 1)

            def cross_step(t, par, round_, first=False, more=True, columns=None, sums=False):
                scores(cross, t)
                if not first:
                    cross_out_transposes(t - 1)
                if more:
                    cross_front_transposes(t + 1, 1 - par, round_ + par)
                if not first:
                    cross_out(t - 1)
                if columns is not None:
                    ternary_transposes(columns)
                if more:
                    cross_queries_keys(t + 1)
                if not first:
                    pe.wait_ge(cross.ot_copied, t)
                probs_transposes(cross, t, 0)
                if not first:
                    pe.wait_ge(cross.x_done, t)
                probs_transposes(cross, t, 1)
                if sums:
                    pe.wait_ge(wabs_ready, 2)
                    pe.matmul(bank_o[:, 0:4], ones[:], wabs[:], start=True, stop=True).then_inc(wtot_done, 1)
                if more:
                    cross_values(t + 1)
                if sums:
                    pe.wait_ge(wscale_ready, 1)
                if columns is not None:
                    pe.wait_ge(wtr_copied, columns + 1)
                values(cross, t, par)

            cross_step(0, 0, 0, first=True)
            cross_step(1, 1, 0, sums=True)
            with pe.Fori(1, T // 2 - 1) as r:
                cross_step(2 * r, 0, r)
                cross_step(2 * r + 1, 1, r)
            cross_step(T - 2, 0, T // 2 - 1, columns=0)
            cross_step(T - 1, 1, T // 2 - 1, more=False, columns=1)
            own_front(0)
            cross_out_transposes(T - 1)
            own_key_transposes(0)
            cross_out(T - 1)

            def own_step(t, par, back=2, more=True):
                scores(own, t)
                if back >= 2:
                    own_out(t - 2)
                if more:
                    own_front(t + 1)
                probs_transposes(own, t, 0)
                if more:
                    own_key_transposes(t + 1)
                if back >= 2:
                    pe.wait_ge(own.x_done, t - 1)
                else:
                    pe.wait_ge(cross.x_done, T)
                probs_transposes(own, t, 1)
                values(own, t, par)
                if back >= 1:
                    own_out_transposes(t - 1)

            own_step(0, 0, back=0)
            own_step(1, 1, back=1)
            with pe.Fori(1, T // 2 - 1) as r:
                own_step(2 * r, 0)
                own_step(2 * r + 1, 1)
            own_step(T - 2, 0)
            own_step(T - 1, 1, more=False)
            own_out(T - 2)
            own_out_transposes(T - 1)
            pe.wait_ge(own.x_done, T - 1)
            own_out(T - 1)

            def logits(r):
                for par in range(2):
                    t = 2 * r + par
                    pe.wait_ge(xr_ready, t + 1)
                    after(pe, gtr_copied, t - 1)
                    for k in range(KC):
                        last = transpose((bank_tr, bank_v)[par][:, k * P:(k + 1) * P],
                                         z[:, par, k * P:(k + 1) * P], ident[:])
                    last.then_inc(gtr_done, 1)
                for par in range(2):
                    t = 2 * r + par
                    pe.wait_ge(gtr_copied, t + 1)
                    for k in range(KC):
                        last = pe.matmul(bank_qk[:, at(t * E, E)], (oT, qT)[par][:, k, :], gate_sb[:, k, :],
                                         start=(k == 0), stop=(k == KC - 1))
                    last.then_inc(logit_done, 1)

            logits(0)
            with pe.Fori(1, T // 2) as r:
                logits(r)

            pe.wait_ge(oh_ready, 1)
            pe.wait_ge(tables_ready, TABLES)
            flat = oh_bf[:, :, :].rearrange("p t e -> p (t e)")
            n = T * E
            pe.matmul(bank_qk[:, 0:n], before[:], flat, start=True, stop=False, skip_group_check=True)
            for s in range(1, T):
                pe.matmul(bank_qk[:, s * E:n], ones_bf[:], flat[:, 0:n - s * E],
                          start=False, stop=(s == T - 1), skip_group_check=True)
            for t in range(T):
                last = pe.matmul(bank_qk[:, n:n + E], ones_bf[:], flat[:, t * E:(t + 1) * E],
                                 start=False, stop=(t == T - 1), skip_group_check=True)
            last.then_inc(rank_done, 1)
            pe.wait_ge(tile_tokens_ready, TOPK)
            for n in range(TOPK * T):
                if n % 4 == 0:
                    pe.wait_ge(places_ready, n // 4 + 1)
                last = pe.matmul(bank_v[:, 0:TILES], place_oh[:, n, :], tile_oh[:, n, :],
                                 start=(n == 0), stop=(n == TOPK * T - 1))
            last.then_inc(inverse_done, 1)

            pe.wait_ge(tile_ready, 1)
            pe.wait_ge(w_ready, 16 * 16)

            def rows_transposed(j, par, round_):
                pe.wait_ge(xg_ready[par], 16 * (round_ + 1))
                after(pe, e_tr_copied, j)
                for k in range(KC):
                    last = transpose(bank_tr[:, k * P:(k + 1) * P], xg[:, par, k * P:(k + 1) * P], ident[:])
                last.then_inc(e_tr_done, 1)

            def up(j):
                e = pe.value_load(tile_e[0:1, at(j, 1)], min_val=0, max_val=E - 1)
                pe.wait_ge(e_tr_copied, j + 1)
                after(pe, h_ready, 2 * j)
                for half in range(2):
                    for k in range(KC):
                        last = pe.matmul(bank_s[half][:, :], xgT[:, k, :],
                                         w1_sb[:, at(e, 1), k, half * 512:(half + 1) * 512].rearrange("p e f -> p (e f)"),
                                         start=(k == 0), stop=(k == KC - 1))
                    last.then_inc(up_done, 1)

            def hidden(j):
                for g in range(2):
                    pe.wait_ge(h_ready, 2 * j + g + 1)
                    after(pe, gelu_done, 2 * j)
                    for c in range(4):
                        last = transpose(bank_p[g][:, c * P:(c + 1) * P],
                                         h_sb[:, (4 * g + c) * P:(4 * g + c + 1) * P], ident[:])
                    last.then_inc(ht_done[g], 1)

            def down(j):
                e = pe.value_load(tile_e[0:1, at(j, 1)], min_val=0, max_val=E - 1)
                after(pe, y_sum, j)
                for c in range(FC):
                    if c % 4 == 0:
                        pe.wait_ge(gelu_done, 2 * j + c // 4 + 1)
                    last = pe.matmul(bank_o[:, 0:D], gT[:, c, :],
                                     w2_sb[:, at(e, 1), c, :].rearrange("p e d -> p (e d)"),
                                     start=(c == 0), stop=(c == FC - 1))
                last.then_inc(down_done, 1)

            rows_transposed(0, 0, 0)
            up(0)
            rows_transposed(1, 1, 0)

            def two_tiles(r, more=True):
                for par in range(2):
                    j = 2 * r + par
                    hidden(j)
                    up(j + 1)
                    if more or par == 0:
                        rows_transposed(j + 2, par, r + 1)
                    down(j)

            two_tiles(0)
            with pe.Fori(1, TILES // 2 - 1) as r:
                two_tiles(r)
            two_tiles(TILES // 2 - 1, more=False)
            hidden(TILES - 1)
            down(TILES - 1)

        @block.vector
        def _(dve):
            def norm_stats(a_sem, b_sem, count, src, dst, src_sem):
                dve.bn_stats(stats[:], src).then_inc(a_sem, 1)
                dve.wait_ge(a_sem, count)
                return dve.bn_aggr(dst, stats[:]).then_inc(b_sem, 1)

            def cross_norm(t):
                dve.wait_ge(x_rstd, min(t + 1, 2) if isinstance(t, int) and t < 3 else 3)
                after(dve, cross.tr_done, t)
                dve.tensor_scalar(xn[:], x_sb[:, at(t, 1), :].rearrange("p a d -> p (a d)"),
                                  mv[:, 0, at(t, 1), 0], rstd[:, 0, at(t, 1)],
                                  ALU.subtract, ALU.mult).then_inc(cross.xn_ready, 1)

            def key_blocks(a, t):
                dve.wait_ge(a.k_ready, t + 1)
                after(dve, a.scores_done, 2 * t)
                for i in range(2):
                    rows_ = slice(32 * i, 32 * i + 32)
                    for g in range(KC):
                        last = dve.tensor_tensor(
                            k_bd[rows_, g, :, 2 * i:2 * i + 2, :],
                            kT[rows_, g, :].rearrange("p (b s) -> p b s", b=2).unsqueeze(2).to_broadcast([32, 2, 2, S]),
                            odd_head[rows_, :].unsqueeze(1).unsqueeze(3).to_broadcast([32, 2, 2, S]), ALU.mult)
                last.then_inc(a.kbd_low_ready, 1)

            def value_blocks(a, t, par, put):
                dve.wait_ge(a.v_done, t + 1)
                if not isinstance(t, int) or t >= 2:
                    dve.wait_ge(a.pv_done, t - 1)
                for b in range(2):
                    for odd in range(2):
                        src = bank_v[S * b:S * b + S, 0:D].rearrange("p (c o d) -> p c o d", o=2, d=HD)[:, :, odd, :]
                        dst = v_bd[S * odd:S * odd + S, par, b, :, HD * odd:HD * odd + HD]
                        last = put(dst, src, S * b, odd)
                last.then_inc(a.vbd_ready, 1)

            def cross_values(dst, src, row, odd):
                bias = bv_row[row:row + S, :].rearrange("p (c o d) -> p c o d", o=2, d=HD)[:, :, odd, :]
                return dve.tensor_tensor(dst, src, bias, ALU.add)

            def shift(a, t):
                for g in range(2):
                    dve.wait_ge(a.scores_done, 2 * t + g + 1)
                    s = bank_s[g][:, :].rearrange("p (h s) -> p h s", s=S)
                    dve.tensor_reduce(rmax[:, HG * g:HG * g + HG], s, AX.X, ALU.max).then_inc(a.max_done, 1)
                    dve.wait_ge(a.max_done, 2 * t + g + 1)
                    after(dve, a.pt_done[g], t)
                    dve.tensor_tensor(probs[:, HG * g:HG * g + HG, :], s,
                                      rmax[:, HG * g:HG * g + HG].unsqueeze(2).to_broadcast([P, HG, S]),
                                      ALU.subtract).then_inc(a.shifted[g], 1)

            def copy_probs(a, t):
                dve.wait_ge(a.pt_done[1], t + 1)
                after(dve, a.pv_done, t)
                dve.tensor_copy(pT[:, 4:8, :].rearrange("p a b -> p (a b)"), bank_p[1][:]).then_inc(a.pt1_copied, 1)

            def normalise(a, t):
                o = bank_o[:, 0:PAIRS * VW].rearrange("p (c w) -> p c w", w=VW)
                dve.wait_ge(a.pv_done, t + 1)
                dve.reciprocal(rinv[:], o[:, :, 2 * HD:]).then_inc(a.rinv_ready, 1)
                dve.wait_ge(a.rinv_ready, t + 1)
                after(dve, a.ot_done, t)
                dve.tensor_tensor(o_sb[:, :].rearrange("p (c o d) -> p c o d", o=2, d=HD),
                                  o[:, :, 0:2 * HD].rearrange("p c (o d) -> p c o d", d=HD),
                                  rinv[:].unsqueeze(3).to_broadcast([P, PAIRS, 2, HD]),
                                  ALU.mult).then_inc(a.o_ready, 1)

            def tile_stats(a, t):
                dve.wait_ge(x_ready, 16)
                dve.wait_ge(a.x_done, t + 1)
                dve.bn_stats(stats[:], x_sb[:, at(t, 1), :].rearrange("p a d -> p (a d)")).then_inc(a.stats_done, 1)

            def tile_moments(a, t):
                dve.wait_ge(x_ready, 16)
                dve.wait_ge(a.stats_done, t + 1)
                dve.bn_aggr(mv_tile[:], stats[:]).then_inc(a.mv_done, 1)

            def keep_moments(a, t, n):
                dve.wait_ge(a.mv_done, 2 * t + 1)
                dve.tensor_copy(mv[:, n, at(t, 1), :].rearrange("p a d -> p (a d)"), mv_tile[:]).then_inc(a.mv_done, 1)

            def next_stats(a, t, n):
                tile_stats(a, t)
                tile_moments(a, t)
                keep_moments(a, t, n)

            def cross_residual(t):
                dve.wait_ge(bo_added, t + 1)
                dve.wait_ge(cross.out_done, t + 1)
                xt = x_sb[:, at(t, 1), :].rearrange("p a d -> p (a d)")
                dve.tensor_tensor(xt, bank_p[1][:, 0:D], xt, ALU.add).then_inc(cross.x_done, 1)

            dve.wait_ge(first_ready, 16)
            norm_stats(x_stats, x_stats, 1, x_sb[:, 0, :], mv[:, 0, 0, :], None)
            dve.wait_ge(x_stats, 2)
            dve.tensor_scalar(ve[:, 0, 0:1], mv[:, 0, 0:1, 1], LN_EPS, None, ALU.add).then_inc(x_ve, 1)
            cross_norm(0)
            dve.wait_ge(bias_done, 1)
            dve.tensor_copy(bias_col[:], bank_o[:, 0:E * FC + 2 * KC]).then_inc(bias_ready, 1)

            def first_stats(lo, hi, loaded):
                dve.wait_ge(loaded, 16)
                for t in range(lo, hi):
                    norm_stats(x_stats, x_stats, 2 * t + 1, x_sb[:, t, :], mv[:, 0, t, :], None)
                    dve.wait_ge(x_stats, 2 * t + 2)
                dve.tensor_scalar(ve[:, 0, lo:hi], mv[:, 0, lo:hi, 1], LN_EPS, None, ALU.add).then_inc(x_ve, 1)

            first_stats(1, 3, second_ready)
            dve.wait_ge(const_ready, CONSTS)
            key_blocks(cross, 0)
            dve.wait_ge(bv_ready, 16)
            value_blocks(cross, 0, 0, cross_values)

            def ternary_sums(h):
                dve.wait_ge(raw_ready, 64)
                dve.tensor_reduce(wabs[:, 2 * h:2 * h + 2], wraw[:, 2 * h:2 * h + 2].rearrange("p w k d -> p w (k d)"),
                                  AX.X, ALU.add, apply_absolute_value=True).then_inc(wabs_ready, 1)

            def ternary_scales():
                dve.wait_ge(wtot_done, 1)
                dve.tensor_scalar(wscale[:], bank_o[:, 0:4], 1.0 / (D * D), Q_EPS, ALU.mult, ALU.max).then_inc(wscale_ready, 1)
                dve.wait_ge(wscale_ready, 1)
                dve.reciprocal(wrecip[:], wscale[:]).then_inc(wscale_ready, 1)
                dve.tensor_tensor(qk_scale[:], wscale[:, 0:1], wscale[:, 1:2], ALU.mult).then_inc(wscale_ready, 1)

            def ternary_columns(h):
                dve.wait_ge(wtr_done, h + 1)
                dve.tensor_copy(wtern[:, 2 * h:2 * h + 2].rearrange("p w k d -> p (w k d)"),
                                bank_o[:, :].bitcast(BF16)).then_inc(wtr_copied, 1)

            def add_bo(t):
                dve.wait_ge(cross.xn_ready, t + 1)
                xt = x_sb[:, at(t, 1), :].rearrange("p a d -> p (a d)")
                dve.tensor_tensor(xt, xt, bo_row[:], ALU.add).then_inc(bo_added, 1)

            def tile_of(buf, t):
                return buf[:, at(t, 1), :].rearrange("p a d -> p (a d)")

            def own_key_blocks(t):
                dve.wait_ge(own.kt_done, t + 1)
                after(dve, own.scores_done, 2 * t)
                for i in range(OWN_LOW):
                    rows_ = slice(32 * i, 32 * i + 32)
                    last = dve.tensor_tensor(
                        k_bd[rows_, :, :, 2 * i:2 * i + 2, :].rearrange("p k b h s -> p (k b) h s"),
                        bank_v[rows_, D:2 * D].rearrange("p (n s) -> p n s", s=S).unsqueeze(2)
                        .to_broadcast([32, 2 * KC, 2, S]),
                        odd_head[rows_, :].unsqueeze(1).unsqueeze(3).to_broadcast([32, 2 * KC, 2, S]), ALU.mult)
                last.then_inc(own.kbd_low_ready, 1)

            def own_norm(t):
                dve.wait_ge(ln1_r, 1 if isinstance(t, int) and t < T - 2 else 2)
                after(dve, own.z_ready, t)
                dve.tensor_scalar(xn[:], tile_of(x_sb, t), mv[:, 1, at(t, 1), 0], rboth[:, 0, at(t, 1)],
                                  ALU.subtract, ALU.mult).then_inc(own.xn_ready, 1)

            def own_scales(t, par, stats_of=None):
                dve.wait_ge(own.z_ready, t + 1)
                dve.tensor_reduce(amax[:], z[:], AX.X, ALU.max, apply_absolute_value=True).then_inc(own.amax_ready, 1)
                if stats_of is not None:
                    tile_stats(own, stats_of)
                dve.wait_ge(own.amax_ready, 2 * t + 1)
                dve.tensor_scalar(amax[:], amax[:], Q_EPS, 1.0 / 127, ALU.max, ALU.mult).then_inc(own.amax_ready, 1)
                if stats_of is not None:
                    tile_moments(own, stats_of)
                dve.wait_ge(own.amax_ready, 2 * t + 2)
                after(dve, own.rounded, t)
                dve.reciprocal(arecip[:], amax[:]).then_inc(own.qscale_ready, 1)
                if stats_of is not None:
                    keep_moments(own, stats_of, 2)
                if not isinstance(t, int) or t >= 2:
                    dve.wait_ge(own.exp_done, 2 * t - 2)
                    dve.wait_ge(own.k_ready, t - 1)
                    dve.wait_ge(own.vbd_ready, t - 1)
                dve.tensor_tensor(deq[:, par], amax[:], wfac[:], ALU.mult).then_inc(own.deq_ready, 1)

            def own_ints(t):
                dve.wait_ge(own.rounded, t + 1)
                after(dve, own.tr_done, t)
                dve.tensor_scalar(zi[:].rearrange("p n d -> p (n d)"), z[:].rearrange("p n d -> p (n d)"),
                                  -ROUND, 127.0, ALU.add, ALU.min).then_inc(own.ints_ready, 1)

            def second_norm(lo, hi):
                dve.wait_ge(cross.mv_done, 2 * hi)
                dve.tensor_scalar(ve[:, 1, lo:hi], mv[:, 1, lo:hi, 1], 1.0 + RMS_EPS, LN_EPS * RMS_EPS,
                                  ALU.mult, ALU.add).then_inc(ln1_ve, 1)

            def cross_step(t, par, first=False, more=True, columns=None, sums=None):
                if not first:
                    normalise(cross, t - 1)
                if more:
                    cross_norm(t + 1)
                else:
                    dve.wait_ge(cross.tr_done, T)
                    own_norm(0)
                shift(cross, t)
                if not first:
                    cross_residual(t - 1)
                    if more:
                        next_stats(cross, t - 1, 1)
                if columns is not None:
                    ternary_columns(columns)
                if first:
                    first_stats(3, T, x_ready)
                    dve.wait_ge(rows_ready, 16 * 8)
                if more:
                    add_bo(t)
                if sums == 1:
                    ternary_sums(1)
                copy_probs(cross, t)
                if sums == 1:
                    ternary_scales()
                if more:
                    key_blocks(cross, t + 1)
                    value_blocks(cross, t + 1, 1 - par, cross_values)
                if sums == 0:
                    ternary_sums(0)

            def own_factors():
                dve.tensor_scalar(wfac[:, 0:1], qk_scale[:], SCALE, None, ALU.mult)
                dve.memset(wfac[:, 1:2], 1.0)
                dve.tensor_copy(wfac[:, 2:3], wscale[:, 2:3]).then_inc(both1, 1)
                dve.wait_ge(both1, 1)

            cross_step(0, 0, first=True, sums=0)
            cross_step(1, 1, sums=1)
            with dve.Fori(1, T // 2 - 1) as r:
                cross_step(2 * r, 0)
                cross_step(2 * r + 1, 1)
            cross_step(T - 2, 0, columns=0)
            second_norm(0, T - 2)
            own_factors()
            cross_step(T - 1, 1, more=False, columns=1)
            own_scales(0, 0)
            next_stats(cross, T - 2, 1)
            add_bo(T - 1)

            chained = [0]

            def link(ins):
                chained[0] += 1
                ins.then_inc(g_chain, 1)
                dve.wait_ge(g_chain, chained[0])

            def third_norm(lo, hi):
                dve.wait_ge(own.mv_done, 2 * hi)
                dve.tensor_scalar(ve[:, 2, lo:hi], mv[:, 2, lo:hi, 1], LN_EPS, None, ALU.add)
                dve.tensor_scalar(ve[:, 3, lo:hi], mv[:, 2, lo:hi, 1], 1.0 + LN_EPS, LN_EPS * LN_EPS,
                                  ALU.mult, ALU.add).then_inc(ln2_ve, 1)

            def third_factors(n, lo, hi):
                dve.wait_ge(ln2_r, n)
                dve.tensor_scalar(base_f[:, 0, lo:hi], r2[:, 0, lo:hi], 1.0, None, ALU.add)
                dve.scalar_tensor_tensor(base_f[:, 1, lo:hi], mv[:, 2, lo:hi, 0], -1.0, r2[:, 0, lo:hi], ALU.mult,
                                         ALU.mult).then_inc(base_f_ready, 1)

            def expert_norms(r):
                dve.wait_ge(ln2_r, 1 if isinstance(r, int) else 2)
                for par in range(2):
                    t = 2 * r + par
                    after(dve, xr_ready, t - 1)
                    dve.scalar_tensor_tensor(centred[par], tile_of(x_sb, t), mv[:, 2, at(t, 1), 0], gamma_row[:],
                                             ALU.subtract, ALU.mult).then_inc(x_read, 1)
                for par in range(2):
                    t = 2 * r + par
                    dve.wait_ge(x_read, t + 1)
                    after(dve, gtr_done, t - 1)
                    after(dve, row_copied, t - 1)
                    dve.scalar_tensor_tensor(z[:, par], centred[par], r2[:, 1, at(t, 1)], beta_row[:],
                                             ALU.mult, ALU.add).then_inc(xr_ready, 1)

            def own_square(t):
                dve.wait_ge(own.o_ready, t + 1)
                after(dve, own.orms_ready, t)
                dve.tensor_tensor_reduce(osq[:], o_sb[:], o_sb[:], 1.0 / D, RMS_EPS, ALU.mult, ALU.add,
                                         small[:, 0:1]).then_inc(own.sumsq_ready, 1)

            def own_out_gain(t):
                dve.wait_ge(own.orms_ready, t + 1)
                dve.scalar_tensor_tensor(o_sb[:], o_sb[:], small[:, 1:2], g_row[:, 3], ALU.mult,
                                         ALU.mult).then_inc(own.oz_ready, 1)
                dve.wait_ge(own.oz_ready, t + 1)
                dve.tensor_reduce(small[:, 2:3], o_sb[:], AX.X, ALU.max,
                                  apply_absolute_value=True).then_inc(own.omax_ready, 1)

            def own_out_ints(t):
                dve.wait_ge(own.omax_ready, 2 * t + 1)
                dve.tensor_scalar(small[:, 3:4], small[:, 2:3], Q_EPS, 1.0 / 127, ALU.max,
                                  ALU.mult).then_inc(own.omax_ready, 1)
                dve.wait_ge(own.omax_ready, 2 * t + 2)
                dve.reciprocal(small[:, 4:5], small[:, 3:4]).then_inc(own.oscale_ready, 1)
                after(dve, own.x_done, t)
                dve.tensor_tensor(small[:, 5:6], small[:, 3:4], wscale[:, 3:4], ALU.mult)
                dve.wait_ge(own.oscale_ready, t + 1)
                dve.tensor_scalar(osq[:], o_sb[:], small[:, 4:5], ROUND, ALU.mult, ALU.add).then_inc(own.orounded, 1)
                dve.wait_ge(own.orounded, t + 1)
                after(dve, own.ot_done, t)
                dve.tensor_scalar(oi[:], osq[:], -ROUND, 127.0, ALU.add, ALU.min).then_inc(own.oints_ready, 1)

            def own_residual(t):
                dve.wait_ge(own.out_done, t + 1)
                dve.scalar_tensor_tensor(tile_of(x_sb, t), bank_p[1][:, 0:D], small[:, 5:6], tile_of(x_sb, t),
                                         ALU.mult, ALU.add).then_inc(own.x_done, 1)

            own_ints(0)
            own_norm(1)
            normalise(cross, T - 1)
            own_scales(1, 1)
            own_key_blocks(0)
            cross_residual(T - 1)
            next_stats(cross, T - 1, 1)
            second_norm(T - 2, T)

            def own_step(t, par, back=2, more=True, ahead=True):
                if back >= 1:
                    normalise(own, t - 1)
                if ahead:
                    own_norm(t + 2)
                if back >= 1:
                    own_square(t - 1)
                if more:
                    own_ints(t + 1)
                shift(own, t)
                if back >= 2:
                    own_residual(t - 2)
                if back >= 1:
                    own_out_gain(t - 1)
                if more:
                    own_key_blocks(t + 1)
                copy_probs(own, t)
                if back >= 1:
                    own_out_ints(t - 1)
                if ahead:
                    own_scales(t + 2, par, t - 2 if back >= 2 else None)
                else:
                    next_stats(own, t - 2, 2)

            own_step(0, 0, back=0)
            own_step(1, 1, back=1)
            with dve.Fori(1, T // 2 - 1) as r:
                own_step(2 * r, 0)
                own_step(2 * r + 1, 1)
            own_step(T - 2, 0, ahead=False)
            third_norm(0, T - 3)
            own_step(T - 1, 1, more=False, ahead=False)
            normalise(own, T - 1)
            own_square(T - 1)
            own_residual(T - 2)
            next_stats(own, T - 2, 2)
            own_out_gain(T - 1)
            own_out_ints(T - 1)
            dve.wait_ge(own.oints_ready, T)
            expert_norms(0)
            own_residual(T - 1)
            next_stats(own, T - 1, 2)
            third_norm(T - 3, T)
            expert_norms(1)
            with dve.Fori(2, T // 2) as r:
                expert_norms(r)

            def wide(a):
                return a.unsqueeze(2).to_broadcast([P, T, E])

            third_factors(2, 0, T)
            lg = bank_qk[:, 0:T * E].rearrange("p (t e) -> p t e", e=E)
            dve.wait_ge(logit_done, T)
            link(dve.tensor_reduce(gm[:, 0], lg, AX.X, ALU.max))
            dve.tensor_tensor(gp[:], lg, wide(gm[:, 0]), ALU.subtract).then_inc(max_ready, 1)
            dve.wait_ge(exp_ready, 1)
            link(dve.tensor_reduce(gm[:, 1], gp[:], AX.X, ALU.add))
            link(dve.reciprocal(gm[:, 0], gm[:, 1]))
            link(dve.tensor_tensor(gp[:], gp[:], wide(gm[:, 0]), ALU.mult))
            for k, p in enumerate((gp, gp2)):
                link(dve.tensor_reduce(gm[:, k], p[:], AX.X, ALU.max))
                link(dve.tensor_tensor(eq[:], p[:], wide(gm[:, k]), ALU.is_equal))
                link(dve.tensor_tensor(eq[:], eq[:], rev[:].unsqueeze(1).to_broadcast([P, T, E]), ALU.mult))
                link(dve.tensor_reduce(gm[:, 2], eq[:], AX.X, ALU.max))
                link(dve.tensor_tensor(oh[:, k], eq[:], wide(gm[:, 2]), ALU.is_equal))
                if k == 0:
                    link(dve.scalar_tensor_tensor(gp2[:].rearrange("p t e -> p (t e)"),
                                                  oh[:, 0].rearrange("p t e -> p (t e)"), -2.0,
                                                  gp[:].rearrange("p t e -> p (t e)"), ALU.mult, ALU.add))
            dve.tensor_tensor(oh_bf[:], oh[:, 0], oh[:, 1], ALU.add).then_inc(oh_ready, 1)
            n = T * E
            link(dve.tensor_tensor(gm[:, 2], gm[:, 0], gm[:, 1], ALU.add))
            link(dve.reciprocal(gm[:, 3], gm[:, 2]))
            dve.wait_ge(rank_done, 1)
            dve.tensor_scalar(cnt_i[:, 0], bank_qk[:, n:n + E], P - 1.0, None, ALU.add).then_inc(c_chain, 1)
            link(dve.tensor_tensor(gm[:, 0:2], gm[:, 0:2],
                                   gm[:, 3].unsqueeze(1).to_broadcast([P, 2, T]), ALU.mult))
            dve.wait_ge(c_chain, 1)
            dve.tensor_scalar(cnt_i[:, 1], cnt_i[:, 0], 7, None, ALU.logical_shift_right).then_inc(c_chain, 1)
            dve.tensor_tensor(gp[:], oh[:, 0], wide(gm[:, 0]), ALU.mult).then_inc(g_pair, 1)
            dve.wait_ge(c_chain, 2)
            dve.tensor_copy(cnt[:, 0], cnt_i[:, 1]).then_inc(c_chain, 1)
            dve.tensor_tensor(gp2[:], oh[:, 1], wide(gm[:, 1]), ALU.mult).then_inc(g_pair, 1)
            dve.wait_ge(c_chain, 3)
            dve.tensor_tensor_scan(cnt[:, 1], ones[:, 0:E], cnt[:, 0], 0.0, ALU.mult, ALU.add).then_inc(c_chain, 1)
            dve.wait_ge(tables_ready, TABLES)
            dve.wait_ge(g_pair, 2)
            dve.tensor_tensor(xr[:, :, D:ROW], gp[:], gp2[:], ALU.add).then_inc(cw_ready, 1)
            dve.wait_ge(c_chain, 4)
            link(dve.tensor_tensor(cnt[:, 2], cnt[:, 1], cnt[:, 0], ALU.subtract))
            link(dve.tensor_scalar(cnt[:, 2], cnt[:, 2], float(P), None, ALU.mult))
            link(dve.tensor_tensor(slots[:], lg, cnt[:, 2].unsqueeze(1).to_broadcast([P, T, E]), ALU.add))
            for k in range(TOPK):
                link(dve.tensor_tensor(eq[:], oh[:, k], slots[:], ALU.mult))
                link(dve.tensor_reduce(slot_f[:, k], eq[:], AX.X, ALU.add))
            link(dve.tensor_copy(slot_i[:], slot_f[:]))
            link(dve.tensor_scalar(slot_i[:], slot_i[:], 7, None, ALU.logical_shift_right))
            dve.tensor_copy(slot_tile[:], slot_i[:]).then_inc(slot_tile_ready, 1)
            dve.wait_ge(slot_tile_ready, 1)
            link(dve.scalar_tensor_tensor(slot_f[:].rearrange("p k t -> p (k t)"),
                                          slot_tile[:].rearrange("p k t -> p (k t)"), -float(P),
                                          slot_f[:].rearrange("p k t -> p (k t)"), ALU.mult, ALU.add))
            N = TOPK * T
            dve.tensor_tensor(tile_eq[:], tile_no[:].unsqueeze(1).to_broadcast([P, N, TILES]),
                              slot_tile[:].rearrange("p k t -> p (k t)").unsqueeze(2).to_broadcast([P, N, TILES]),
                              ALU.is_equal).then_inc(tile_eq_ready, 1)
            flat_slot = slot_f[:].rearrange("p k t -> p (k t)")
            for n in range(N):
                last = dve.tensor_scalar(place_oh[:, n, :], place_no[:], flat_slot[:, n:n + 1], None, ALU.is_equal)
                if n % 4 == 3:
                    last.then_inc(places_ready, 1)
            link(dve.tensor_tensor(tile_cmp[:], tile_no[:].unsqueeze(2).to_broadcast([P, TILES, E]),
                                   cnt[:, 1].unsqueeze(1).to_broadcast([P, TILES, E]), ALU.is_ge))
            dve.wait_ge(inverse_done, 1)
            found = bank_v[:, 0:TILES]
            dve.tensor_scalar(source_i[:], found, -1.0, 0.0, ALU.add, ALU.max).then_inc(source_ready, 1)
            link(dve.tensor_reduce(tile_f[:], tile_cmp[:], AX.X, ALU.add))
            dve.tensor_scalar(tile_e[:], tile_f[:], E - 1.0, None, ALU.min).then_inc(tile_ready, 1)
            link(dve.tensor_scalar(tile_cmp[:, :, 0], found, 0.0, beyond[:], ALU.is_equal, ALU.mult))
            link(dve.scalar_tensor_tensor(target_i[:], found, -1.0, tile_cmp[:, :, 0], ALU.add, ALU.add))

            def hidden(j):
                for g in range(2):
                    dve.wait_ge(up_done, 2 * j + g + 1)
                    after(dve, ht_done[g], j)
                    dve.tensor_copy(h_sb[:, g * 512:(g + 1) * 512], bank_s[g][:]).then_inc(h_ready, 1)

            def rows_transposed(j):
                dve.wait_ge(e_tr_done, j + 1)
                after(dve, up_done, 2 * j)
                dve.tensor_copy(xgT[:].rearrange("p a b -> p (a b)"), bank_tr[:, 0:D]).then_inc(e_tr_copied, 1)

            def keep_meta(j, par, round_):
                dve.wait_ge(xg_ready[par], 16 * (round_ + 1))
                after(dve, y_ready, j - 1)
                dve.tensor_copy(meta[:, par], xg[:, par, D:ROW]).then_inc(meta_ready, 1)

            def weighted(j, par, round_):
                e = dve.value_load(tile_e[0:1, at(j, 1)], min_val=0, max_val=E - 1)
                after(dve, y_added[par], 16 * round_)
                dve.wait_ge(down_done, j + 1)
                dve.tensor_tensor(y_sb[:, par, :], bank_o[:, 0:D],
                                  b2_row[:, at(e, 1), :].rearrange("p a d -> p (a d)"), ALU.add).then_inc(y_sum, 1)
                dve.wait_ge(y_sum, j + 1)
                dve.wait_ge(meta_ready, j + 1)
                dve.tensor_scalar(y_sb[:, par, :], y_sb[:, par, :], meta[:, par, bass.ds(e, 1)], None,
                                  ALU.mult).then_inc(y_ready, 1)

            dve.wait_ge(tile_ready, 1)
            dve.wait_ge(b2_ready, 16)
            rows_transposed(0)
            keep_meta(0, 0, 0)
            hidden(0)
            rows_transposed(1)
            keep_meta(1, 1, 0)

            def two_tiles(r, more=True):
                for par in range(2):
                    j = 2 * r + par
                    hidden(j + 1)
                    if more or par == 0:
                        rows_transposed(j + 2)
                    weighted(j, par, r)
                    if more or par == 0:
                        keep_meta(j + 2, par, r + 1)

            two_tiles(0)
            with dve.Fori(1, TILES // 2 - 1) as r:
                two_tiles(r)
            two_tiles(TILES // 2 - 1, more=False)
            weighted(TILES - 1, 0, TILES // 2)

        @block.scalar
        def _(act):
            def copy(dst, src):
                return act.activation(dst, src, ACT.Copy)

            def load_expert(e):
                act.dma_start(w1_sb[:, at(e, 1)], w1[at(e, 1)].rearrange("e (k p) f -> p e k f", p=P)).then_inc(w_ready, 16)
                if not isinstance(e, int) or e < E - 1:
                    act.dma_start(w2_sb[:, at(e, 1)],
                                  w2[at(e, 1)].rearrange("e (c p) d -> p e c d", p=P)).then_inc(w_ready, 16)

            def exps(a, t, g, scale):
                act.wait_ge(a.shifted[g], t + 1)
                p = probs[:, HG * g:HG * g + HG, :].rearrange("p h s -> p (h s)")
                act.activation(p, p, ACT.Exp, scale=scale).then_inc(a.exp_done, 1)

            def key_blocks(a, t, src, src_sem):
                act.wait_ge(src_sem, t + 1)
                after(act, a.scores_done, 2 * t)
                for i in range(OWN_LOW if a is own else 2, 4):
                    rows_ = slice(32 * i, 32 * i + 32)
                    for odd in range(2):
                        last = act.activation(k_bd[rows_, :, :, 2 * i + odd, :],
                                              src[rows_].rearrange("p k (b s) -> p k b s", b=2), ACT.Copy,
                                              scale=odd_head[rows_, odd:odd + 1])
                last.then_inc(a.kbd_high_ready, 1)

            def cross_front(t):
                act.wait_ge(cross.tr_done, t + 1)
                after(act, cross.v_done, t)
                copy(xcT[:], bank_tr[:]).then_inc(cross.tr_copied, 1)

            def cross_qk(t):
                act.wait_ge(cross.qk_done, t + 1)
                after(act, cross.scores_done, 2 * t)
                after(act, cross.kbd_low_ready, t)
                after(act, cross.kbd_high_ready, t)
                for f in range(KC):
                    last = act.activation(kT[:, f, :], bank_qk[:, (KC + f) * P:(KC + f + 1) * P], ACT.Identity,
                                          bias=bk_col[:, f:f + 1])
                last.then_inc(cross.k_ready, 1)
                for f in range(KC):
                    last = act.activation(qT[:, f, :], bank_qk[:, f * P:(f + 1) * P], ACT.Identity,
                                          bias=bq_col[:, f:f + 1])
                last.then_inc(cross.q_ready, 1)

            def copy_probs(a, t):
                act.wait_ge(a.pt_done[0], t + 1)
                after(act, a.pv_done, t)
                copy(pT[:, 0:4, :].rearrange("p a b -> p (a b)"), bank_p[0][:]).then_inc(a.pt0_copied, 1)

            def cross_out(t):
                act.wait_ge(cross.ot_done, t + 1)
                after(act, cross.out_done, t)
                copy(oT[:].rearrange("p a b -> p (a b)"), bank_p[0][:, 0:D]).then_inc(cross.ot_copied, 1)

            for n, w in enumerate((xWq, xWk, xWv, xWo)):
                act.dma_start(wproj[:, n], w.rearrange("(k p) o -> p k o", p=P)).then_inc(proj_ready, 16)
            act.wait_ge(const_ready, 3)
            act.activation(warm[:], neg_half[:, 0, 0:1], ACT.Exp)
            cross_front(0)
            act.wait_ge(bias_ready, 1)
            cross_qk(0)
            act.wait_ge(const_ready, CONSTS)
            key_blocks(cross, 0, kT, cross.k_ready)
            assert T == E

            def own_round(t):
                act.wait_ge(own.qscale_ready, t + 1)
                for n in range(3):
                    last = act.activation(z[:, n], z[:, n], ACT.Identity, scale=arecip[:, n:n + 1], bias=round_col[:])
                last.then_inc(own.rounded, 1)

            def cross_step(t, first=False, more=True, own_first=False):
                load_expert(t)
                if not first:
                    cross_out(t - 1)
                if more:
                    cross_front(t + 1)
                exps(cross, t, 0, SCALE)
                exps(cross, t, 1, SCALE)
                if more:
                    cross_qk(t + 1)
                copy_probs(cross, t)
                if own_first:
                    own_round(0)
                if more:
                    key_blocks(cross, t + 1, kT, cross.k_ready)

            cross_step(0, first=True)
            cross_step(1)
            act.wait_ge(wscale_ready, 2)
            for w in range(4):
                v = wraw[:, w].rearrange("p k d -> p (k d)")
                act.activation(v, v, ACT.Identity, scale=wrecip[:, w:w + 1], bias=round_col[:]).then_inc(wrounded, 1)

            with act.Fori(2, T - 1) as t:
                cross_step(t)
            cross_step(T - 1, more=False, own_first=True)

            def own_columns(t):
                act.wait_ge(own.tr_done, t + 1)
                after(act, own.v_done, t)
                copy(ziT[:].rearrange("p a b c -> p (a b c)"),
                     bank_tr[:, :].bitcast(BF16)[:, 0:3 * D]).then_inc(own.tr_copied, 1)

            def own_keys(t, par):
                act.wait_ge(own.qk_done, t + 1)
                after(act, own.kt_done, t)
                act.wait_ge(own.deq_ready, t + 1)
                act.activation(kT[:].rearrange("p a b -> p (a b)"), bank_qk[:, D:2 * D], ACT.Copy,
                               scale=deq[:, par, 1:2]).then_inc(own.k_ready, 1)

            def own_queries(t):
                act.wait_ge(own.qk_done, t + 1)
                after(act, own.scores_done, 2 * t)
                copy(qT[:].rearrange("p a b -> p (a b)"), bank_qk[:, 0:D]).then_inc(own.q_ready, 1)

            def own_key_blocks(t):
                key_blocks(own, t, bank_tr[:, 0:D].rearrange("p (k s) -> p k s", k=KC), own.kt_done)

            def own_value_blocks(t, par):
                act.wait_ge(own.v_done, t + 1)
                act.wait_ge(own.kbd_low_ready, t + 1)
                if not isinstance(t, int) or t >= 2:
                    act.wait_ge(own.pv_done, t - 1)
                for b in range(2):
                    for odd in range(2):
                        src = bank_v[S * b:S * b + S, 0:D].rearrange("p (c o d) -> p c o d", o=2, d=HD)[:, :, odd, :]
                        dst = v_bd[S * odd:S * odd + S, par, b, :, HD * odd:HD * odd + HD]
                        last = act.activation(dst, src, ACT.Copy, scale=deq[S * b:S * b + S, par, 2:3])
                last.then_inc(own.vbd_ready, 1)

            def own_out(t):
                act.wait_ge(own.ot_done, t + 1)
                after(act, own.out_done, t)
                copy(oiT[:].rearrange("p a b -> p (a b)"),
                     bank_p[0][:, 0:P].bitcast(BF16)).then_inc(own.ot_copied, 1)

            own_columns(0)
            own_keys(0, 0)
            own_queries(0)
            cross_out(T - 1)
            own_key_blocks(0)
            own_round(1)
            own_value_blocks(0, 0)

            def own_step(t, par, back=2, more=True, ahead=True):
                if more:
                    own_columns(t + 1)
                exps(own, t, 0, deq[:, par, 0:1])
                if more:
                    own_keys(t + 1, 1 - par)
                exps(own, t, 1, deq[:, par, 0:1])
                copy_probs(own, t)
                if more:
                    own_queries(t + 1)
                    own_key_blocks(t + 1)
                if back >= 1:
                    own_out(t - 1)
                if ahead:
                    own_round(t + 2)
                if more:
                    own_value_blocks(t + 1, 1 - par)

            own_step(0, 0, back=0)
            own_step(1, 1, back=1)
            with act.Fori(1, T // 2 - 1) as r:
                own_step(2 * r, 0)
                own_step(2 * r + 1, 1)
            own_step(T - 2, 0, ahead=False)
            own_step(T - 1, 1, more=False, ahead=False)
            own_out(T - 1)

            def expert_rows(r):
                for par in range(2):
                    t = 2 * r + par
                    act.wait_ge(gtr_done, t + 1)
                    after(act, logit_done, t - 1)
                    copy((oT, qT)[par][:].rearrange("p a b -> p (a b)"),
                         (bank_tr, bank_v)[par][:, 0:D]).then_inc(gtr_copied, 1)
                    copy(xr[:, at(t, 1), 0:D].rearrange("p a d -> p (a d)"), z[:, par]).then_inc(row_copied, 1)

            expert_rows(0)
            with act.Fori(1, T // 2) as r:
                expert_rows(r)
            act.wait_ge(max_ready, 1)
            act.activation(gp[:], gp[:], ACT.Exp).then_inc(exp_ready, 1)
            act.wait_ge(base_f_ready, 1)
            act.wait_ge(x_read, T)

            def residual_base(t):
                xt = x_sb[:, at(t, 1), :].rearrange("p a d -> p (a d)")
                act.activation(xt, xt, ACT.Identity, scale=base_f[:, 0, at(t, 1)],
                               bias=base_f[:, 1, at(t, 1)]).then_inc(base_ready, 1)

            with act.Fori(0, T) as t:
                residual_base(t)

            def gelus(j):
                e = act.value_load(tile_e[0:1, at(j, 1)], min_val=0, max_val=E - 1)
                after(act, down_done, j)
                for g in range(2):
                    act.wait_ge(ht_done[g], j + 1)
                    for c in range(4):
                        last = act.activation(gT[:, 4 * g + c, :], bank_p[g][:, c * P:(c + 1) * P], ACT.Gelu,
                                              bias=b1_col[:, bass.ds(e * FC + (4 * g + c), 1)])
                    last.then_inc(gelu_done, 1)

            act.wait_ge(tile_ready, 1)
            gelus(0)
            with act.Fori(1, TILES) as j:
                gelus(j)


_INS = ['x', 'ctx_1024', 'L0_xattn_Wq', 'L0_xattn_bq', 'L0_xattn_Wk', 'L0_xattn_bk', 'L0_xattn_Wv', 'L0_xattn_bv',
        'L0_xattn_Wo', 'L0_xattn_bo', 'L0_attn_wq', 'L0_attn_wk', 'L0_attn_wv', 'L0_attn_wo', 'L0_attn_gq',
        'L0_attn_gk', 'L0_attn_gv', 'L0_attn_go', 'L0_ffn_gate_w', 'L0_ffn_w1', 'L0_ffn_b1', 'L0_ffn_w2',
        'L0_ffn_b2', 'L0_ffn_gamma', 'L0_ffn_beta']


def kernel(**inputs):
    import concourse.bacc as bacc
    from concourse.bass_utils import run_bass_kernel_spmd

    nc = bacc.Bacc("TRN2", target_bir_lowering=False, num_devices=1)
    arrays, args = {}, []
    for name in _INS:
        a = np.ascontiguousarray(inputs[name])
        arrays[f"in_{name}"] = a
        args.append(nc.dram_tensor(f"in_{name}", a.shape, mybir.dt.from_np(a.dtype), kind="ExternalInput").ap())
    args.append(nc.dram_tensor("rows", (TOK, ROW), F32, kind="Internal").ap())
    args.append(nc.dram_tensor("out", (B, S, D), F32, kind="ExternalOutput").ap())
    program(nc, *args)
    r = run_bass_kernel_spmd(nc, [arrays], core_ids=[0])
    return r.results[0]["out"]
```
